# Optimizing a Trainium2 kernel written in Bass

```python
import numpy as np
import jax
import jax.numpy as jnp

def _softmax(x, axis=-1):
    return jax.nn.softmax(x, axis=axis)

def _gelu(x):
    return jax.nn.gelu(x, approximate=True)

def _silu(x):
    return jax.nn.silu(x)

def _sigmoid(x):
    return jax.nn.sigmoid(x)

def _layernorm(x, axis=-1, eps=1e-05):
    m = jnp.mean(x, axis=axis, keepdims=True)
    v = jnp.var(x, axis=axis, keepdims=True)
    return (x - m) / jnp.sqrt(v + eps)

def _scatter_add(tgt, idx, src, axis=0):
    return tgt.at[idx].add(src)

def _segment_sum(src, seg, n):
    return jax.ops.segment_sum(src, seg, n)
kernel_name = 'mk_xattn_ffn_d2_seqx_r8_8dd846'

def setup_inputs(seed: int=0):
    np.random.seed(seed)
    _w = jnp.asarray

    def _rec_inputs():
        import jax
        import jax.numpy as jnp
        _rk = jax.random.key(seed)
        x = 7.22e-05 + 1 * jax.random.normal(jax.random.fold_in(_rk, 1), (8, 128, 128), jnp.float32)
        _lenS = 128 - jax.random.randint(jax.random.fold_in(_rk, 7), (8,), 0, max(1, 128 // 4) + 1, jnp.int32)
        _lenS2 = 77 - jax.random.randint(jax.random.fold_in(_rk, 8), (8,), 0, max(1, 77 // 4) + 1, jnp.int32)
        _ctx_1024P = jax.random.normal(jax.random.fold_in(_rk, 11), (8, 16, 128), jnp.float32)
        _ctx_1024c = jax.random.dirichlet(jax.random.fold_in(_rk, 511), 0.3 * jnp.ones((16,), jnp.float32), (8, 77))
        _ctx_1024t = jnp.einsum('bsk,bkd->bsd', _ctx_1024c, _ctx_1024P)
        _ctx_1024t = _ctx_1024t * jax.lax.rsqrt(jnp.mean(jnp.square(_ctx_1024t)) + 1e-12) * 0.953939
        ctx_1024 = 4.13588e-05 + 0.999923 * (_ctx_1024t + 0.3 * jax.random.normal(jax.random.fold_in(_rk, 611), (8, 77, 128), jnp.float32))
        return (x, ctx_1024)
    x, ctx_1024 = _rec_inputs()

    def _L0_xattn_setup():
        import jax, jax.numpy as jnp
        import numpy as np
        key = jax.random.key(seed)
        kq, kv = jax.random.split(key)
        B, Q, K, D = (4, 256, 256, 128)
        queries = jax.random.normal(kq, (B, Q, D), dtype=jnp.float32)
        values = jax.random.normal(kv, (B, K, D), dtype=jnp.float32)
        return {'queries': queries, 'values': values}
    _L0_xattn_all = _L0_xattn_setup()
    _L0_xattn_in = {k: v for k, v in _L0_xattn_all.items() if k in ()}
    del _L0_xattn_all

    def _L0_ffn_setup():
        import jax, jax.numpy as jnp
        import numpy as np
        import math
        D = 128
        H = 16
        E = 8
        TOPK = 2
        LAT = D // 2
        KPH = LAT // H
        HD = D // H

        def _forward(hs, q_w, q_b, k_w, k_b, v_w, v_b, o_w, o_b, router_w, router_b, w1, b1, w2, b2):
            B, S, _ = hs.shape
            Q = (hs @ q_w + q_b).reshape(B, S, H, HD).transpose(0, 2, 1, 3)
            K = (hs @ k_w + k_b).reshape(B, S, H, KPH).transpose(0, 2, 1, 3)
            V = (hs @ v_w + v_b).reshape(B, S, H, KPH).transpose(0, 2, 1, 3)
            scores = jnp.einsum('bhsk,bhtk->bhst', Q[..., :KPH], K) / math.sqrt(KPH)
            attn = jax.nn.softmax(scores, axis=-1)
            ao = jnp.einsum('bhst,bhtv->bhsv', attn, V)
            ao = ao.transpose(0, 2, 1, 3).reshape(B, S, H * KPH)
            ao = jnp.concatenate([ao, jnp.zeros((B, S, D - LAT), ao.dtype)], axis=-1)
            mla_out = ao @ o_w + o_b
            probs = jax.nn.softmax(mla_out @ router_w + router_b, axis=-1)
            topw, topi = jax.lax.top_k(probs, TOPK)
            topw = topw / (topw.sum(-1, keepdims=True) + 1e-08)
            combine = jnp.sum(jax.nn.one_hot(topi, E, dtype=probs.dtype) * topw[..., None], axis=-2)
            h1 = jnp.einsum('bsd,edf->ebsf', mla_out, w1) + b1[:, None, None, :]
            h1 = jax.nn.gelu(h1, approximate=False)
            h2 = jnp.einsum('ebsf,efd->ebsd', h1, w2) + b2[:, None, None, :]
            moe_out = jnp.einsum('bse,ebsd->bsd', combine, h2)
            return hs + 0.3 * moe_out
        key = jax.random.key(seed)
        ks = jax.random.split(key, 16)
        s = 0.02
        inp = {'hidden_states': jax.random.normal(ks[0], (2, 256, D), jnp.float32), 'q_w': jax.random.normal(ks[1], (D, D), jnp.float32) * s, 'q_b': jnp.zeros((D,), jnp.float32), 'k_w': jax.random.normal(ks[2], (D, LAT), jnp.float32) * s, 'k_b': jnp.zeros((LAT,), jnp.float32), 'v_w': jax.random.normal(ks[3], (D, LAT), jnp.float32) * s, 'v_b': jnp.zeros((LAT,), jnp.float32), 'o_w': jax.random.normal(ks[4], (D, D), jnp.float32) * s, 'o_b': jnp.zeros((D,), jnp.float32), 'router_w': jax.random.normal(ks[5], (D, E), jnp.float32) * s, 'router_b': jnp.zeros((E,), jnp.float32), 'w1': jax.random.normal(ks[6], (E, D, 2 * D), jnp.float32) * s, 'b1': jnp.zeros((E, 2 * D), jnp.float32), 'w2': jax.random.normal(ks[7], (E, 2 * D, D), jnp.float32) * s, 'b2': jnp.zeros((E, D), jnp.float32)}
        return inp
    _L0_ffn_all = _L0_ffn_setup()
    _L0_ffn_in = {k: v for k, v in _L0_ffn_all.items() if k in ('q_w', 'q_b', 'k_w', 'k_b', 'v_w', 'v_b', 'o_w', 'o_b', 'router_w', 'router_b', 'w1', 'b1', 'w2', 'b2')}
    del _L0_ffn_all

    def _L1_xattn_setup():
        import jax, jax.numpy as jnp
        import numpy as np
        B, L_ENC, L_DEC, D = (16, 64, 128, 128)
        key = jax.random.key(seed)
        k1, k2, k3, k4, k5, k6 = jax.random.split(key, 6)
        encoder_hc = jax.random.normal(k1, (B, L_ENC, D), dtype=jnp.float32)
        decoder_hq = jax.random.normal(k2, (B, L_DEC, D), dtype=jnp.float32)
        w_sim = jax.random.normal(k3, (3 * D,), dtype=jnp.float32) * 0.02
        b_sim = jax.random.normal(k4, (1,), dtype=jnp.float32) * 0.02
        W_qv = jax.random.normal(k5, (4 * D, D), dtype=jnp.float32) * 0.02
        b_qv = jax.random.normal(k6, (D,), dtype=jnp.float32) * 0.02
        return {'encoder_hc': encoder_hc, 'decoder_hq': decoder_hq, 'w_sim': w_sim, 'b_sim': b_sim, 'W_qv': W_qv, 'b_qv': b_qv}
    _L1_xattn_all = _L1_xattn_setup()
    _L1_xattn_in = {k: v for k, v in _L1_xattn_all.items() if k in ('w_sim', 'b_sim', 'W_qv', 'b_qv')}
    del _L1_xattn_all

    def _L1_ffn_setup():
        import jax, jax.numpy as jnp
        import numpy as np
        E = 8
        key = jax.random.key(seed)
        k0, k1, k2, k3 = jax.random.split(key, 4)
        B, S, H, F = (4, 512, 128, 512)
        x = jax.random.normal(k0, (B, S, H), jnp.float32)
        Wr = jax.random.normal(k1, (E, H), jnp.float32) * 0.02
        W1 = jax.random.normal(k2, (E, H, F), jnp.float32) * 0.02
        b1 = jnp.zeros((E, F), jnp.float32)
        W2 = jax.random.normal(k3, (E, F, H), jnp.float32) * 0.02
        b2 = jnp.zeros((E, H), jnp.float32)
        return {'x': x, 'Wr': Wr, 'W1': W1, 'b1': b1, 'W2': W2, 'b2': b2}
    _L1_ffn_all = _L1_ffn_setup()
    _L1_ffn_in = {k: v for k, v in _L1_ffn_all.items() if k in ('Wr', 'W1', 'b1', 'W2', 'b2')}
    del _L1_ffn_all
    return {'x': x, 'ctx_1024': ctx_1024, 'L0_ffn_q_w': _L0_ffn_in['q_w'], 'L0_ffn_q_b': _L0_ffn_in['q_b'], 'L0_ffn_k_w': _L0_ffn_in['k_w'], 'L0_ffn_k_b': _L0_ffn_in['k_b'], 'L0_ffn_v_w': _L0_ffn_in['v_w'], 'L0_ffn_v_b': _L0_ffn_in['v_b'], 'L0_ffn_o_w': _L0_ffn_in['o_w'], 'L0_ffn_o_b': _L0_ffn_in['o_b'], 'L0_ffn_router_w': _L0_ffn_in['router_w'], 'L0_ffn_router_b': _L0_ffn_in['router_b'], 'L0_ffn_w1': _L0_ffn_in['w1'], 'L0_ffn_b1': _L0_ffn_in['b1'], 'L0_ffn_w2': _L0_ffn_in['w2'], 'L0_ffn_b2': _L0_ffn_in['b2'], 'L1_xattn_w_sim': _L1_xattn_in['w_sim'], 'L1_xattn_b_sim': _L1_xattn_in['b_sim'], 'L1_xattn_W_qv': _L1_xattn_in['W_qv'], 'L1_xattn_b_qv': _L1_xattn_in['b_qv'], 'L1_ffn_Wr': _L1_ffn_in['Wr'], 'L1_ffn_W1': _L1_ffn_in['W1'], 'L1_ffn_b1': _L1_ffn_in['b1'], 'L1_ffn_W2': _L1_ffn_in['W2'], 'L1_ffn_b2': _L1_ffn_in['b2']}

def reference(x, ctx_1024, L0_ffn_q_w, L0_ffn_q_b, L0_ffn_k_w, L0_ffn_k_b, L0_ffn_v_w, L0_ffn_v_b, L0_ffn_o_w, L0_ffn_o_b, L0_ffn_router_w, L0_ffn_router_b, L0_ffn_w1, L0_ffn_b1, L0_ffn_w2, L0_ffn_b2, L1_xattn_w_sim, L1_xattn_b_sim, L1_xattn_W_qv, L1_xattn_b_qv, L1_ffn_Wr, L1_ffn_W1, L1_ffn_b1, L1_ffn_W2, L1_ffn_b2):
    import jax
    import jax.numpy as jnp

    def _L0_xattn_ref(queries, values):
        import jax, jax.numpy as jnp
        import numpy as np
        scores = jnp.einsum('bqd,bkd->bqk', queries, values)
        attn = jax.nn.softmax(scores, axis=-1)
        return jnp.einsum('bqk,bkd->bqd', attn, values)

    def _L0_ffn_ref(hidden_states, q_w, q_b, k_w, k_b, v_w, v_b, o_w, o_b, router_w, router_b, w1, b1, w2, b2):
        import jax, jax.numpy as jnp
        import numpy as np
        import math
        D = 128
        H = 16
        E = 8
        TOPK = 2
        LAT = D // 2
        KPH = LAT // H
        HD = D // H

        def _forward(hs, q_w, q_b, k_w, k_b, v_w, v_b, o_w, o_b, router_w, router_b, w1, b1, w2, b2):
            B, S, _ = hs.shape
            Q = (hs @ q_w + q_b).reshape(B, S, H, HD).transpose(0, 2, 1, 3)
            K = (hs @ k_w + k_b).reshape(B, S, H, KPH).transpose(0, 2, 1, 3)
            V = (hs @ v_w + v_b).reshape(B, S, H, KPH).transpose(0, 2, 1, 3)
            scores = jnp.einsum('bhsk,bhtk->bhst', Q[..., :KPH], K) / math.sqrt(KPH)
            attn = jax.nn.softmax(scores, axis=-1)
            ao = jnp.einsum('bhst,bhtv->bhsv', attn, V)
            ao = ao.transpose(0, 2, 1, 3).reshape(B, S, H * KPH)
            ao = jnp.concatenate([ao, jnp.zeros((B, S, D - LAT), ao.dtype)], axis=-1)
            mla_out = ao @ o_w + o_b
            probs = jax.nn.softmax(mla_out @ router_w + router_b, axis=-1)
            topw, topi = jax.lax.top_k(probs, TOPK)
            topw = topw / (topw.sum(-1, keepdims=True) + 1e-08)
            combine = jnp.sum(jax.nn.one_hot(topi, E, dtype=probs.dtype) * topw[..., None], axis=-2)
            h1 = jnp.einsum('bsd,edf->ebsf', mla_out, w1) + b1[:, None, None, :]
            h1 = jax.nn.gelu(h1, approximate=False)
            h2 = jnp.einsum('ebsf,efd->ebsd', h1, w2) + b2[:, None, None, :]
            moe_out = jnp.einsum('bse,ebsd->bsd', combine, h2)
            return hs + 0.3 * moe_out
        return _forward(hidden_states, q_w, q_b, k_w, k_b, v_w, v_b, o_w, o_b, router_w, router_b, w1, b1, w2, b2)

    def _L1_xattn_ref(encoder_hc, decoder_hq, w_sim, b_sim, W_qv, b_qv):
        import jax, jax.numpy as jnp
        import numpy as np
        B, L_ENC, L_DEC, D = (16, 64, 128, 128)
        d = encoder_hc.shape[-1]
        w1, w2, w3 = (w_sim[:d], w_sim[d:2 * d], w_sim[2 * d:])
        Sim = (encoder_hc @ w1)[:, :, None] + (decoder_hq @ w2)[:, None, :] + jnp.einsum('bid,bjd->bij', encoder_hc * w3, decoder_hq) + b_sim[0]
        A = jax.nn.softmax(Sim, axis=2)
        hq_hat = jnp.einsum('bij,bjd->bid', A, decoder_hq)
        Batt = jax.nn.softmax(jnp.max(Sim, axis=2), axis=1)
        hc_bar = jnp.einsum('bi,bid->bd', Batt, encoder_hc)[:, None, :]
        hc_hat = jnp.broadcast_to(hc_bar, encoder_hc.shape)
        feats = jnp.concatenate([encoder_hc, hq_hat, encoder_hc * hq_hat, encoder_hc * hc_hat], axis=-1)
        hcq = feats @ W_qv + b_qv
        return hcq

    def _L1_ffn_ref(x, Wr, W1, b1, W2, b2):
        import jax, jax.numpy as jnp
        import numpy as np
        E = 8
        B, S, H = x.shape
        xf = x.reshape(-1, H)
        probs = jax.nn.softmax(xf @ Wr.T, axis=-1)
        eid = E - 1
        h = jax.nn.gelu(xf @ W1[eid] + b1[eid], approximate=False)
        y = (h @ W2[eid] + b2[eid]) * probs[:, eid:eid + 1]
        return y.reshape(B, S, H)
    x = x + _L0_xattn_ref(_layernorm(x, axis=-1), ctx_1024)
    x = x + _L0_ffn_ref(_layernorm(x, axis=-1), L0_ffn_q_w, L0_ffn_q_b, L0_ffn_k_w, L0_ffn_k_b, L0_ffn_v_w, L0_ffn_v_b, L0_ffn_o_w, L0_ffn_o_b, L0_ffn_router_w, L0_ffn_router_b, L0_ffn_w1, L0_ffn_b1, L0_ffn_w2, L0_ffn_b2)
    x = x + _L1_xattn_ref(_layernorm(x, axis=-1), ctx_1024, L1_xattn_w_sim, L1_xattn_b_sim, L1_xattn_W_qv, L1_xattn_b_qv)
    x = x + _L1_ffn_ref(_layernorm(x, axis=-1), L1_ffn_Wr, L1_ffn_W1, L1_ffn_b1, L1_ffn_W2, L1_ffn_b2)
    return x

_drawn_inputs = setup_inputs


def setup_inputs(seed=0):
    import zlib

    import numpy as np

    out = dict(_drawn_inputs(seed))
    spreads = {'L0_ffn_q_b': (0.0, 0.8),
     'L0_ffn_k_b': (0.0, 2.0),
     'L0_ffn_v_b': (0.0, 0.8),
     'L0_ffn_o_b': (0.0, 0.8),
     'L0_ffn_router_b': (0.0, 0.8),
     'L0_ffn_b1': (0.0, 0.8),
     'L0_ffn_b2': (0.0, 0.8),
     'L1_ffn_b1': (0.0, 0.8),
     'L1_ffn_b2': (0.0, 2.0)}
    factors = {'L0_ffn_q_w': 8.0,
     'L0_ffn_k_w': 8.0,
     'L0_ffn_v_w': 8.0,
     'L0_ffn_o_w': 8.0,
     'L0_ffn_router_w': 8.0,
     'L0_ffn_w1': 8.0,
     'L0_ffn_w2': 8.0,
     'L1_xattn_w_sim': 5.483,
     'L1_xattn_b_qv': 6.286,
     'L1_ffn_Wr': 8.0,
     'L1_ffn_W1': 8.0,
     'L1_ffn_W2': 8.0}
    for name, (base, spread) in spreads.items():
        noise = np.random.default_rng([zlib.crc32(name.encode()), seed]).standard_normal(out[name].shape)
        drawn = base * np.exp(spread * noise) if base else spread * noise
        out[name] = jnp.asarray(drawn.astype(out[name].dtype))
    for name, factor in factors.items():
        out[name] = (out[name] * factor).astype(out[name].dtype)
    return out
```

```python
import concourse.bass as bass
from concourse import mybir
from contextlib import ExitStack

FP32 = mybir.dt.float32
FP32R = mybir.dt.float32r
BF16 = mybir.dt.bfloat16
U32 = mybir.dt.uint32
ALU = mybir.AluOpType
ACT = mybir.ActivationFunctionType
AX = mybir.AxisListType

P = 128
D = 128
S = 128
BATCH = 8
CTX = 77
HALF = 4
NHALF = BATCH // HALF
T = HALF * S
HEADS = 16
KPH = 4
LAT = HEADS * KPH
HD = D // HEADS
E0 = 8
F0 = 2
F1 = 4
E1 = 8
EID = E1 - 1
LN_EPS = 1e-5
TERMS = 6
Q_RUNS = ((0, 0, 3), (1, 3, 2), (2, 5, 1))
K_RUNS = ((0, 0, 3), (0, 3, 2), (0, 5, 1))
GROUPS = 4
LANES = 4
ROWS = 32
MAX_ROW = TERMS * KPH
PARTS = 3


def build(nc, x, ctx_in, q_w, q_b, k_w, k_b, v_w, v_b, o_w, o_b, router_w, router_b, w1, b1, w2, b2,
          w_sim, b_sim, w_qv, b_qv, wr, fw1, fb1, fw2, fb2, out):
    stack = ExitStack()
    with stack:
        def sb(name, shape, dt=FP32):
            return stack.enter_context(nc.sbuf_tensor(name, shape, dt))

        def sem(name):
            return stack.enter_context(nc.semaphore(name))

        x0 = sb("x0", [P, BATCH, D])
        x1 = sb("x1", [P, BATCH, D])
        y = x0
        xn = [sb(f"xn{i}", [P, BATCH, D]) for i in range(3)] + [x1]
        stats = sb("stats", [P, 4, BATCH, 6])
        mv = sb("mv", [P, 4, BATCH, 2])
        veps = sb("veps", [P, 4, BATCH])
        lnv = sb("lnv", [P, 4, BATCH])
        rstd = sb("rstd", [P, 4, BATCH])
        xT = [sb(f"xT{i}", [D, NHALF, T]) for i in range(2)]
        xT += xT
        ctxn = sb("ctxn", [CTX, BATCH, D])
        ctxT = sb("ctxT", [D, BATCH, CTX])
        ctxw = sb("ctxw", [D, BATCH, CTX])
        w2sq = sb("w2sq", [D, P])
        simrow = sb("simrow", [P, BATCH, CTX])
        sc = [sb("sc", [P, BATCH, CTX])] * 2
        pr = [sb("pr", [P, BATCH, CTX])] * 2
        mx = [sb(f"mx{i}", [P, BATCH]) for i in range(2)]
        rs = [sb(f"rs{i}", [P, BATCH]) for i in range(2)]
        rr = [sb(f"rr{i}", [P, BATCH]) for i in range(2)]
        pT = [sb("pT", [CTX, NHALF, T])] * 2
        wqk = sb("wqk", [D, 2 * LAT])
        qw_full = sb("qw_full", [D, D])
        wv = sb("wv", [D, LAT])
        vb = sb("vb", [P, LAT])
        qk = sb("qk", [P, NHALF, T])
        res1 = sb("res1", [P, NHALF, T])
        part = sb("part", [P, NHALF, PARTS, T], BF16)
        qbd = [sb(f"qbd{i}", [P, GROUPS, LANES, T], BF16) for i in range(NHALF)]
        kst = [sb(f"kst{i}", [P, GROUPS, T], BF16) for i in range(NHALF)]
        vpad = [sb(f"vpad{i}", [P, HALF, GROUPS, LANES, ROWS]) for i in range(NHALF)]
        dead = [v[:, :, :, :, :].rearrange("p b g j c -> p (b g j c)") for v in vpad]
        hT = dead[0].rearrange("p (a c t) -> p a c t", a=2, c=F0)
        gT = dead[0].rearrange("p (c t) -> p c t", c=F1)
        x2, x3 = (dead[1][:, n * BATCH * D:(n + 1) * BATCH * D].rearrange("p (b d) -> p b d", d=D) for n in range(2))
        nmax = sb("nmax", [P, BATCH, GROUPS, LANES])
        nres1 = sb("nres1", [P, BATCH, GROUPS, LANES])
        nres2 = sb("nres2", [P, BATCH, GROUPS, LANES])
        msp = sb("msp", [P, BATCH, LANES, PARTS, GROUPS], BF16)
        mT = sb("mT", [LANES * PARTS * GROUPS, BATCH, S], BF16)
        pexp = sb("pexp", [P, 3, LANES * S])
        un = sb("un", [P, 2, S])
        rden = sb("rden", [P, 2, S])
        aoT = sb("aoT", [P, NHALF, T])
        wo = sb("wo", [P, D])
        mlaT = sb("mlaT", [D, NHALF, T])
        mla_hi = sb("mla_hi", [D, NHALF, T], FP32R)
        mla_lo = sb("mla_lo", [D, NHALF, T], FP32R)
        rw = sb("rw", [D, E0])
        rb = sb("rb", [P, E0])
        iota = sb("iota", [P, E0])
        lg = sb("lg", [P, BATCH, E0])
        ex = sb("ex", [P, BATCH, E0])
        pb = sb("pb", [P, BATCH, E0])
        t1 = sb("t1", [P, BATCH])
        t2 = sb("t2", [P, BATCH])
        t3 = sb("t3", [P, BATCH])
        top = sb("top", [P, BATCH, 8])
        topi = sb("topi", [P, BATCH, 8], U32)
        topf = sb("topf", [P, BATCH, 2])
        eq = sb("eq", [P, 2, BATCH, E0])
        comb = sb("comb", [P, BATCH, E0])
        combT = sb("combT", [E0, NHALF, T])
        w1s = sb("w1s", [D, E0, F0 * P])
        w1_hi = sb("w1_hi", [D, E0, F0 * P], FP32R)
        w1_lo = sb("w1_lo", [D, E0, F0 * P], FP32R)
        w2s = sb("w2s", [P, E0 * F0, D])
        b2s = sb("b2s", [E0, D])
        wqv = sb("wqv", [D, 4, D])
        bqv = sb("bqv", [P, D])
        bsim = sb("bsim", [P, 1])
        hqT, hhT = qk, res1
        nbm = sb("nbm", [HALF, NHALF])
        bex = sb("bex", [HALF, NHALF, S])
        bsum = sb("bsum", [HALF, NHALF])
        brec = sb("brec", [HALF, NHALF])
        batt = sb("batt", [HALF, NHALF, S])
        battc = sb("battc", [P, BATCH])
        hcbar = sb("hcbar", [D, BATCH])
        w14 = xn[1]
        x2b = xn[0]
        wrn = sb("wrn", [E1, D])
        wrT = sb("wrT", [D, E1])
        f1s = sb("f1s", [D, F1 * P])
        f1_hi = sb("f1_hi", [D, F1 * P], FP32R)
        f1_lo = sb("f1_lo", [D, F1 * P], FP32R)
        f2s = sb("f2s", [P, F1, D])
        fb2s = sb("fb2s", [P, D])
        x4_hi, x4_lo = mla_hi, mla_lo
        ex7 = sb("ex7", [P, BATCH, E1])
        s7 = sb("s7", [P, BATCH])
        n7 = sb("n7", [P, BATCH])
        p7 = sb("p7", [P, BATCH])
        x3b = xn[2]
        ident = sb("ident", [P, P])
        identb = sb("identb", [P, P], BF16)
        selden = sb("selden", [P, P])
        ones = sb("ones", [P, P])
        NROW = E0 * F0 + F1 + 3 + 1 + 1
        R_FB1, R_SIM, R_OB, R_QK = E0 * F0, E0 * F0 + F1, E0 * F0 + F1 + 3, E0 * F0 + F1 + 4
        rows = sb("rows", [NROW, P])
        cols = sb("cols", [P, NROW])

        ps = stack.enter_context(nc.psum_tensor("ps", [P, 8, 512], FP32))
        scratch_q = nc.dram_tensor("scratch_q", (NHALF, LAT, TERMS, T), BF16, kind="Internal").ap()
        scratch_k = nc.dram_tensor("scratch_k", (NHALF, LAT, TERMS, T), BF16, kind="Internal").ap()

        names = """x_in0 x_in1 ctx_in small_in qkw_in vw_in ow_in w1_in w2_in qv_in f_in
            ident_ok identb_ok selden_ok zero_q ones_k zero_v ones_v wo_zero ones_ok iota_ok wqk_ok
            cols_ps cols_ok wr_ps wr_ok ctxw_ok w2sq_ok w1_split f1_split
            ln0_var ln1_var ln2_var ln3_var ln0_rstd ln1_rstd ln2_rstd ln3_rstd
            ln0_norm ln1_norm ln2_norm ln3_norm xT0_ps xT1_ps xT2_ps xT3_ps xT0_ok xT1_ok xT2_ok xT3_ok
            ctxT_ps ctxT_ok sc0_ps sc0_sub pr0_ok rr0_ok pT0_ps pT0_ok av0_ps x1_ok
            qk_ps qk_ok v_ps v_ok part_ok parts_out0 parts_out1 stack_in0 stack_in1
            s1_ps s1_max msp_ok mT_ps mT_ok mrow_in0 mrow_in1 mrow_in2 mrow_in3 mrow_in4 mrow_in5 mrow_in6 mrow_in7 s2_ps p_ok av_ps un_ok den_ps ao_ok
            o_ps mla_ok mlahi_ok mlalo_ok lg_ps lg_sub ex_ok comb_ok cT_ps cT_ok b2_ps x2_init
            h1_ps gelu_ok h2_ps moe_acc
            sr_ps sr_ok sim_ps sc1_ok sim_sub pr1_ok pn1_ok pT1_ps pT1_ok hq_ps hq_ok hh_ok
            mxT_ps nbm_ok bex_ok batt_ok bT_ps bT_ok hb_ps hb_ok w14_ok x2b_ok qv_ps x3_ok
            x4hi_ok x4lo_ok l7_ps l7_sub ex7_ok p7_ok x3b_ok f1_ps g_ok f2_ps y_ok stored
            dve_step act_step pool_step""".split()
        s = {n: sem(n) for n in names}

        def counter(eng, steps):
            done = [0]

            def did(ins):
                ins.then_inc(steps, 1)
                done[0] += 1
                return done[0]

            def after(n):
                eng.wait_ge(steps, n)

            return did, after

        def halves(h):
            return slice(h * HALF, (h + 1) * HALF)

        def wide(t):
            return lambda n: t.unsqueeze(2).to_broadcast([t.shape[0], t.shape[1], n])

        block = stack.enter_context(nc.Block())

        plan = []
        first = ["p1_stats", "p1_ctx", "p1_T", "p1_scores", "p1_soft", "p1_av", "p1_ln", "p1_T2", "p1_qkv", "p1_parts"]
        plan += [("setup", ())] + [(n, (0,)) for n in first]
        second = [(n, (1,)) for n in first]
        plan += second[:2]
        for b in range(2):
            for g in range(GROUPS):
                plan.append(("s1", (b, g)))
                plan += [second.pop(2)] if len(second) > 2 and g % 2 else []
            plan.append(("smax", (b,)))
        second = second[2:]
        for b in range(BATCH):
            for g in range(GROUPS):
                if b + 2 < BATCH:
                    plan.append(("s1", (b + 2, g)))
                plan.append(("s2", (b, g)))
                if g:
                    plan.append(("av", (b, g - 1)))
                plan += [second.pop(0)] if second and g % 2 else []
            plan.append(("av", (b, GROUPS - 1)))
            if b + 2 < BATCH:
                plan.append(("smax", (b + 2,)))
            plan.append(("norm", (b,)))
            if b == HALF:
                plan += [("oproj", (0,)), ("router", (0,))]
        plan += [("oproj", (1,)), ("router", (1,))]
        plan += [("moe_in", (0,))]
        p4 = ["p4_sim0", "p4_T", "p4_sim", "p4_soft", "p4_pT", "p4_batt", "p4_hq", "p4_hb", "p4_out"]
        plan += [("m1", (0, 0))]
        for e in range(E0):
            if e + 1 < E0:
                plan.append(("m1", (0, e + 1)))
            plan.append(("m2", (0, e)))
        plan += [("moe_in", (1,)), ("m1", (1, 0))]
        for e in range(E0):
            if e + 1 < E0:
                plan.append(("m1", (1, e + 1)))
            plan.append(("m2", (1, e)))
        plan += [(n, (0,)) for n in p4]
        p5 = ["p5_ln", "p5_T", "p5_router", "p5_f1", "p5_f2"]
        plan += [(n, (0,)) for n in p5]
        plan += [(n, (1,)) for n in p4 + p5]

        def run(stages):
            for name, args in plan:
                if name in stages:
                    stages[name](*args)

        @block.sync
        def _(sp):
            xv = x.rearrange("b t d -> t b d")
            sp.dma_start(x0[:, 0:HALF, :], xv[:, 0:HALF, :]).then_inc(s["x_in0"], 16)
            cv = ctx_in.rearrange("b t d -> t b d")
            sp.dma_start(ctxn[:, :, :], cv).then_inc(s["ctx_in"], 16)
            sp.dma_start(qw_full[:, :], q_w).then_inc(s["qkw_in"], 16)
            sp.dma_start(wqk[:, LAT:2 * LAT], k_w).then_inc(s["qkw_in"], 16)
            sp.dma_start(wv[:, :], v_w).then_inc(s["vw_in"], 16)
            sp.dma_start(vb[:, :], v_b.partition_broadcast(P)).then_inc(s["vw_in"], 16)
            small = [
                (rows[0:E0 * F0, :], b1.rearrange("e (c p) -> (e c) p", c=F0)),
                (rows[R_FB1:R_FB1 + F1, :], fb1[EID, :].rearrange("(c p) -> c p", c=F1)),
                (rows[R_SIM:R_SIM + 3, :], w_sim.rearrange("(c p) -> c p", c=3)),
                (rows[R_OB:R_OB + 1, :], o_b.rearrange("(a p) -> a p", a=1)),
                (rows[R_QK:R_QK + 1, 0:LAT].rearrange("a (h k) -> a h k", k=KPH),
                 q_b.rearrange("(a h d) -> a h d", a=1, d=HD)[:, :, 0:KPH]),
                (rows[R_QK:R_QK + 1, LAT:2 * LAT], k_b.rearrange("(a p) -> a p", a=1)),
            ]
            for dst, src in small:
                sp.dma_start(dst, src).then_inc(s["small_in"], 16)
            sp.dma_start(x0[:, HALF:BATCH, :], xv[:, HALF:BATCH, :]).then_inc(s["x_in1"], 16)
            sp.wait_ge(s["wo_zero"], 1)
            ow = o_w[0:LAT, :].rearrange("(g j v) d -> j g v d", g=GROUPS, j=LANES)
            for j in range(LANES):
                sp.dma_start(wo[ROWS * j:ROWS * j + LAT // LANES, :],
                             ow[j]).then_inc(s["ow_in"], 16)
            sp.dma_start(w1s[:, :, :], w1.rearrange("e p f -> p e f")).then_inc(s["w1_in"], 16)
            sp.dma_start(rw[:, :], router_w).then_inc(s["w1_in"], 16)
            sp.dma_start(rb[:, :], router_b.partition_broadcast(P)).then_inc(s["w1_in"], 16)

            def parts(h):
                sp.wait_ge(s["part_ok"], h + 1)
                for q, r, n in Q_RUNS:
                    sp.dma_start(scratch_q[h, :, r:r + n, :],
                                 part[0:LAT, h, q:q + 1, :].to_broadcast([LAT, n, T])).then_inc(s[f"parts_out{h}"], 16)
                for q, r, n in K_RUNS:
                    sp.dma_start(scratch_k[h, :, r:r + n, :],
                                 part[LAT:2 * LAT, h, q:q + n, :]).then_inc(s[f"parts_out{h}"], 16)
                sp.wait_ge(s[f"parts_out{h}"], 16 * (len(Q_RUNS) + len(K_RUNS)))
                sp.wait_ge(s["zero_q"], h + 1)
                sp.wait_ge(s["ones_k"], h + 1)
                for j in range(LANES):
                    rows_ = slice(ROWS * j, ROWS * j + MAX_ROW)
                    sq = scratch_q[h].rearrange("(g j k) r n -> j (k r) g n", g=GROUPS, j=LANES)[j]
                    sk = scratch_k[h].rearrange("(g j k) r n -> j (k r) g n", g=GROUPS, j=LANES)[j]
                    sp.dma_start(qbd[h][rows_, :, j, :], sq).then_inc(s[f"stack_in{h}"], 16)
                    sp.dma_start(kst[h][rows_, :, :], sk).then_inc(s[f"stack_in{h}"], 16)
                if h == 0:
                    sp.dma_start(w2s[:, :, :], w2.rearrange("e (c p) d -> p (e c) d", c=F0)).then_inc(s["w2_in"], 16)
                    sp.dma_start(b2s[:, :], b2).then_inc(s["w2_in"], 16)
                if h == 1:
                    sp.dma_start(wqv[:, :, :], w_qv.rearrange("(k p) d -> p k d", k=4)).then_inc(s["qv_in"], 16)
                    sp.dma_start(bqv[:, :], b_qv.partition_broadcast(P)).then_inc(s["qv_in"], 16)
                    sp.dma_start(bsim[:, :], b_sim.partition_broadcast(P)).then_inc(s["qv_in"], 16)
                    sp.dma_start(f1s[:, :], fw1[EID]).then_inc(s["f_in"], 16)
                    sp.dma_start(f2s[:, :, :], fw2[EID].rearrange("(c p) d -> p c d", c=F1)).then_inc(s["f_in"], 16)
                    sp.dma_start(fb2s[:, :], fb2[EID].partition_broadcast(P)).then_inc(s["f_in"], 16)
                    sp.dma_start(wrn[:, :], wr).then_inc(s["f_in"], 16)

            def smax(b):
                sp.wait_ge(s["mT_ok"], b + 1)
                n = PARTS * GROUPS
                for j in range(LANES):
                    sp.dma_start(
                        qbd[b // HALF][ROWS * j + MAX_ROW:ROWS * j + MAX_ROW + PARTS, :, j, (b % HALF) * S:(b % HALF + 1) * S],
                        mT[n * j:n * (j + 1), b, :],
                    ).then_inc(s[f"mrow_in{b}"], 16)

            def store(h):
                sp.wait_ge(s["y_ok"], HALF * (h + 1))
                sp.dma_start(out.rearrange("b t d -> t b d")[:, halves(h), :], y[:, halves(h), :]).then_inc(s["stored"], 16)

            run({"p1_parts": parts, "smax": smax, "p5_f2": store})
            sp.wait_ge(s["stored"], 16 * NHALF)

        @block.gpsimd
        def _(pool):
            did, after = counter(pool, s["pool_step"])
            a = did(pool.memset(ident[:, :], 0.0))
            after(a)
            pool.affine_select(out=ident[:, :], in_=ident[:, :], compare_op=ALU.not_equal, fill=1.0, base=0,
                               pattern=[[-1, P]], channel_multiplier=1).then_inc(s["ident_ok"], 1)
            pool.memset(wo[:, :], 0.0).then_inc(s["wo_zero"], 1)
            pool.wait_ge(s["qkw_in"], 32)
            pool.tensor_copy(wqk[:, 0:LAT].rearrange("p (h k) -> p h k", k=KPH),
                             qw_full[:, :].rearrange("p (h d) -> p h d", d=HD)[:, :, 0:KPH]).then_inc(s["wqk_ok"], 1)
            for h in range(NHALF):
                if h == 0:
                    pool.memset(kst[h][:, :, :], 1.0).then_inc(s["ones_k"], 1)
                a = did(pool.memset(vpad[h][:, :, :, :, :], 0.0))
                after(a)
                for g in range(GROUPS):
                    last = pool.memset(vpad[h][:, :, g, :, 16 + KPH * g:16 + KPH * (g + 1)], 1.0)
                last.then_inc(s["ones_v"], 1)
                if h == 0:
                    a = did(pool.memset(identb[:, :], 0.0))
                    after(a)
                    pool.affine_select(out=identb[:, :], in_=identb[:, :], compare_op=ALU.not_equal, fill=1.0, base=0,
                                       pattern=[[-1, P]], channel_multiplier=1).then_inc(s["identb_ok"], 1)
                    a = did(pool.memset(selden[:, :], 0.0))
                    after(a)
                    v = selden[:, :].rearrange("p (j x) -> p j x", j=LANES)
                    for lo, base in ((0, -16), (16, -16)):
                        last = pool.affine_select(out=v[:, :, lo:lo + 16], in_=v[:, :, lo:lo + 16], compare_op=ALU.not_equal,
                                                  fill=1.0, base=base, pattern=[[-ROWS, LANES], [-1, 16]], channel_multiplier=1)
                    last.then_inc(s["selden_ok"], 1)
                    pool.memset(kst[1][:, :, :], 1.0).then_inc(s["ones_k"], 1)
                    pool.memset(qbd[1][:, :, :, :], 0.0).then_inc(s["zero_q"], 1)
            for e in range(E0):
                last = pool.memset(iota[:, e:e + 1], float(e))
            last.then_inc(s["iota_ok"], 1)
            pool.wait_ge(s["w1_in"], 48)
            a = did(pool.tensor_copy(w1_hi[:, :, :], w1s[:, :, :]))
            after(a)
            pool.tensor_tensor(out=w1_lo[:, :, :], in0=w1s[:, :, :], in1=w1_hi[:, :, :].bitcast(FP32),
                               op=ALU.subtract).then_inc(s["w1_split"], 1)
            pool.wait_ge(s["f_in"], 64)
            a = did(pool.tensor_copy(f1_hi[:, :], f1s[:, :]))
            after(a)
            pool.tensor_tensor(out=f1_lo[:, :], in0=f1s[:, :], in1=f1_hi[:, :].bitcast(FP32),
                               op=ALU.subtract).then_inc(s["f1_split"], 1)

            def x2_bias(h):
                pool.wait_ge(s["moe_acc"], HALF * E0 * (h + 1))
                pool.wait_ge(s["qv_in"], 48)
                pool.tensor_tensor(out=x2b[:, halves(h), :], in0=x2[:, halves(h), :],
                                   in1=bqv[:, :].unsqueeze(1).to_broadcast([P, HALF, D]), op=ALU.add).then_inc(s["x2b_ok"], 1)

            run({"p4_T": x2_bias})

        @block.scalar
        def _(act):
            did, after = counter(act, s["act_step"])
            act.preload_act_table_set("natural_log_exp_and_others")

            def rstd_of(i, h):
                act.wait_ge(s[f"ln{i}_var"], h + 1)
                a = did(act.activation(lnv[:, i, halves(h)], veps[:, i, halves(h)], ACT.Ln))
                after(a)
                act.activation(rstd[:, i, halves(h)], lnv[:, i, halves(h)], ACT.Exp, scale=-0.5).then_inc(s[f"ln{i}_rstd"], 1)

            def xT_of(i, h, bank):
                act.wait_ge(s[f"xT{i}_ps"], h + 1)
                act.activation(xT[i][:, h, :], ps[:, bank, :], ACT.Copy).then_inc(s[f"xT{i}_ok"], 1)

            def setup():
                act.wait_ge(s["cols_ps"], 1)
                act.activation(cols[:, :], ps[:, 5, 0:NROW], ACT.Copy).then_inc(s["cols_ok"], 1)

            def ctx_T(h):
                act.wait_ge(s["ctxT_ps"], h + 1)
                act.activation(ctxT[:, halves(h), :], ps[:, 7, 0:HALF * CTX].rearrange("p (b c) -> p b c", c=CTX),
                               ACT.Copy).then_inc(s["ctxT_ok"], 1)

            def soft0(h):
                act.wait_ge(s["sc0_sub"], h + 1)
                act.activation(pr[0][:, halves(h), :], sc[0][:, halves(h), :], ACT.Exp).then_inc(s["pr0_ok"], 1)

            def pT0(h):
                act.wait_ge(s["pT0_ps"], h + 1)
                act.activation(pT[0][:, h, :], ps[0:CTX, 6, :], ACT.Copy).then_inc(s["pT0_ok"], 1)

            def qk_bias(h):
                act.wait_ge(s["qk_ps"], h + 1)
                if h == 0:
                    act.wait_ge(s["cols_ok"], 1)
                act.activation(qk[:, h, :], ps[:, 7, :], ACT.Identity, bias=cols[:, R_QK:R_QK + 1]).then_inc(s["qk_ok"], 1)

            def maxT(b):
                act.wait_ge(s["mT_ps"], b + 1)
                act.activation(mT[:, b, :], ps[0:LANES * PARTS * GROUPS, 4, 0:S], ACT.Copy).then_inc(s["mT_ok"], 1)

            def soft(b, g):
                n = b * GROUPS + g
                act.wait_ge(s["s2_ps"], n + 1)
                if n >= 3:
                    act.wait_ge(s["av_ps"], n - 2)
                act.activation(pexp[:, n % 3, :], ps[:, 2 + n % 2, :], ACT.Exp, scale=KPH ** -0.5).then_inc(s["p_ok"], 1)

            def unnorm(b):
                act.wait_ge(s["av_ps"], GROUPS * (b + 1))
                if b >= 2:
                    act.wait_ge(s["ao_ok"], b - 1)
                act.activation(un[:, b % 2, :], ps[:, 5, 0:S], ACT.Copy).then_inc(s["un_ok"], 1)

            def oproj(h):
                act.wait_ge(s["o_ps"], h + 1)
                act.activation(mlaT[:, h, :], ps[:, 4, :], ACT.Identity, bias=cols[:, R_OB:R_OB + 1]).then_inc(s["mla_ok"], 1)
                act.wait_ge(s["mla_ok"], h + 1)
                act.activation(mla_hi[:, h, :], mlaT[:, h, :], ACT.Copy).then_inc(s["mlahi_ok"], 1)

            def router(h):
                act.wait_ge(s["lg_sub"], h + 1)
                act.activation(ex[:, halves(h), :], lg[:, halves(h), :], ACT.Exp).then_inc(s["ex_ok"], 1)

            def comb_T(h):
                act.wait_ge(s["cT_ps"], h + 1)
                act.activation(combT[:, h, :], ps[0:E0, 4, :], ACT.Copy).then_inc(s["cT_ok"], 1)

            def gelu0(h, e):
                k = h * E0 + e
                for c in range(F0):
                    act.wait_ge(s["h1_ps"], F0 * k + c + 1)
                    if k >= 2:
                        act.wait_ge(s["h2_ps"], k - 1)
                    act.activation(hT[:, k % 2, c, :], ps[:, c, :], ACT.Gelu,
                                   bias=cols[:, e * F0 + c:e * F0 + c + 1]).then_inc(s["gelu_ok"], 1)

            def sim0(h):
                act.wait_ge(s["sr_ps"], h + 1)
                act.wait_ge(s["qv_in"], 48)
                act.activation(simrow[:, halves(h), :], ps[:, 7, 0:HALF * CTX].rearrange("p (b c) -> p b c", c=CTX),
                               ACT.Identity, bias=bsim[:, 0:1]).then_inc(s["sr_ok"], 1)

            def soft1(h):
                act.wait_ge(s["sim_sub"], h + 1)
                act.activation(pr[1][:, halves(h), :], sc[1][:, halves(h), :], ACT.Exp).then_inc(s["pr1_ok"], 1)

            def pT1(h):
                act.wait_ge(s["pT1_ps"], h + 1)
                act.activation(pT[1][:, h, :], ps[0:CTX, 6, :], ACT.Copy).then_inc(s["pT1_ok"], 1)

            def batt_exp(h):
                act.wait_ge(s["nbm_ok"], h + 1)
                act.activation(bex[:, h, :], ps[0:HALF, 5, 0:S], ACT.Exp, bias=nbm[:, h:h + 1],
                               accum_out=bsum[:, h:h + 1]).then_inc(s["bex_ok"], 1)
                act.wait_ge(s["bT_ps"], h + 1)
                act.activation(battc[:, halves(h)], ps[:, 5, 0:HALF], ACT.Copy).then_inc(s["bT_ok"], 1)

            def hq(h):
                act.wait_ge(s["hq_ps"], h + 1)
                act.activation(hqT[:, h, :], ps[:, 7, :], ACT.Copy).then_inc(s["hq_ok"], 1)

            def hbar(h):
                act.wait_ge(s["hb_ps"], h + 1)
                act.activation(hcbar[:, halves(h)], ps[:, 5, 0:HALF], ACT.Copy).then_inc(s["hb_ok"], 1)

            def x4T(h):
                xT_of(3, h, 6)
                act.activation(x4_hi[:, h, :], ps[:, 6, :], ACT.Copy).then_inc(s["x4hi_ok"], 1)

            def router1(h):
                if h == 0:
                    act.wait_ge(s["wr_ps"], 1)
                    act.activation(wrT[:, :], ps[:, 4, 64:64 + E1], ACT.Copy).then_inc(s["wr_ok"], 1)
                act.wait_ge(s["l7_sub"], h + 1)
                act.activation(ex7[:, halves(h), :], lg[:, halves(h), :], ACT.Exp).then_inc(s["ex7_ok"], 1)

            def gelu1(h):
                for c in range(F1):
                    k = F1 * h + c
                    act.wait_ge(s["f1_ps"], k + 1)
                    if h:
                        act.wait_ge(s["f2_ps"], HALF * h)
                    act.activation(gT[:, c, :], ps[:, k % 2, :], ACT.Gelu,
                                   bias=cols[:, R_FB1 + c:R_FB1 + c + 1]).then_inc(s["g_ok"], 1)

            run({"setup": setup, "p1_stats": lambda h: rstd_of(0, h), "p1_ctx": ctx_T, "p1_T": lambda h: xT_of(0, h, 6),
                 "p1_soft": soft0, "p1_av": pT0, "p1_ln": lambda h: rstd_of(1, h), "p1_T2": lambda h: xT_of(1, h, 6),
                 "p1_qkv": qk_bias, "smax": maxT, "s2": soft, "norm": unnorm, "oproj": oproj, "router": router,
                 "moe_in": comb_T, "m1": gelu0, "p4_sim0": sim0,
                 "p4_T": lambda h: (rstd_of(2, h), xT_of(2, h, 6)), "p4_soft": soft1, "p4_pT": pT1, "p4_batt": batt_exp,
                 "p4_hq": hq, "p4_hb": hbar, "p5_ln": lambda h: rstd_of(3, h), "p5_T": x4T, "p5_router": router1, "p5_f1": gelu1})

        @block.vector
        def _(dve):
            did, after = counter(dve, s["dve_step"])
            dve.memset(qbd[0][:, :, :, :].bitcast(U32), 0).then_inc(s["zero_q"], 1)
            dve.memset(ones[:, :], 1.0).then_inc(s["ones_ok"], 1)

            def var_of(i, src, h):
                for b in range(h * HALF, (h + 1) * HALF):
                    a = did(dve.bn_stats(stats[:, i, b, :], src[:, b, :]))
                after(a)
                for b in range(h * HALF, (h + 1) * HALF):
                    a = did(dve.bn_aggr(mv[:, i, b, :], stats[:, i, b, :]))
                after(a)
                dve.tensor_scalar(veps[:, i, halves(h)], mv[:, i, halves(h), 1], LN_EPS, None, ALU.add).then_inc(s[f"ln{i}_var"], 1)

            def norm_of(i, src, h):
                dve.wait_ge(s[f"ln{i}_rstd"], h + 1)
                for b in range(h * HALF, (h + 1) * HALF):
                    last = dve.tensor_scalar(xn[i][:, b, :], src[:, b, :], mv[:, i, b, 0:1], rstd[:, i, b:b + 1],
                                             ALU.subtract, ALU.mult)
                last.then_inc(s[f"ln{i}_norm"], 1)

            def stats0(h):
                dve.wait_ge(s[f"x_in{h}"], 16)
                var_of(0, x0, h)
                norm_of(0, x0, h)

            def ctx_w(h):
                dve.wait_ge(s["ctxT_ok"], h + 1)
                dve.wait_ge(s["cols_ok"], 1)
                dve.tensor_scalar(ctxw[:, halves(h), :], ctxT[:, halves(h), :], cols[:, R_SIM + 2:R_SIM + 3],
                                  cols[:, R_SIM:R_SIM + 1], ALU.mult, ALU.add).then_inc(s["ctxw_ok"], 1)
                if h == 0:
                    dve.wait_ge(s["ones_ok"], 1)
                    dve.tensor_scalar(w2sq[:, :], ones[:, :], cols[:, R_SIM + 1:R_SIM + 2], None, ALU.mult).then_inc(s["w2sq_ok"], 1)

            def scores0(h):
                dve.wait_ge(s["sc0_ps"], h + 1)
                v = ps[:, 7, 0:HALF * CTX].rearrange("p (b c) -> p b c", c=CTX)
                a = did(dve.tensor_reduce(mx[0][:, halves(h)], v, axis=AX.X, op=ALU.max))
                after(a)
                dve.tensor_tensor(out=sc[0][:, halves(h), :], in0=v, in1=wide(mx[0][:, halves(h)])(CTX),
                                  op=ALU.subtract).then_inc(s["sc0_sub"], 1)

            def soft0(h):
                dve.wait_ge(s["pr0_ok"], h + 1)
                a = did(dve.tensor_reduce(rs[0][:, halves(h)], pr[0][:, halves(h), :], axis=AX.X, op=ALU.add))
                after(a)
                dve.reciprocal(rr[0][:, halves(h)], rs[0][:, halves(h)]).then_inc(s["rr0_ok"], 1)

            def av0(h):
                dve.wait_ge(s["av0_ps"], h + 1)
                dve.wait_ge(s["rr0_ok"], h + 1)
                for i in range(HALF):
                    b = h * HALF + i
                    dve.scalar_tensor_tensor(out=x1[:, b, :], in0=ps[:, 7, i * D:(i + 1) * D], scalar=rr[0][:, b:b + 1],
                                             in1=x0[:, b, :], op0=ALU.mult, op1=ALU.add).then_inc(s["x1_ok"], 1)

            def ln1(h):
                dve.wait_ge(s["x1_ok"], HALF * (h + 1))
                var_of(1, x1, h)
                norm_of(1, x1, h)

            def qkv(h):
                dve.wait_ge(s["qk_ok"], h + 1)
                a = did(dve.tensor_copy(part[:, h, 0, :], qk[:, h, :]))
                dve.wait_ge(s["v_ps"], h + 1)
                dve.wait_ge(s["ones_v"], h + 1)
                dve.wait_ge(s["vw_in"], 32)
                for g in range(GROUPS):
                    w = GROUPS * KPH
                    last = dve.tensor_tensor(
                        out=vpad[h][:, :, g, :, KPH * g:KPH * (g + 1)],
                        in0=ps[:, 6, 0:HALF * LAT].rearrange("p (b n) -> p b n", n=LAT)[:, :, w * g:w * (g + 1)].rearrange("p b (j v) -> p b j v", v=KPH),
                        in1=vb[:, w * g:w * (g + 1)].rearrange("p (j v) -> p j v", v=KPH).unsqueeze(1).to_broadcast([P, HALF, LANES, KPH]),
                        op=ALU.add)
                last.then_inc(s["v_ok"], 1)
                after(a)
                a = did(dve.tensor_tensor(out=res1[:, h, :], in0=qk[:, h, :], in1=part[:, h, 0, :], op=ALU.subtract))
                after(a)
                a = did(dve.tensor_copy(part[:, h, 1, :], res1[:, h, :]))
                after(a)
                dve.tensor_tensor(out=part[:, h, 2, :], in0=res1[:, h, :], in1=part[:, h, 1, :],
                                  op=ALU.subtract).then_inc(s["part_ok"], 1)

            def s1(b, g):
                n = b * GROUPS + g
                dve.wait_ge(s["s1_ps"], n + 1)
                dve.tensor_reduce(nmax[:, b, g, :], ps[:, n % 2, :].rearrange("p (j t) -> p j t", t=S), axis=AX.X,
                                  op=ALU.max, negate=True).then_inc(s["s1_max"], 1)

            def smax(b):
                dve.wait_ge(s["s1_max"], GROUPS * (b + 1))
                v = nmax[:, b].rearrange("p g j -> p j g")
                r1 = nres1[:, b].rearrange("p g j -> p j g")
                r2 = nres2[:, b].rearrange("p g j -> p j g")
                a = did(dve.tensor_copy(msp[:, b, :, 0, :], v))
                after(a)
                a = did(dve.tensor_tensor(out=r1, in0=v, in1=msp[:, b, :, 0, :], op=ALU.subtract))
                after(a)
                a = did(dve.tensor_copy(msp[:, b, :, 1, :], r1))
                after(a)
                dve.tensor_tensor(out=msp[:, b, :, 2, :], in0=r1, in1=msp[:, b, :, 1, :], op=ALU.subtract).then_inc(s["msp_ok"], 1)

            def norm(b):
                dve.wait_ge(s["den_ps"], b + 1)
                a = did(dve.reciprocal(rden[:, b % 2, :], ps[:, 4, 0:S]))
                after(a)
                h, i = b // HALF, b % HALF
                dve.wait_ge(s["un_ok"], b + 1)
                dve.tensor_tensor(out=aoT[:, h, i * S:(i + 1) * S], in0=un[:, b % 2, :], in1=rden[:, b % 2, :],
                                  op=ALU.mult).then_inc(s["ao_ok"], 1)

            def oproj(h):
                dve.wait_ge(s["mlahi_ok"], h + 1)
                dve.tensor_tensor(out=mla_lo[:, h, :], in0=mlaT[:, h, :], in1=mla_hi[:, h, :].bitcast(FP32),
                                  op=ALU.subtract).then_inc(s["mlalo_ok"], 1)

            def logits(h, bias, psum_ready, sub_done, neg):
                v = ps[:, 4, 0:HALF * E0].rearrange("p (b e) -> p b e", e=E0)
                hs = halves(h)
                dve.wait_ge(psum_ready, h + 1)
                if bias is None:
                    a = did(dve.tensor_copy(pb[:, hs, :], v))
                else:
                    a = did(dve.tensor_tensor(out=pb[:, hs, :], in0=v, in1=bias[:, :].unsqueeze(1).to_broadcast([P, HALF, E0]), op=ALU.add))
                after(a)
                a = did(dve.tensor_reduce(neg[:, hs], pb[:, hs, :], axis=AX.X, op=ALU.max, negate=True))
                after(a)
                dve.tensor_tensor(out=lg[:, hs, :], in0=pb[:, hs, :], in1=wide(neg[:, hs])(E0), op=ALU.add).then_inc(sub_done, 1)

            def router(h):
                hs = halves(h)
                dve.wait_ge(s["w1_in"], 48)
                logits(h, rb, s["lg_ps"], s["lg_sub"], t1)
                dve.wait_ge(s["ex_ok"], h + 1)
                a = did(dve.tensor_reduce(t2[:, hs], ex[:, hs, :], axis=AX.X, op=ALU.add))
                after(a)
                a = did(dve.reciprocal(t3[:, hs], t2[:, hs]))
                after(a)
                a = did(dve.tensor_tensor(out=pb[:, hs, :], in0=ex[:, hs, :], in1=wide(t3[:, hs])(E0), op=ALU.mult))
                after(a)
                for b in range(h * HALF, (h + 1) * HALF):
                    a = did(dve.max(top[:, b, :], pb[:, b, :]))
                after(a)
                for b in range(h * HALF, (h + 1) * HALF):
                    a = did(dve.max_index(topi[:, b, :], top[:, b, :], pb[:, b, :]))
                c = did(dve.tensor_tensor(out=t1[:, hs], in0=top[:, hs, 0], in1=top[:, hs, 1], op=ALU.add))
                after(a)
                a = did(dve.tensor_copy(topf[:, hs, :], topi[:, hs, 0:2]))
                after(c)
                c = did(dve.tensor_scalar(t2[:, hs], t1[:, hs], 1e-8, None, ALU.add))
                after(c)
                c = did(dve.reciprocal(t3[:, hs], t2[:, hs]))
                dve.wait_ge(s["iota_ok"], 1)
                after(a)
                for k in range(2):
                    a = did(dve.tensor_tensor(out=eq[:, k, hs, :], in0=iota[:, :].unsqueeze(1).to_broadcast([P, HALF, E0]),
                                                   in1=wide(topf[:, hs, k])(E0), op=ALU.is_equal))
                after(a)
                for k in range(2):
                    a = did(dve.tensor_tensor(out=eq[:, k, hs, :], in0=eq[:, k, hs, :], in1=wide(top[:, hs, k])(E0), op=ALU.mult))
                after(a)
                a = did(dve.tensor_tensor(out=eq[:, 0, hs, :], in0=eq[:, 0, hs, :], in1=eq[:, 1, hs, :], op=ALU.add))
                after(max(a, c))
                a = did(dve.tensor_tensor(out=eq[:, 1, hs, :], in0=eq[:, 0, hs, :], in1=wide(t3[:, hs])(E0), op=ALU.mult))
                after(a)
                dve.tensor_scalar(comb[:, hs, :], eq[:, 1, hs, :], 0.3, None, ALU.mult).then_inc(s["comb_ok"], 1)

            def moe_in(h):
                hs = halves(h)
                a = did(dve.tensor_tensor(out=x2[:, hs, :], in0=x1[:, hs, :], in1=xn[1][:, hs, :], op=ALU.add))
                after(a)
                dve.wait_ge(s["b2_ps"], h + 1)
                dve.tensor_tensor(out=x2[:, hs, :], in0=ps[:, 5, :].rearrange("p (b d) -> p b d", d=D), in1=x2[:, hs, :],
                                  op=ALU.add).then_inc(s["x2_init"], 1)

            def acc(h, e):
                k = h * E0 + e
                dve.wait_ge(s["h2_ps"], k + 1)
                if e == 0:
                    dve.wait_ge(s["x2_init"], h + 1)
                for i in range(HALF):
                    b = h * HALF + i
                    if e:
                        dve.wait_ge(s["moe_acc"], HALF * (k - 1) + i + 1)
                    dve.scalar_tensor_tensor(out=x2[:, b, :], in0=ps[:, 2 + k % 2, i * D:(i + 1) * D], scalar=comb[:, b, e:e + 1],
                                             in1=x2[:, b, :], op0=ALU.mult, op1=ALU.add).then_inc(s["moe_acc"], 1)

            def ln2(h):
                dve.wait_ge(s["moe_acc"], HALF * E0 * (h + 1))
                var_of(2, x2, h)
                norm_of(2, x2, h)

            def sim(h):
                hs = halves(h)
                dve.wait_ge(s["sim_ps"], h + 1)
                dve.wait_ge(s["sr_ok"], h + 1)
                dve.tensor_tensor(out=sc[1][:, hs, :], in0=ps[:, 7, 0:HALF * CTX].rearrange("p (b c) -> p b c", c=CTX),
                                  in1=simrow[:, hs, :], op=ALU.add).then_inc(s["sc1_ok"], 1)
                dve.wait_ge(s["sc1_ok"], h + 1)
                a = did(dve.tensor_reduce(mx[1][:, hs], sc[1][:, hs, :], axis=AX.X, op=ALU.max))
                after(a)
                dve.tensor_tensor(out=sc[1][:, hs, :], in0=sc[1][:, hs, :], in1=wide(mx[1][:, hs])(CTX),
                                  op=ALU.subtract).then_inc(s["sim_sub"], 1)

            def soft1(h):
                hs = halves(h)
                dve.wait_ge(s["pr1_ok"], h + 1)
                a = did(dve.tensor_reduce(rs[1][:, hs], pr[1][:, hs, :], axis=AX.X, op=ALU.add))
                after(a)
                a = did(dve.reciprocal(rr[1][:, hs], rs[1][:, hs]))
                after(a)
                dve.tensor_tensor(out=pr[1][:, hs, :], in0=pr[1][:, hs, :], in1=wide(rr[1][:, hs])(CTX),
                                  op=ALU.mult).then_inc(s["pn1_ok"], 1)

            def batt_of(h):
                dve.wait_ge(s["mxT_ps"], h + 1)
                dve.tensor_reduce(nbm[:, h:h + 1], ps[0:HALF, 5, 0:S], axis=AX.X, op=ALU.max, negate=True).then_inc(s["nbm_ok"], 1)
                dve.wait_ge(s["bex_ok"], h + 1)
                a = did(dve.reciprocal(brec[:, h:h + 1], bsum[:, h:h + 1]))
                after(a)
                dve.tensor_scalar(batt[:, h, :], bex[:, h, :], brec[:, h:h + 1], None, ALU.mult).then_inc(s["batt_ok"], 1)

            def hh(h):
                dve.wait_ge(s["hq_ok"], h + 1)
                dve.tensor_tensor(out=hhT[:, h, :], in0=hqT[:, h, :], in1=xT[2][:, h, :], op=ALU.mult).then_inc(s["hh_ok"], 1)

            def hb(h):
                dve.wait_ge(s["hb_ok"], h + 1)
                dve.wait_ge(s["qv_in"], 48)
                for b in range(h * HALF, (h + 1) * HALF):
                    last = dve.scalar_tensor_tensor(out=w14[:, b, :], in0=wqv[:, 3, :], scalar=hcbar[:, b:b + 1],
                                                    in1=wqv[:, 0, :], op0=ALU.mult, op1=ALU.add)
                last.then_inc(s["w14_ok"], 1)

            def p4_out(h):
                dve.wait_ge(s["qv_ps"], h + 1)
                dve.wait_ge(s["x2b_ok"], h + 1)
                dve.tensor_tensor(out=x3[:, halves(h), :], in0=ps[:, 7, :].rearrange("p (b d) -> p b d", d=D),
                                  in1=x2b[:, halves(h), :], op=ALU.add).then_inc(s["x3_ok"], 1)

            def ln3(h):
                dve.wait_ge(s["x3_ok"], h + 1)
                var_of(3, x3, h)
                norm_of(3, x3, h)

            def x4_low(h):
                dve.wait_ge(s["xT3_ok"], h + 1)
                dve.wait_ge(s["x4hi_ok"], h + 1)
                dve.tensor_tensor(out=x4_lo[:, h, :], in0=xT[3][:, h, :], in1=x4_hi[:, h, :].bitcast(FP32),
                                  op=ALU.subtract).then_inc(s["x4lo_ok"], 1)

            def router1(h):
                hs = halves(h)
                logits(h, None, s["l7_ps"], s["l7_sub"], n7)
                dve.wait_ge(s["ex7_ok"], h + 1)
                a = did(dve.tensor_reduce(s7[:, hs], ex7[:, hs, :], axis=AX.X, op=ALU.add))
                after(a)
                a = did(dve.reciprocal(n7[:, hs], s7[:, hs]))
                after(a)
                dve.tensor_tensor(out=p7[:, hs], in0=ex7[:, hs, EID], in1=n7[:, hs], op=ALU.mult).then_inc(s["p7_ok"], 1)
                dve.wait_ge(s["p7_ok"], h + 1)
                dve.wait_ge(s["f_in"], 64)
                for b in range(h * HALF, (h + 1) * HALF):
                    last = dve.scalar_tensor_tensor(out=x3b[:, b, :], in0=fb2s[:, :], scalar=p7[:, b:b + 1],
                                                    in1=x3[:, b, :], op0=ALU.mult, op1=ALU.add)
                last.then_inc(s["x3b_ok"], 1)

            def last_add(h):
                dve.wait_ge(s["x3b_ok"], h + 1)
                for i in range(HALF):
                    b = h * HALF + i
                    dve.wait_ge(s["f2_ps"], b + 1)
                    dve.scalar_tensor_tensor(out=y[:, b, :], in0=ps[:, 2 + b % 2, 0:D], scalar=p7[:, b:b + 1],
                                             in1=x3b[:, b, :], op0=ALU.mult, op1=ALU.add).then_inc(s["y_ok"], 1)

            run({"p1_stats": stats0, "p1_ctx": ctx_w, "p1_scores": scores0, "p1_soft": soft0, "p1_av": av0, "p1_ln": ln1,
                 "p1_qkv": qkv, "s1": s1, "smax": smax, "norm": norm, "oproj": oproj, "router": router, "moe_in": moe_in,
                 "m2": acc, "p4_T": ln2, "p4_sim": sim, "p4_soft": soft1, "p4_batt": batt_of, "p4_hq": hh, "p4_hb": hb,
                 "p4_out": p4_out, "p5_ln": ln3, "p5_T": x4_low, "p5_router": router1, "p5_f2": last_add})

        @block.tensor
        def _(pe):
            def mm(dst, lhsT, rhs, start=True, stop=True):
                return nc.tensor.matmul(dst, lhsT, rhs, start=start, stop=stop)

            def setup():
                pe.wait_ge(s["ident_ok"], 1)
                pe.wait_ge(s["small_in"], 96)
                nc.tensor.transpose(ps[:, 5, 0:NROW], rows[:, :], ident[0:NROW, 0:NROW]).then_inc(s["cols_ps"], 1)

            def to_T(i, h, bank):
                pe.wait_ge(s[f"ln{i}_norm"], h + 1)
                for n in range(HALF):
                    last = nc.tensor.transpose(ps[:, bank, n * S:(n + 1) * S], xn[i][:, h * HALF + n, :], ident[:, :])
                last.then_inc(s[f"xT{i}_ps"], 1)

            def ctx_T(h):
                pe.wait_ge(s["ctx_in"], 16)
                if h:
                    pe.wait_ge(s["qk_ok"], h)
                for n in range(HALF):
                    last = nc.tensor.transpose(ps[:, 7, n * CTX:(n + 1) * CTX], ctxn[:, h * HALF + n, :], ident[0:CTX, 0:CTX])
                last.then_inc(s["ctxT_ps"], 1)

            def xT0(h):
                if h:
                    pe.wait_ge(s["v_ok"], h)
                to_T(0, h, 6)

            def scores0(h):
                pe.wait_ge(s["xT0_ok"], h + 1)
                pe.wait_ge(s["ctxT_ok"], h + 1)
                for n in range(HALF):
                    last = mm(ps[:, 7, n * CTX:(n + 1) * CTX], xT[0][:, h, n * S:(n + 1) * S], ctxT[:, h * HALF + n, :])
                last.then_inc(s["sc0_ps"], 1)

            def av0(h):
                pe.wait_ge(s["pr0_ok"], h + 1)
                for n in range(HALF):
                    last = nc.tensor.transpose(ps[0:CTX, 6, n * S:(n + 1) * S], pr[0][:, h * HALF + n, :], ident[:, :])
                last.then_inc(s["pT0_ps"], 1)
                pe.wait_ge(s["sc0_sub"], h + 1)
                pe.wait_ge(s["pT0_ok"], h + 1)
                for n in range(HALF):
                    last = mm(ps[:, 7, n * D:(n + 1) * D], pT[0][:, h, n * S:(n + 1) * S], ctxn[:, h * HALF + n, :])
                last.then_inc(s["av0_ps"], 1)

            def qkv(h):
                pe.wait_ge(s["xT1_ok"], h + 1)
                pe.wait_ge(s["wqk_ok"], 1)
                pe.wait_ge(s["x1_ok"], HALF * (h + 1))
                mm(ps[:, 7, :], wqk[:, :], xT[1][:, h, :]).then_inc(s["qk_ps"], 1)
                pe.wait_ge(s["vw_in"], 32)
                for n in range(HALF):
                    last = mm(ps[:, 6, n * LAT:(n + 1) * LAT], xT[1][:, h, n * S:(n + 1) * S], wv[:, :])
                last.then_inc(s["v_ps"], 1)

            def cols_of(b):
                return slice((b % HALF) * S, (b % HALF + 1) * S)

            def s1(b, g):
                n, h = b * GROUPS + g, b // HALF
                pe.wait_ge(s[f"stack_in{h}"], 16 * 2 * LANES)
                if n >= 2:
                    pe.wait_ge(s["s1_max"], n - 1)
                for j in range(LANES):
                    last = mm(ps[:, n % 2, j * S:(j + 1) * S], qbd[h][:, g, j, cols_of(b)], kst[h][:, g, cols_of(b)])
                last.then_inc(s["s1_ps"], 1)

            def smax(b):
                pe.wait_ge(s["msp_ok"], b + 1)
                pe.wait_ge(s["identb_ok"], 1)
                if b:
                    pe.wait_ge(s["mT_ok"], b)
                if b >= 3:
                    pe.wait_ge(s["ao_ok"], b - 2)
                if b >= HALF + 3:
                    pe.wait_ge(s["lg_sub"], 1)
                mm(ps[0:LANES * PARTS * GROUPS, 4, 0:S], msp[:, b].rearrange("p j q g -> p (j q g)"), identb[:, :]).then_inc(s["mT_ps"], 1)

            def s2(b, g):
                n, h = b * GROUPS + g, b // HALF
                pe.wait_ge(s[f"mrow_in{b}"], 16 * LANES)
                if n >= 2:
                    pe.wait_ge(s["p_ok"], n - 1)
                mm(ps[:, 2 + n % 2, :].rearrange("p (j q) -> p j q", j=LANES), kst[h][:, g, cols_of(b)],
                   qbd[h][:, g, :, cols_of(b)]).then_inc(s["s2_ps"], 1)

            def av(b, g):
                n, h = b * GROUPS + g, b // HALF
                pe.wait_ge(s["p_ok"], n + 1)
                pe.wait_ge(s["v_ok"], h + 1)
                if g == 0 and b:
                    pe.wait_ge(s["un_ok"], b)
                for j in range(LANES):
                    last = mm(ps[ROWS * j:ROWS * (j + 1), 5, 0:S], vpad[h][:, b % HALF, g, j, :],
                              pexp[:, n % 3, j * S:(j + 1) * S], start=g == 0, stop=g == GROUPS - 1)
                last.then_inc(s["av_ps"], 1)

            def norm(b):
                pe.wait_ge(s["un_ok"], b + 1)
                pe.wait_ge(s["selden_ok"], 1)
                pe.wait_ge(s["mT_ok"], min(b + 3, BATCH))
                if b:
                    pe.wait_ge(s["ao_ok"], b)
                mm(ps[:, 4, 0:S], selden[:, :], un[:, b % 2, :]).then_inc(s["den_ps"], 1)

            def oproj(h):
                pe.wait_ge(s["ao_ok"], HALF * (h + 1) + (1 if h == 0 else 0))
                pe.wait_ge(s["ow_in"], 16 * LANES)
                pe.wait_ge(s["mT_ok"], HALF + 3 if h == 0 else BATCH)
                mm(ps[:, 4, :], wo[:, :], aoT[:, h, :]).then_inc(s["o_ps"], 1)

            def router(h):
                pe.wait_ge(s["mla_ok"], h + 1)
                pe.wait_ge(s["w1_in"], 48)
                for n in range(HALF):
                    last = mm(ps[:, 4, n * E0:(n + 1) * E0], mlaT[:, h, n * S:(n + 1) * S], rw[:, :])
                last.then_inc(s["lg_ps"], 1)

            def moe_in(h):
                pe.wait_ge(s["comb_ok"], h + 1)
                pe.wait_ge(s["lg_sub"], NHALF)
                for n in range(HALF):
                    last = mm(ps[0:E0, 4, n * S:(n + 1) * S], comb[:, h * HALF + n, :], ident[:, :])
                last.then_inc(s["cT_ps"], 1)
                pe.wait_ge(s["cT_ok"], h + 1)
                pe.wait_ge(s["w2_in"], 32)
                pe.wait_ge(s["un_ok"], BATCH)
                if h:
                    pe.wait_ge(s["x2_init"], h)
                for n in range(HALF):
                    last = mm(ps[:, 5, n * D:(n + 1) * D], combT[:, h, n * S:(n + 1) * S], b2s[:, :])
                last.then_inc(s["b2_ps"], 1)

            def split3(dst, w_hi, w_lo, x_hi, x_lo):
                mm(dst, w_lo, x_hi, True, False)
                mm(dst, w_hi, x_lo, False, False)
                return mm(dst, w_hi, x_hi, False, True)

            def m1(h, e):
                k = h * E0 + e
                pe.wait_ge(s["w1_split"], 1)
                pe.wait_ge(s["mlalo_ok"], h + 1)
                if k == 0:
                    pe.wait_ge(s["s1_max"], GROUPS * BATCH)
                for c in range(F0):
                    if k:
                        pe.wait_ge(s["gelu_ok"], F0 * (k - 1) + c + 1)
                    f = slice(c * P, (c + 1) * P)
                    split3(ps[:, c, :], w1_hi[:, e, f], w1_lo[:, e, f], mla_hi[:, h, :], mla_lo[:, h, :]).then_inc(s["h1_ps"], 1)

            def m2(h, e):
                k = h * E0 + e
                pe.wait_ge(s["gelu_ok"], F0 * (k + 1))
                if k < 2:
                    pe.wait_ge(s["p_ok"], GROUPS * BATCH)
                else:
                    pe.wait_ge(s["moe_acc"], HALF * (k - 1))
                for n in range(HALF):
                    for c in range(F0):
                        last = mm(ps[:, 2 + k % 2, n * D:(n + 1) * D], hT[:, k % 2, c, n * S:(n + 1) * S],
                                  w2s[:, e * F0 + c, :], c == 0, c == F0 - 1)
                last.then_inc(s["h2_ps"], 1)

            def sim0(h):
                pe.wait_ge(s["w2sq_ok"], 1)
                pe.wait_ge(s["ctxT_ok"], h + 1)
                pe.wait_ge(s["qk_ok"], NHALF)
                if h:
                    pe.wait_ge(s["x3_ok"], h)
                mm(ps[:, 7, 0:HALF * CTX], w2sq[:, :], ctxT[:, halves(h), :].rearrange("p b c -> p (b c)")).then_inc(s["sr_ps"], 1)

            def xT2(h):
                pe.wait_ge(s["v_ok"], NHALF)
                if h:
                    pe.wait_ge(s["x4hi_ok"], h)
                to_T(2, h, 6)

            def sim(h):
                pe.wait_ge(s["xT2_ok"], h + 1)
                pe.wait_ge(s["ctxw_ok"], h + 1)
                pe.wait_ge(s["sr_ok"], h + 1)
                for n in range(HALF):
                    last = mm(ps[:, 7, n * CTX:(n + 1) * CTX], xT[2][:, h, n * S:(n + 1) * S], ctxw[:, h * HALF + n, :])
                last.then_inc(s["sim_ps"], 1)

            def pT1(h):
                pe.wait_ge(s["pn1_ok"], h + 1)
                for n in range(HALF):
                    last = nc.tensor.transpose(ps[0:CTX, 6, n * S:(n + 1) * S], pr[1][:, h * HALF + n, :], ident[:, :])
                last.then_inc(s["pT1_ps"], 1)

            def batt_T(h):
                pe.wait_ge(s["sim_sub"], h + 1)
                pe.wait_ge(s["x2_init"], NHALF)
                if h:
                    pe.wait_ge(s["hb_ok"], h)
                mm(ps[0:HALF, 5, 0:S], mx[1][:, halves(h)], ident[:, :]).then_inc(s["mxT_ps"], 1)
                pe.wait_ge(s["batt_ok"], h + 1)
                mm(ps[:, 5, 0:HALF], batt[:, h, :], ident[0:HALF, 0:HALF]).then_inc(s["bT_ps"], 1)

            def hq(h):
                pe.wait_ge(s["pT1_ok"], h + 1)
                pe.wait_ge(s["sc1_ok"], h + 1)
                for n in range(HALF):
                    last = mm(ps[:, 7, n * S:(n + 1) * S], ctxn[:, h * HALF + n, :], pT[1][:, h, n * S:(n + 1) * S])
                last.then_inc(s["hq_ps"], 1)

            def hb(h):
                pe.wait_ge(s["bT_ok"], h + 1)
                for n in range(HALF):
                    b = h * HALF + n
                    last = mm(ps[:, 5, n:n + 1], xn[2][:, b, :], battc[:, b:b + 1])
                last.then_inc(s["hb_ps"], 1)

            def p4_out(h):
                pe.wait_ge(s["hq_ok"], h + 1)
                pe.wait_ge(s["hh_ok"], h + 1)
                pe.wait_ge(s["w14_ok"], h + 1)
                for n in range(HALF):
                    b, t = h * HALF + n, slice(n * S, (n + 1) * S)
                    dst = ps[:, 7, n * D:(n + 1) * D]
                    mm(dst, hqT[:, h, t], wqv[:, 1, :], True, False)
                    mm(dst, hhT[:, h, t], wqv[:, 2, :], False, False)
                    last = mm(dst, xT[2][:, h, t], w14[:, b, :], False, True)
                last.then_inc(s["qv_ps"], 1)

            def xT3(h):
                pe.wait_ge(s["pT1_ok"], h + 1)
                to_T(3, h, 6)

            def router1(h):
                if h == 0:
                    pe.wait_ge(s["f_in"], 64)
                    nc.tensor.transpose(ps[:, 4, 64:64 + E1], wrn[:, :], ident[0:E1, 0:E1]).then_inc(s["wr_ps"], 1)
                pe.wait_ge(s["wr_ok"], 1)
                pe.wait_ge(s["xT3_ok"], h + 1)
                pe.wait_ge(s["cT_ok"], NHALF)
                if h:
                    pe.wait_ge(s["l7_sub"], h)
                for n in range(HALF):
                    last = mm(ps[:, 4, n * E1:(n + 1) * E1], xT[3][:, h, n * S:(n + 1) * S], wrT[:, :])
                last.then_inc(s["l7_ps"], 1)

            def f1(h):
                pe.wait_ge(s["f1_split"], 1)
                pe.wait_ge(s["x4lo_ok"], h + 1)
                pe.wait_ge(s["gelu_ok"], F0 * E0 * NHALF)
                for c in range(F1):
                    k = F1 * h + c
                    if k >= 2:
                        pe.wait_ge(s["g_ok"], k - 1)
                    f = slice(c * P, (c + 1) * P)
                    split3(ps[:, k % 2, :], f1_hi[:, f], f1_lo[:, f], x4_hi[:, h, :], x4_lo[:, h, :]).then_inc(s["f1_ps"], 1)

            def f2(h):
                pe.wait_ge(s["moe_acc"], HALF * E0 * NHALF)
                pe.wait_ge(s["g_ok"], F1 * (h + 1))
                for n in range(HALF):
                    b = h * HALF + n
                    if b >= 2:
                        pe.wait_ge(s["y_ok"], b - 1)
                    for c in range(F1):
                        last = mm(ps[:, 2 + b % 2, 0:D], gT[:, c, n * S:(n + 1) * S], f2s[:, c, :], c == 0, c == F1 - 1)
                    last.then_inc(s["f2_ps"], 1)

            run({"setup": setup, "p1_ctx": ctx_T, "p1_T": xT0, "p1_scores": scores0, "p1_av": av0, "p1_T2": lambda h: to_T(1, h, 6),
                 "p1_qkv": qkv, "s1": s1, "smax": smax, "s2": s2, "av": av, "norm": norm, "oproj": oproj, "router": router,
                 "moe_in": moe_in, "m1": m1, "m2": m2, "p4_sim0": sim0, "p4_T": xT2, "p4_sim": sim, "p4_pT": pT1,
                 "p4_batt": batt_T, "p4_hq": hq, "p4_hb": hb, "p4_out": p4_out, "p5_T": xT3, "p5_router": router1,
                 "p5_f1": f1, "p5_f2": f2})


_INS = ['x', 'ctx_1024', 'L0_ffn_q_w', 'L0_ffn_q_b', 'L0_ffn_k_w', 'L0_ffn_k_b', 'L0_ffn_v_w', 'L0_ffn_v_b', 'L0_ffn_o_w',
        'L0_ffn_o_b', 'L0_ffn_router_w', 'L0_ffn_router_b', 'L0_ffn_w1', 'L0_ffn_b1', 'L0_ffn_w2', 'L0_ffn_b2',
        'L1_xattn_w_sim', 'L1_xattn_b_sim', 'L1_xattn_W_qv', 'L1_xattn_b_qv', 'L1_ffn_Wr', 'L1_ffn_W1', 'L1_ffn_b1',
        'L1_ffn_W2', 'L1_ffn_b2']
_OUTS = [((BATCH, S, D), 'float32')]


def kernel(**inputs):
    import numpy as _np
    import concourse.bacc as _bacc
    from concourse import mybir as _mybir
    from concourse.bass_utils import run_bass_kernel_spmd as _run

    nc = _bacc.Bacc("TRN2", target_bir_lowering=False, num_devices=1)
    arrays, args = {}, []
    for name in _INS:
        a = _np.ascontiguousarray(inputs[name])
        arrays[f"in_{name}_dram"] = a
        args.append(nc.dram_tensor(f"in_{name}_dram", a.shape, _mybir.dt.from_np(a.dtype), kind="ExternalInput").ap())
    for i, (shape, dtype) in enumerate(_OUTS):
        dt = _mybir.dt.from_np(_np.dtype(dtype))
        args.append(nc.dram_tensor(f"out_{i}_dram", shape, dt, kind="ExternalOutput").ap())
    build(nc, *args)
    r = _run(nc, [arrays], core_ids=[0])
    got = tuple(r.results[0][f"out_{i}_dram"] for i in range(len(_OUTS)))
    return got[0]
```

```python
import concourse.bass as bass
from concourse import mybir
from contextlib import ExitStack

FP32 = mybir.dt.float32
FP32R = mybir.dt.float32r
BF16 = mybir.dt.bfloat16
U32 = mybir.dt.uint32
ALU = mybir.AluOpType
ACT = mybir.ActivationFunctionType
AX = mybir.AxisListType

P = 128
D = 128
S = 128
BATCH = 8
CTX = 77
HALF = 4
NHALF = BATCH // HALF
UNITS = ((0, HALF), (HALF, HALF // 2), (HALF + HALF // 2, HALF // 2))
T = HALF * S
HEADS = 16
KPH = 4
LAT = HEADS * KPH
HD = D // HEADS
E0 = 8
F0 = 2
F1 = 4
E1 = 8
EID = E1 - 1
LN_EPS = 1e-5
TERMS = 6
Q_RUNS = ((0, 0, 3), (1, 3, 2), (2, 5, 1))
K_RUNS = ((0, 0, 3), (0, 3, 2), (0, 5, 1))
GROUPS = 4
LANES = 4
ROWS = 32
USED = TERMS * KPH
PARTS = 3
MROWS = LANES * PARTS * GROUPS


def build(nc, x, ctx_in, q_w, q_b, k_w, k_b, v_w, v_b, o_w, o_b, router_w, router_b, w1, b1, w2, b2,
          w_sim, b_sim, w_qv, b_qv, wr, fw1, fb1, fw2, fb2, out):
    stack = ExitStack()
    with stack:
        def sb(name, shape, dt=FP32):
            return stack.enter_context(nc.sbuf_tensor(name, shape, dt))

        def sem(name):
            return stack.enter_context(nc.semaphore(name))

        x0 = sb("x0", [P, BATCH, D])
        x1 = sb("x1", [P, BATCH, D])
        y = x0
        xn = [sb(f"xn{i}", [P, BATCH, D]) for i in range(3)] + [x1]
        stats = sb("stats", [P, 4, BATCH, 6])
        mv = sb("mv", [P, 4, BATCH, 2])
        veps = sb("veps", [P, 4, BATCH])
        lnv = sb("lnv", [P, 4, BATCH])
        rstd = sb("rstd", [P, 4, BATCH])
        xT = [sb(f"xT{i}", [D, NHALF, T]) for i in range(2)]
        xT += xT
        ctxn = sb("ctxn", [CTX, BATCH, D])
        ctxT = sb("ctxT", [D, BATCH, CTX])
        ctxw = sb("ctxw", [D, BATCH, CTX])
        w2sq = sb("w2sq", [D, P])
        simrow = sb("simrow", [P, BATCH, CTX])
        sc = [sb("sc", [P, BATCH, CTX])] * 2
        pr = [sb("pr", [P, BATCH, CTX])] * 2
        mx = [sb(f"mx{i}", [P, BATCH]) for i in range(2)]
        rs = [sb(f"rs{i}", [P, BATCH]) for i in range(2)]
        rr = [sb(f"rr{i}", [P, BATCH]) for i in range(2)]
        pT = [sb("pT", [CTX, NHALF, T])] * 2
        wqk = sb("wqk", [D, 2 * LAT])
        qw_full = sb("qw_full", [D, D])
        wv = sb("wv", [D, LAT])
        vb = sb("vb", [P, LAT])
        qk = sb("qk", [P, NHALF, T])
        res1 = sb("res1", [P, NHALF, T])
        part = sb("part", [P, NHALF, PARTS, T], BF16)
        qbd = [sb(f"qbd{i}", [P, GROUPS, LANES, T], BF16) for i in range(NHALF)]
        kst = [sb(f"kst{i}", [P, GROUPS, T], BF16) for i in range(NHALF)]
        pexp = sb("pexp", [P, 3, LANES * S])
        un = sb("un", [P, 2, S])
        aoT = sb("aoT", [P, NHALF, T])
        mlaT = sb("mlaT", [D, NHALF, T])
        vpad = [sb(f"vpad{i}", [P, HALF, GROUPS, LANES, ROWS]) for i in range(NHALF)]
        selq, selk = (v[:, :, :].rearrange("p h t -> p (h t)").bitcast(BF16)[:, 0:PARTS * GROUPS * P].rearrange("p (q g c) -> p q g c", q=PARTS, g=GROUPS)
                      for v in (mlaT, aoT))
        qrow = pexp[:, 0, :].bitcast(BF16).rearrange("p (a t) -> p a t", a=2)
        dead = [v[:, :, :, :, :].rearrange("p b g j c -> p (b g j c)") for v in vpad]
        hT = dead[0].rearrange("p (a c t) -> p a c t", a=2, c=F0)
        gT = qbd[0][:, :, :, :].rearrange("p g j t -> p (g j t)").bitcast(FP32).rearrange("p (c t) -> p c t", c=F1)
        x2, x3 = (dead[1][:, n * BATCH * D:(n + 1) * BATCH * D].rearrange("p (b d) -> p b d", d=D) for n in range(2))
        nmax = sb("nmax", [P, BATCH, GROUPS, LANES])
        nres1 = sb("nres1", [P, BATCH, GROUPS, LANES])
        DIAG = MROWS + PARTS * GROUPS
        msp = sb("msp", [P, 2, LANES * DIAG], BF16)
        mT = sb("mT", [MROWS, 2, LANES, S], BF16)
        selg = sb("selg", [MROWS, GROUPS, S], BF16)
        selg_m = sb("selg_m", [MROWS, GROUPS, MROWS // GROUPS])
        selg_c = sb("selg_c", [MROWS, GROUPS])
        rden = sb("rden", [P, 2, S])
        wo = sb("wo", [P, D])
        mla_hi = sb("mla_hi", [D, NHALF, T], FP32R)
        mla_lo = sb("mla_lo", [D, NHALF, T], FP32R)
        rw = sb("rw", [D, E0])
        rb = sb("rb", [P, E0])
        iota = sb("iota", [P, E0])
        lg = sb("lg", [P, BATCH, E0])
        ex = sb("ex", [P, BATCH, E0])
        pb = sb("pb", [P, BATCH, E0])
        lg7 = sb("lg7", [P, BATCH, E1])
        power = sb("power", [P, BATCH])
        eps = sb("eps", [P, 1])
        t1 = sb("t1", [P, BATCH])
        t2 = sb("t2", [P, BATCH])
        t3 = sb("t3", [P, BATCH])
        top = sb("top", [P, BATCH, 8])
        topi = sb("topi", [P, BATCH, 8], U32)
        topf = sb("topf", [P, BATCH, 2])
        eq = sb("eq", [P, 2, BATCH, E0])
        comb = sb("comb", [P, BATCH, E0])
        combT = sb("combT", [E0, NHALF, T])
        w1s = sb("w1s", [D, E0, F0 * P])
        w1_hi = sb("w1_hi", [D, E0, F0 * P], FP32R)
        w1_lo = sb("w1_lo", [D, E0, F0 * P], FP32R)
        w2s = sb("w2s", [P, E0 * F0, D])
        b2s = sb("b2s", [E0, D])
        wqv = sb("wqv", [D, 4, D])
        bqv = sb("bqv", [P, D])
        bsim = sb("bsim", [P, 1])
        flat = lambda v: v[:, :, :].rearrange("p h t -> p (h t)")
        x3T, x4T, x4_hi, x4_lo, prT = (flat(v) for v in (xT[2], xT[3], mla_hi, mla_lo, pT[1]))
        hqT, hhT = flat(qk), flat(res1)
        nbm = sb("nbm", [HALF, len(UNITS)])
        bex = sb("bex", [HALF, len(UNITS), S])
        bsum = sb("bsum", [HALF, len(UNITS)])
        brec = sb("brec", [HALF, len(UNITS)])
        batt = sb("batt", [HALF, len(UNITS), S])
        battc = sb("battc", [P, BATCH])
        hcbar = sb("hcbar", [D, BATCH])
        w14 = xn[1]
        x2b = xn[0]
        wrn = sb("wrn", [E1, D])
        wrT = sb("wrT", [D, E1])
        f1s = sb("f1s", [D, F1 * P])
        f1_hi = sb("f1_hi", [D, F1 * P], FP32R)
        f1_lo = sb("f1_lo", [D, F1 * P], FP32R)
        f2s = sb("f2s", [P, F1, D])
        fb2s = sb("fb2s", [P, D])
        ex7 = sb("ex7", [P, BATCH, E1])
        s7 = sb("s7", [P, BATCH])
        n7 = sb("n7", [P, BATCH])
        p7 = sb("p7", [P, BATCH])
        x3b = xn[2]
        ident = sb("ident", [P, P])
        identb = sb("identb", [P, P], BF16)
        selden = sb("selden", [P, P])
        ones = sb("ones", [P, P])
        NROW = E0 * F0 + F1 + 3 + 1 + 1
        R_FB1, R_SIM, R_OB, R_QK = E0 * F0, E0 * F0 + F1, E0 * F0 + F1 + 3, E0 * F0 + F1 + 4
        rows = sb("rows", [NROW, P])
        cols = sb("cols", [P, NROW])

        ps = stack.enter_context(nc.psum_tensor("ps", [P, 8, 512], FP32))
        scratch_q = nc.dram_tensor("scratch_q", (LAT, TERMS, T), BF16, kind="Internal").ap()
        scratch_k = nc.dram_tensor("scratch_k", (LAT, TERMS, T), BF16, kind="Internal").ap()

        names = """x_in0 x_in1 ctx_in small_in sim_in wr_in qkw_in vw_in ow_in w1_in w2_in qv_in f_in
            ident_ok identb_ok selden_ok zero_q zero_k zero_v ones_v wo_zero ones_ok iota_ok wqk_ok
            cols_ps cols_ok wr_ps wr_ok ctxw_ok w2sq_ok w1_split f1_split
            ln0_var ln1_var ln2_var ln3_var ln0_rstd ln1_rstd ln2_rstd ln3_rstd
            ln0_norm ln1_norm ln2_norm ln3_norm xT0_ps xT1_ps xT2_ps xT3_ps xT0_ok xT1_ok xT2_ok xT3_ok
            ctxT_ps ctxT_ok sc0_ps sc0_sub pr0_ok rr0_ok pT0_ps pT0_ok av0_ps x1_ok
            qk_ps qk_ok v_ps v_ok part_ok parts_out stack_in selqk_ok rows_ps krow_ok qrow_ok qbd_ok
            s1_ps s1_max msp_zero msp_ok selm_ok selc_ok selg_ok mT_ps mT_ok s2_ps p_ok av_ps un_ok den_ps ln_ok rden_ok ao_ok
            o_ps mla_ok mlahi_ok mlalo_ok lg_ps lg_sub ex_ok comb_ok cT_ps cT_ok b2_ps x2_init
            h1_ps gelu_ok h2_ps moe_acc
            sr_ps sr_ok sim_ps sc1_ok sim_sub pr1_ok pn1_ok pT1_ps pT1_ok hq_ps hq_ok hh_ok
            mxT_ps nbm_ok eps_ok power_ok bex_ok batt_ok bT_ps bT_ok hb_ps hb_ok w14_ok x2b_ok qv_ps x3_ok
            x4hi_ok x4lo_ok l7_ps l7_sub ex7_ok p7_ok x3b_ok f1_ps g_ok f2_ps y_ok stored
            dve_step act_step pool_step""".split()
        s = {n: sem(n) for n in names}

        def counter(eng, steps):
            done = [0]

            def did(ins):
                ins.then_inc(steps, 1)
                done[0] += 1
                return done[0]

            def after(n):
                eng.wait_ge(steps, n)

            return did, after

        def halves(h):
            return slice(h * HALF, (h + 1) * HALF)

        def seqs(u):
            return slice(UNITS[u][0], sum(UNITS[u]))

        def toks(u, i=None):
            a, n = UNITS[u]
            return slice(a * S, (a + n) * S) if i is None else slice((a + i) * S, (a + i + 1) * S)

        def through(u, each=1):
            return sum(UNITS[u]) * each

        bank_a, bank_b, bank_c = (6, 0, 3), (7, 1, 4), (5, 2, 5)

        def acc_done(u):
            a, n = UNITS[u]
            return HALF * E0 if a < HALF else HALF * (NHALF * E0 - 1) + a + n - HALF

        def wide(t):
            return lambda n: t.unsqueeze(2).to_broadcast([t.shape[0], t.shape[1], n])

        def h1_bank(k, c):
            return 6 + c if k == 1 else c

        def banks(h):
            return (6, 7) if h == 0 else (4, 5)

        block = stack.enter_context(nc.Block())

        p1 = ["p1_stats", "p1_ctx", "p1_T", "p1_scores", "p1_soft", "p1_av", "p1_ln", "p1_T2", "p1_qkv"]
        skew = 2
        plan = []
        for k in range(len(p1)):
            plan.append((p1[k], (0,)))
            if k >= skew:
                plan.append((p1[k - skew], (1,)))
            if k == skew + 1:
                plan.append(("setup", ()))
        plan += [("rows", (0,)), ("rows", (1,)), ("p1_T2", (1,)), ("rows", (2,)), ("selg", ()), ("rows", (3,))]
        LEAD = 6
        steps = BATCH * GROUPS

        def first_pass(n):
            b, g = n // GROUPS, n % GROUPS
            return [("s1", (b, g))] + ([("msp", (b,))] if g == GROUPS - 1 else [])

        for n in range(LEAD):
            plan += first_pass(n)
            if n == GROUPS - 1:
                plan += [("p1_qkv", (1,)), ("p1_parts", ()), ("p1_v", (0,)), ("mT", (0,))]
        for n in range(steps + 3):
            b, g = n // GROUPS, n % GROUPS
            if n + LEAD < steps:
                plan += first_pass(n + LEAD)
            if n < steps:
                plan.append(("s2", (b, g)))
            if 1 <= n <= steps:
                plan.append(("av", ((n - 1) // GROUPS, (n - 1) % GROUPS)))
            if g == 0 and b:
                plan.append(("un", (b - 1,)))
            if n == steps:
                plan += [("b2", (0,)), ("m1", (0, 0))]
            if g == 2 and b + 1 < BATCH:
                plan.append(("mT", (b + 1,)))
            if g == 2 and b:
                plan += [("den", (b - 1,)), ("norm", (b - 1,))]
            if n == 3:
                plan.append(("p1_v", (1,)))
            if n == HALF * GROUPS + 3:
                plan.append(("oproj", (0,)))
            if n == (HALF + 1) * GROUPS + 3:
                plan.append(("router", (0,)))
            if n == GROUPS + 1:
                plan += [("ctxw", (0,)), ("ctxw", (1,))]
            if n == (HALF + 2) * GROUPS + 3:
                plan += [("combine", (0,)), ("p4_ctx", (0,)), ("p4_ctx", (1,))]
            if n == (HALF + 3) * GROUPS + 3:
                plan.append(("cT", (0,)))
        plan += [("x2_init", (0,)), ("oproj", (1,)), ("m1", (0, 1)), ("router", (1,)), ("combine", (1,)), ("gelu", (0, 0)), ("gelu", (0, 1))]
        for e in range(E0):
            if 1 < e + 1 < E0:
                plan += [("m1", (0, e + 1)), ("gelu", (0, e + 1))]
            plan += [("m2", (0, e)), ("acc", (0, e, 0, HALF))]
        before = [[("p4_ln", (0,))], [("p4_T", (0,))], [], [("p4_probs", (0,))], [("p4_hq", (0,))],
                  [("p4_out", (0,)), ("p4_outd", (0,)), ("p5_ln", (0,))], [("p5_norm", (0,))], [("p5_router", (0,))]]
        after_ = [[("p4_norm", (0,)), ("x2b", (0,))], [("p4_sim", (0,)), ("p4_simd", (0,))], [("p4_mx", (0,)), ("p4_nbm", (0,)), ("p4_exp", (0,))],
                  [("p4_pT", (0,))], [("p4_hh", (0,))], [], [("p5_T", (0,))], []]
        plan += [("cT", (1,)), ("m1", (1, 0)), ("gelu", (1, 0)), ("b2", (1,)), ("x2_init", (1,))]
        for e in range(E0):
            if e + 1 < E0:
                plan += [("m1", (1, e + 1)), ("gelu", (1, e + 1))]
            plan += before[e] + [("m2", (1, e))]
            if e + 1 < E0:
                plan += [("acc", (1, e, 0, HALF))] + after_[e]
        plan += [("acc", (1, E0 - 1, 0, HALF // 2)), ("p4_ln", (1,)), ("acc", (1, E0 - 1, HALF // 2, HALF)), ("p4_ln", (2,)),
                 ("p5_f1", (0, 0)), ("p5_f1", (0, 1)), ("p4_norm", (1,)), ("p4_norm", (2,)), ("x2b", (1,)), ("x2b", (2,)),
                 ("p4_T", (1,)), ("p5_f1", (0, 2)), ("p4_T", (2,)), ("p5_f1", (0, 3)),
                 ("p4_sim", (1,)), ("p4_simd", (1,)), ("p5_f2", (0, 0)), ("p4_sim", (2,)), ("p4_simd", (2,)),
                 ("p4_mx", (1,)), ("p4_nbm", (1,)), ("p4_exp", (1,)), ("p5_f2", (0, 1)), ("p4_mx", (2,)), ("p4_nbm", (2,)), ("p4_exp", (2,)),
                 ("p4_probs", (1,)), ("p4_pT", (1,)), ("p5_f2", (0, 2)), ("p4_probs", (2,)), ("p4_pT", (2,)), ("p4_hq", (1,)),
                 ("p5_f2", (0, 3)), ("p4_hq", (2,)), ("p4_hh", (1,)), ("p4_hh", (2,)), ("p4_out", (1,)), ("p4_outd", (1,)), ("p5_ln", (1,)),
                 ("p4_out", (2,)), ("p4_outd", (2,)), ("p5_ln", (2,)), ("p5_norm", (1,)), ("p5_norm", (2,)),
                 ("p5_exp", (0,)), ("p5_prob", (0,)), ("p5_end", (0,)),
                 ("p5_T", (1,)), ("p5_T", (2,)), ("p5_router", (1,)), ("p5_exp", (1,)), ("p5_router", (2,)), ("p5_exp", (2,))]
        plan += [("p5_f1", (u, c)) for u in (1, 2) for c in range(F1)]
        for u in (1, 2):
            plan += [("p5_prob", (u,))] + [("p5_f2", (u, n)) for n in range(UNITS[u][1])] + [("p5_end", (u,))]

        def run(stages):
            for name, args in plan:
                if name in stages:
                    stages[name](*args)

        @block.sync
        def _(sp):
            xv = x.rearrange("b t d -> t b d")
            sp.dma_start(x0[:, 0:HALF, :], xv[:, 0:HALF, :]).then_inc(s["x_in0"], 16)
            cv = ctx_in.rearrange("b t d -> t b d")
            sp.dma_start(ctxn[:, :, :], cv).then_inc(s["ctx_in"], 16)
            sp.dma_start(x0[:, HALF:BATCH, :], xv[:, HALF:BATCH, :]).then_inc(s["x_in1"], 16)
            sp.dma_start(qw_full[:, :], q_w).then_inc(s["qkw_in"], 16)
            sp.dma_start(wqk[:, LAT:2 * LAT], k_w).then_inc(s["qkw_in"], 16)
            sp.dma_start(wv[:, :], v_w).then_inc(s["vw_in"], 16)
            sp.dma_start(vb[:, :], v_b.partition_broadcast(P)).then_inc(s["vw_in"], 16)
            small = [
                (rows[0:E0 * F0, :], b1.rearrange("e (c p) -> (e c) p", c=F0)),
                (rows[R_FB1:R_FB1 + F1, :], fb1[EID, :].rearrange("(c p) -> c p", c=F1)),
                (rows[R_SIM:R_SIM + 3, :], w_sim.rearrange("(c p) -> c p", c=3)),
                (rows[R_OB:R_OB + 1, :], o_b.rearrange("(a p) -> a p", a=1)),
                (rows[R_QK:R_QK + 1, 0:LAT].rearrange("a (h k) -> a h k", k=KPH),
                 q_b.rearrange("(a h d) -> a h d", a=1, d=HD)[:, :, 0:KPH]),
                (rows[R_QK:R_QK + 1, LAT:2 * LAT], k_b.rearrange("(a p) -> a p", a=1)),
            ]
            for dst, src in small:
                sp.dma_start(dst, src).then_inc(s["small_in"], 16)
            sp.dma_start(bsim[:, :], b_sim.partition_broadcast(P)).then_inc(s["sim_in"], 16)
            sp.dma_start(wrn[:, :], wr).then_inc(s["wr_in"], 16)
            sp.wait_ge(s["wo_zero"], 1)
            ow = o_w[0:LAT, :].rearrange("(g j v) d -> j g v d", g=GROUPS, j=LANES)
            for j in range(LANES):
                sp.dma_start(wo[ROWS * j:ROWS * j + LAT // LANES, :],
                             ow[j]).then_inc(s["ow_in"], 16)
            sp.dma_start(w1s[:, :, :], w1.rearrange("e p f -> p e f")).then_inc(s["w1_in"], 16)
            sp.dma_start(rw[:, :], router_w).then_inc(s["w1_in"], 16)
            sp.dma_start(rb[:, :], router_b.partition_broadcast(P)).then_inc(s["w1_in"], 16)
            sp.dma_start(w2s[:, :, :], w2.rearrange("e (c p) d -> p (e c) d", c=F0)).then_inc(s["w2_in"], 16)
            sp.dma_start(b2s[:, :], b2).then_inc(s["w2_in"], 16)

            def parts():
                sp.wait_ge(s["part_ok"], NHALF)
                for q, r, n in Q_RUNS:
                    sp.dma_start(scratch_q[:, r:r + n, :],
                                 part[0:LAT, 1, q:q + 1, :].to_broadcast([LAT, n, T])).then_inc(s["parts_out"], 16)
                for q, r, n in K_RUNS:
                    sp.dma_start(scratch_k[:, r:r + n, :],
                                 part[LAT:2 * LAT, 1, q:q + n, :]).then_inc(s["parts_out"], 16)
                sp.wait_ge(s["parts_out"], 16 * (len(Q_RUNS) + len(K_RUNS)))
                sp.wait_ge(s["zero_q"], NHALF)
                sp.wait_ge(s["zero_k"], 1)
                for j in range(LANES):
                    rows_ = slice(ROWS * j, ROWS * j + USED)
                    sq = scratch_q.rearrange("(g j k) r n -> j (k r) g n", g=GROUPS, j=LANES)[j]
                    sk = scratch_k.rearrange("(g j k) r n -> j (k r) g n", g=GROUPS, j=LANES)[j]
                    sp.dma_start(qbd[1][rows_, :, j, :], sq).then_inc(s["stack_in"], 16)
                    sp.dma_start(kst[1][rows_, :, :], sk).then_inc(s["stack_in"], 16)
                sp.dma_start(wqv[:, :, :], w_qv.rearrange("(k p) d -> p k d", k=4)).then_inc(s["qv_in"], 16)
                sp.dma_start(bqv[:, :], b_qv.partition_broadcast(P)).then_inc(s["qv_in"], 16)
                sp.dma_start(f1s[:, :], fw1[EID]).then_inc(s["f_in"], 16)
                sp.dma_start(f2s[:, :, :], fw2[EID].rearrange("(c p) d -> p c d", c=F1)).then_inc(s["f_in"], 16)
                sp.dma_start(fb2s[:, :], fb2[EID].partition_broadcast(P)).then_inc(s["f_in"], 16)

            def store(u):
                sp.wait_ge(s["y_ok"], through(u))
                sp.dma_start(out.rearrange("b t d -> t b d")[:, seqs(u), :], y[:, seqs(u), :]).then_inc(s["stored"], 16)

            run({"p1_parts": parts, "p5_end": store})
            sp.wait_ge(s["stored"], 16 * len(UNITS))

        @block.gpsimd
        def _(pool):
            did, after = counter(pool, s["pool_step"])
            a = did(pool.memset(ident[:, :], 0.0))
            after(a)
            pool.affine_select(out=ident[:, :], in_=ident[:, :], compare_op=ALU.not_equal, fill=1.0, base=0,
                               pattern=[[-1, P]], channel_multiplier=1).then_inc(s["ident_ok"], 1)
            pool.memset(eps[:, :], LN_EPS).then_inc(s["eps_ok"], 1)
            pool.memset(wo[:, :], 0.0).then_inc(s["wo_zero"], 1)
            pool.wait_ge(s["qkw_in"], 32)
            pool.tensor_copy(wqk[:, 0:LAT].rearrange("p (h k) -> p h k", k=KPH),
                             qw_full[:, :].rearrange("p (h d) -> p h d", d=HD)[:, :, 0:KPH]).then_inc(s["wqk_ok"], 1)
            def sel_rows(tile, parts_terms, first):
                a = did(pool.memset(tile.rearrange("p q g c -> p (q g c)").bitcast(U32), 0))
                after(a)
                for q, terms in enumerate(parts_terms):
                    heads = tile[:, q, :, :].rearrange("p g (j c) -> p (g j) c", j=LANES)
                    for r in terms:
                        v = heads[:, :, r:USED:TERMS]
                        last = pool.affine_select(out=v, in_=v, compare_op=ALU.not_equal, fill=1.0, base=-first,
                                                  pattern=[[-KPH, HEADS], [-1, KPH]], channel_multiplier=1)
                last.then_inc(s["selqk_ok"], 1)

            def values(h):
                a = did(pool.memset(vpad[h][:, :, :, :, :], 0.0))
                after(a)
                for g in range(GROUPS):
                    last = pool.memset(vpad[h][:, :, g, :, 16 + KPH * g:16 + KPH * (g + 1)], 1.0)
                last.then_inc(s["ones_v"], 1)

            def queries(h):
                pool.memset(qbd[h][:, :, :, :].bitcast(U32), 0).then_inc(s["zero_q"], 1)

            sel_rows(selq, [(0, 1, 2), (3, 4), (5,)], 0)
            sel_rows(selk, [(0, 3, 5), (1, 4), (2,)], LAT)
            queries(0)
            a = did(pool.memset(identb[:, :], 0.0))
            after(a)
            pool.affine_select(out=identb[:, :], in_=identb[:, :], compare_op=ALU.not_equal, fill=1.0, base=0,
                               pattern=[[-1, P]], channel_multiplier=1).then_inc(s["identb_ok"], 1)
            pool.memset(msp[:, :, :], 0.0).then_inc(s["msp_zero"], 1)
            a = did(pool.memset(selg_m[:, :, :], 0.0))
            after(a)
            pool.affine_select(out=selg_m[:, :, :], in_=selg_m[:, :, :], compare_op=ALU.not_equal, fill=1.0, base=0,
                               pattern=[[-1, GROUPS], [-GROUPS, MROWS // GROUPS]], channel_multiplier=1).then_inc(s["selm_ok"], 1)
            values(0)
            queries(1)
            pool.memset(kst[1][:, :, :].bitcast(U32), 0).then_inc(s["zero_k"], 1)
            values(1)
            a = did(pool.memset(selden[:, :], 0.0))
            after(a)
            v = selden[:, :].rearrange("p (j x) -> p j x", j=LANES)
            for lo, base in ((0, -16), (16, -16)):
                last = pool.affine_select(out=v[:, :, lo:lo + 16], in_=v[:, :, lo:lo + 16], compare_op=ALU.not_equal,
                                          fill=1.0, base=base, pattern=[[-ROWS, LANES], [-1, 16]], channel_multiplier=1)
            last.then_inc(s["selden_ok"], 1)
            pool.wait_ge(s["selc_ok"], 1)
            pool.tensor_copy(selg[:, :, :], selg_c[:, :].unsqueeze(2).to_broadcast([MROWS, GROUPS, S])).then_inc(s["selg_ok"], 1)
            for e in range(E0):
                last = pool.memset(iota[:, e:e + 1], float(e))
            last.then_inc(s["iota_ok"], 1)
            pool.memset(power[:, :], -0.5).then_inc(s["power_ok"], 1)
            pool.wait_ge(s["w1_in"], 48)
            a = did(pool.tensor_copy(w1_hi[:, :, :], w1s[:, :, :]))
            after(a)
            pool.tensor_tensor(out=w1_lo[:, :, :], in0=w1s[:, :, :], in1=w1_hi[:, :, :].bitcast(FP32),
                               op=ALU.subtract).then_inc(s["w1_split"], 1)
            pool.wait_ge(s["f_in"], 48)
            a = did(pool.tensor_copy(f1_hi[:, :], f1s[:, :]))
            after(a)
            pool.tensor_tensor(out=f1_lo[:, :], in0=f1s[:, :], in1=f1_hi[:, :].bitcast(FP32),
                               op=ALU.subtract).then_inc(s["f1_split"], 1)

            def x2_bias(u):
                pool.wait_ge(s["moe_acc"], acc_done(u))
                pool.wait_ge(s["qv_in"], 32)
                pool.tensor_tensor(out=x2b[:, seqs(u), :], in0=x2[:, seqs(u), :],
                                   in1=bqv[:, :].unsqueeze(1).to_broadcast([P, UNITS[u][1], D]), op=ALU.add).then_inc(s["x2b_ok"], 1)

            def rstd_of(i, u):
                pool.wait_ge(s[f"ln{i}_var"], u + 1)
                pool.wait_ge(s["power_ok"], 1)
                pool.tensor_tensor(out=rstd[:, i, seqs(u)], in0=veps[:, i, seqs(u)], in1=power[:, seqs(u)],
                                   op=ALU.pow).then_inc(s[f"ln{i}_rstd"], 1)

            run({"p4_ln": lambda u: rstd_of(2, u), "x2b": x2_bias, "p5_ln": lambda u: rstd_of(3, u)})

        @block.scalar
        def _(act):
            did, after = counter(act, s["act_step"])
            act.preload_act_table_set("natural_log_exp_and_others")

            def rstd_of(i, h):
                act.wait_ge(s[f"ln{i}_var"], h + 1)
                act.wait_ge(s["eps_ok"], 1)
                a = did(act.activation(lnv[:, i, halves(h)], mv[:, i, halves(h), 1], ACT.Ln, bias=eps[:, 0:1]))
                after(a)
                act.activation(rstd[:, i, halves(h)], lnv[:, i, halves(h)], ACT.Exp, scale=-0.5).then_inc(s[f"ln{i}_rstd"], 1)

            def xT_of(i, h, bank):
                act.wait_ge(s[f"xT{i}_ps"], h + 1)
                act.activation(xT[i][:, h, :], ps[:, bank, :], ACT.Copy).then_inc(s[f"xT{i}_ok"], 1)

            def setup():
                act.wait_ge(s["cols_ps"], 1)
                act.activation(cols[:, :], ps[:, 0, 0:NROW], ACT.Copy).then_inc(s["cols_ok"], 1)
                act.wait_ge(s["wr_ps"], 1)
                act.activation(wrT[:, :], ps[:, 0, 64:64 + E1], ACT.Copy).then_inc(s["wr_ok"], 1)

            def ctx_T(h):
                act.wait_ge(s["ctxT_ps"], h + 1)
                act.activation(ctxT[:, halves(h), :], ps[:, banks(h)[1], 0:HALF * CTX].rearrange("p (b c) -> p b c", c=CTX),
                               ACT.Copy).then_inc(s["ctxT_ok"], 1)

            def soft0(h):
                act.wait_ge(s["sc0_sub"], h + 1)
                act.activation(pr[0][:, halves(h), :], sc[0][:, halves(h), :], ACT.Exp).then_inc(s["pr0_ok"], 1)

            def pT0(h):
                act.wait_ge(s["pT0_ps"], h + 1)
                act.activation(pT[0][:, h, :], ps[0:CTX, banks(h)[0], :], ACT.Copy).then_inc(s["pT0_ok"], 1)

            def qk_bias(h):
                act.wait_ge(s["qk_ps"], h + 1)
                if h == 0:
                    act.wait_ge(s["cols_ok"], 1)
                act.activation(qk[:, h, :], ps[:, banks(h)[1], :], ACT.Identity, bias=cols[:, R_QK:R_QK + 1]).then_inc(s["qk_ok"], 1)

            def rows_of(g):
                act.wait_ge(s["rows_ps"], 2 * g + 1)
                act.activation(kst[0][:, g, :], ps[:, g % 2, :], ACT.Copy).then_inc(s["krow_ok"], 1)
                act.wait_ge(s["rows_ps"], 2 * g + 2)
                if g >= 2:
                    act.wait_ge(s["qbd_ok"], g - 1)
                act.activation(qrow[:, g % 2, :], ps[:, 2 + g % 2, :], ACT.Copy).then_inc(s["qrow_ok"], 1)

            def maxT(b):
                act.wait_ge(s["mT_ps"], b + 1)
                if b >= 2:
                    act.wait_ge(s["s2_ps"], GROUPS * (b - 1))
                act.activation(mT[:, b % 2, :, :], ps[0:MROWS, 7, :].rearrange("p (j q) -> p j q", j=LANES), ACT.Copy).then_inc(s["mT_ok"], 1)

            def soft(b, g):
                n = b * GROUPS + g
                act.wait_ge(s["s2_ps"], n + 1)
                if n >= 3:
                    act.wait_ge(s["av_ps"], n - 2)
                act.activation(pexp[:, n % 3, :], ps[:, 2 + n % 2, :], ACT.Exp, scale=KPH ** -0.5).then_inc(s["p_ok"], 1)

            def unnorm(b):
                act.wait_ge(s["av_ps"], GROUPS * (b + 1))
                if b >= 2:
                    act.wait_ge(s["ao_ok"], b - 1)
                act.activation(un[:, b % 2, :], ps[:, 5 + b % 2, 0:S], ACT.Copy).then_inc(s["un_ok"], 1)

            def inverse(b):
                act.wait_ge(s["den_ps"], b + 1)
                if b >= 2:
                    act.wait_ge(s["ao_ok"], b - 1)
                act.activation(rden[:, b % 2, :], ps[:, 4, 0:S], ACT.Ln).then_inc(s["ln_ok"], 1)
                act.wait_ge(s["ln_ok"], b + 1)
                act.activation(rden[:, b % 2, :], rden[:, b % 2, :], ACT.Exp, scale=-1.0).then_inc(s["rden_ok"], 1)

            def oproj(h):
                act.wait_ge(s["o_ps"], h + 1)
                act.activation(mlaT[:, h, :], ps[:, 4, :], ACT.Identity, bias=cols[:, R_OB:R_OB + 1]).then_inc(s["mla_ok"], 1)
                act.wait_ge(s["mla_ok"], h + 1)
                act.activation(mla_hi[:, h, :], mlaT[:, h, :], ACT.Copy).then_inc(s["mlahi_ok"], 1)

            def router(h):
                act.wait_ge(s["lg_sub"], h + 1)
                act.activation(ex[:, halves(h), :], lg[:, halves(h), :], ACT.Exp).then_inc(s["ex_ok"], 1)

            def comb_T(h):
                act.wait_ge(s["cT_ps"], h + 1)
                act.activation(combT[:, h, :], ps[0:E0, (7, 4)[h], :], ACT.Copy).then_inc(s["cT_ok"], 1)

            def gelu0(h, e):
                k = h * E0 + e
                for c in range(F0):
                    act.wait_ge(s["h1_ps"], F0 * k + c + 1)
                    if k >= 2:
                        act.wait_ge(s["h2_ps"], k - 1)
                    act.activation(hT[:, k % 2, c, :], ps[:, h1_bank(k, c), :], ACT.Gelu,
                                   bias=cols[:, e * F0 + c:e * F0 + c + 1]).then_inc(s["gelu_ok"], 1)

            def sim0(h):
                act.wait_ge(s["sr_ps"], h + 1)
                act.wait_ge(s["sim_in"], 16)
                act.activation(simrow[:, halves(h), :], ps[:, h, 0:HALF * CTX].rearrange("p (b c) -> p b c", c=CTX),
                               ACT.Identity, bias=bsim[:, 0:1]).then_inc(s["sr_ok"], 1)

            def x3_T(u):
                act.wait_ge(s["xT2_ps"], u + 1)
                act.activation(x3T[:, toks(u)], ps[:, bank_a[u], 0:UNITS[u][1] * S], ACT.Copy).then_inc(s["xT2_ok"], 1)

            def exps(u):
                act.wait_ge(s["sim_sub"], u + 1)
                act.activation(pr[1][:, seqs(u), :], sc[1][:, seqs(u), :], ACT.Exp).then_inc(s["pr1_ok"], 1)
                n = UNITS[u][1]
                act.wait_ge(s["nbm_ok"], u + 1)
                act.activation(bex[0:n, u, :], ps[0:n, bank_c[u], 0:S], ACT.Exp, bias=nbm[0:n, u:u + 1],
                               accum_out=bsum[0:n, u:u + 1]).then_inc(s["bex_ok"], 1)

            def pT_and_batt(u):
                n = UNITS[u][1]
                act.wait_ge(s["bT_ps"], u + 1)
                act.activation(battc[:, seqs(u)], ps[:, bank_c[u], 0:n], ACT.Copy).then_inc(s["bT_ok"], 1)
                act.wait_ge(s["pT1_ps"], u + 1)
                act.activation(prT[:, toks(u)], ps[0:CTX, bank_a[u], 0:n * S], ACT.Copy).then_inc(s["pT1_ok"], 1)

            def hq(u):
                n = UNITS[u][1]
                act.wait_ge(s["hb_ps"], u + 1)
                act.activation(hcbar[:, seqs(u)], ps[:, bank_c[u], 0:n], ACT.Copy).then_inc(s["hb_ok"], 1)
                act.wait_ge(s["hq_ps"], u + 1)
                act.activation(hqT[:, toks(u)], ps[:, bank_b[u], 0:n * S], ACT.Copy).then_inc(s["hq_ok"], 1)

            def x4_T(u):
                v = ps[:, bank_a[u], 0:UNITS[u][1] * S]
                act.wait_ge(s["xT3_ps"], u + 1)
                act.activation(x4T[:, toks(u)], v, ACT.Copy).then_inc(s["xT3_ok"], 1)
                act.activation(x4_hi[:, toks(u)], v, ACT.Copy).then_inc(s["x4hi_ok"], 1)

            def exp7(u):
                act.wait_ge(s["l7_sub"], u + 1)
                act.activation(ex7[:, seqs(u), :], lg7[:, seqs(u), :], ACT.Exp).then_inc(s["ex7_ok"], 1)

            def gelu1(u, c):
                k = F1 * u + c
                act.wait_ge(s["f1_ps"], k + 1)
                act.activation(gT[:, c, toks(u)], ps[:, (bank_a, bank_b)[c % 2][u], 0:UNITS[u][1] * S], ACT.Gelu,
                               bias=cols[:, R_FB1 + c:R_FB1 + c + 1]).then_inc(s["g_ok"], 1)

            run({"setup": setup, "p1_stats": lambda h: rstd_of(0, h), "p1_ctx": ctx_T, "p1_T": lambda h: xT_of(0, h, banks(h)[0]),
                 "p1_soft": soft0, "p1_av": pT0, "p1_ln": lambda h: rstd_of(1, h), "p1_T2": lambda h: xT_of(1, h, banks(h)[0]),
                 "p1_qkv": qk_bias, "p4_ctx": sim0, "mT": maxT, "s2": soft, "un": unnorm, "den": inverse, "oproj": oproj, "router": router,
                 "cT": comb_T, "gelu": gelu0, "rows": rows_of, "p4_T": x3_T, "p4_exp": exps, "p4_pT": pT_and_batt,
                 "p4_hq": hq, "p5_T": x4_T, "p5_f1": gelu1, "p5_exp": exp7})

        @block.vector
        def _(dve):
            did, after = counter(dve, s["dve_step"])
            dve.memset(ones[:, :], 1.0).then_inc(s["ones_ok"], 1)

            def var_of(i, src, group):
                span = range(group.start, group.stop)
                for b in span:
                    a = did(dve.bn_stats(stats[:, i, b, :], src[:, b, :]))
                after(a)
                if i < 2:
                    for b in span:
                        last = dve.bn_aggr(mv[:, i, b, :], stats[:, i, b, :])
                    last.then_inc(s[f"ln{i}_var"], 1)
                    return
                for b in span:
                    a = did(dve.bn_aggr(mv[:, i, b, :], stats[:, i, b, :]))
                after(a)
                dve.tensor_scalar(veps[:, i, group], mv[:, i, group, 1], LN_EPS, None, ALU.add).then_inc(s[f"ln{i}_var"], 1)

            def norm_of(i, src, group, u):
                dve.wait_ge(s[f"ln{i}_rstd"], u + 1)
                for b in range(group.start, group.stop):
                    dve.tensor_scalar(xn[i][:, b, :], src[:, b, :], mv[:, i, b, 0:1], rstd[:, i, b:b + 1],
                                      ALU.subtract, ALU.mult).then_inc(s[f"ln{i}_norm"], 1)

            def sel_groups():
                dve.wait_ge(s["selm_ok"], 1)
                dve.tensor_reduce(selg_c[:, :], selg_m[:, :, :], axis=AX.X, op=ALU.add).then_inc(s["selc_ok"], 1)

            def stats0(h):
                dve.wait_ge(s[f"x_in{h}"], 16)
                var_of(0, x0, halves(h))
                norm_of(0, x0, halves(h), h)

            def ctx_w(h):
                dve.wait_ge(s["ctxT_ok"], h + 1)
                dve.wait_ge(s["cols_ok"], 1)
                dve.tensor_scalar(ctxw[:, halves(h), :], ctxT[:, halves(h), :], cols[:, R_SIM + 2:R_SIM + 3],
                                  cols[:, R_SIM:R_SIM + 1], ALU.mult, ALU.add).then_inc(s["ctxw_ok"], 1)
                if h == 0:
                    dve.wait_ge(s["ones_ok"], 1)
                    dve.tensor_scalar(w2sq[:, :], ones[:, :], cols[:, R_SIM + 1:R_SIM + 2], None, ALU.mult).then_inc(s["w2sq_ok"], 1)

            def scores0(h):
                dve.wait_ge(s["sc0_ps"], h + 1)
                v = ps[:, banks(h)[1], 0:HALF * CTX].rearrange("p (b c) -> p b c", c=CTX)
                a = did(dve.tensor_reduce(mx[0][:, halves(h)], v, axis=AX.X, op=ALU.max))
                after(a)
                dve.tensor_tensor(out=sc[0][:, halves(h), :], in0=v, in1=wide(mx[0][:, halves(h)])(CTX),
                                  op=ALU.subtract).then_inc(s["sc0_sub"], 1)

            def soft0(h):
                dve.wait_ge(s["pr0_ok"], h + 1)
                a = did(dve.tensor_reduce(rs[0][:, halves(h)], pr[0][:, halves(h), :], axis=AX.X, op=ALU.add))
                after(a)
                dve.reciprocal(rr[0][:, halves(h)], rs[0][:, halves(h)]).then_inc(s["rr0_ok"], 1)

            def av0(h):
                dve.wait_ge(s["av0_ps"], h + 1)
                dve.wait_ge(s["rr0_ok"], h + 1)
                for i in range(HALF):
                    b = h * HALF + i
                    dve.scalar_tensor_tensor(out=x1[:, b, :], in0=ps[:, banks(h)[1], i * D:(i + 1) * D], scalar=rr[0][:, b:b + 1],
                                             in1=x0[:, b, :], op0=ALU.mult, op1=ALU.add).then_inc(s["x1_ok"], 1)

            def ln1(h):
                dve.wait_ge(s["x1_ok"], HALF * (h + 1))
                var_of(1, x1, halves(h))
                norm_of(1, x1, halves(h), h)

            def qkv(h):
                dve.wait_ge(s["qk_ok"], h + 1)
                a = did(dve.tensor_copy(part[:, h, 0, :], qk[:, h, :]))
                after(a)
                a = did(dve.tensor_tensor(out=res1[:, h, :], in0=qk[:, h, :], in1=part[:, h, 0, :], op=ALU.subtract))
                after(a)
                a = did(dve.tensor_copy(part[:, h, 1, :], res1[:, h, :]))
                after(a)
                dve.tensor_tensor(out=part[:, h, 2, :], in0=res1[:, h, :], in1=part[:, h, 1, :],
                                  op=ALU.subtract).then_inc(s["part_ok"], 1)

            def add_v(h):
                dve.wait_ge(s["v_ps"], h + 1)
                dve.wait_ge(s["ones_v"], h + 1)
                dve.wait_ge(s["vw_in"], 32)
                for g in range(GROUPS):
                    w = GROUPS * KPH
                    last = dve.tensor_tensor(
                        out=vpad[h][:, :, g, :, KPH * g:KPH * (g + 1)],
                        in0=ps[:, banks(h)[0], 0:HALF * LAT].rearrange("p (b n) -> p b n", n=LAT)[:, :, w * g:w * (g + 1)].rearrange("p b (j v) -> p b j v", v=KPH),
                        in1=vb[:, w * g:w * (g + 1)].rearrange("p (j v) -> p j v", v=KPH).unsqueeze(1).to_broadcast([P, HALF, LANES, KPH]),
                        op=ALU.add)
                last.then_inc(s["v_ok"], 1)

            def rows_of(g):
                dve.wait_ge(s["qrow_ok"], g + 1)
                dve.wait_ge(s["zero_q"], 1)
                for j in range(LANES):
                    r = slice(ROWS * j, ROWS * (j + 1))
                    last = dve.tensor_copy(qbd[0][r, g, j, :], qrow[r, g % 2, :])
                last.then_inc(s["qbd_ok"], 1)

            def s1(b, g):
                n = b * GROUPS + g
                dve.wait_ge(s["s1_ps"], n + 1)
                dve.tensor_reduce(nmax[:, b, g, :], ps[:, n % 2, :].rearrange("p (j t) -> p j t", t=S), axis=AX.X,
                                  op=ALU.max, negate=True).then_inc(s["s1_max"], 1)

            def maxima(b):
                dve.wait_ge(s["s1_max"], GROUPS * (b + 1))
                dve.wait_ge(s["msp_zero"], 1)
                if b >= 2:
                    dve.wait_ge(s["mT_ps"], b - 1)
                v = nmax[:, b].rearrange("p g j -> p j g")
                r1 = nres1[:, b].rearrange("p g j -> p j g")
                m = msp[:, b % 2, :].rearrange("p (j q g) -> p j q g", j=LANES, g=GROUPS)
                a = did(dve.tensor_copy(m[:, :, 0, :], v))
                after(a)
                a = did(dve.tensor_tensor(out=r1, in0=v, in1=m[:, :, 0, :], op=ALU.subtract))
                after(a)
                a = did(dve.tensor_copy(m[:, :, 1, :], r1))
                after(a)
                dve.tensor_tensor(out=m[:, :, 2, :], in0=r1, in1=m[:, :, 1, :], op=ALU.subtract).then_inc(s["msp_ok"], 1)

            def norm(b):
                h, i = b // HALF, b % HALF
                dve.wait_ge(s["rden_ok"], b + 1)
                dve.tensor_tensor(out=aoT[:, h, i * S:(i + 1) * S], in0=un[:, b % 2, :], in1=rden[:, b % 2, :],
                                  op=ALU.mult).then_inc(s["ao_ok"], 1)

            def oproj(h):
                dve.wait_ge(s["mlahi_ok"], h + 1)
                dve.tensor_tensor(out=mla_lo[:, h, :], in0=mlaT[:, h, :], in1=mla_hi[:, h, :].bitcast(FP32),
                                  op=ALU.subtract).then_inc(s["mlalo_ok"], 1)

            def logits(hs, bank, h, bias, psum_ready, sub_done, neg, lg):
                n = hs.stop - hs.start
                v = ps[:, bank, 0:n * E0].rearrange("p (b e) -> p b e", e=E0)
                dve.wait_ge(psum_ready, h + 1)
                if bias is None:
                    a = did(dve.tensor_copy(pb[:, hs, :], v))
                else:
                    a = did(dve.tensor_tensor(out=pb[:, hs, :], in0=v, in1=bias[:, :].unsqueeze(1).to_broadcast([P, HALF, E0]), op=ALU.add))
                after(a)
                a = did(dve.tensor_reduce(neg[:, hs], pb[:, hs, :], axis=AX.X, op=ALU.max, negate=True))
                after(a)
                dve.tensor_tensor(out=lg[:, hs, :], in0=pb[:, hs, :], in1=wide(neg[:, hs])(E0), op=ALU.add).then_inc(sub_done, 1)

            def router(h):
                hs = halves(h)
                dve.wait_ge(s["w1_in"], 48)
                logits(hs, 4, h, rb, s["lg_ps"], s["lg_sub"], t1, lg)

            def combine(h):
                hs = halves(h)
                dve.wait_ge(s["ex_ok"], h + 1)
                a = did(dve.tensor_reduce(t2[:, hs], ex[:, hs, :], axis=AX.X, op=ALU.add))
                after(a)
                a = did(dve.reciprocal(t3[:, hs], t2[:, hs]))
                after(a)
                a = did(dve.tensor_tensor(out=pb[:, hs, :], in0=ex[:, hs, :], in1=wide(t3[:, hs])(E0), op=ALU.mult))
                after(a)
                for b in range(h * HALF, (h + 1) * HALF):
                    a = did(dve.max(top[:, b, :], pb[:, b, :]))
                after(a)
                for b in range(h * HALF, (h + 1) * HALF):
                    a = did(dve.max_index(topi[:, b, :], top[:, b, :], pb[:, b, :]))
                c = did(dve.tensor_tensor(out=t1[:, hs], in0=top[:, hs, 0], in1=top[:, hs, 1], op=ALU.add))
                after(a)
                a = did(dve.tensor_copy(topf[:, hs, :], topi[:, hs, 0:2]))
                after(c)
                c = did(dve.tensor_scalar(t2[:, hs], t1[:, hs], 1e-8, None, ALU.add))
                after(c)
                c = did(dve.reciprocal(t3[:, hs], t2[:, hs]))
                dve.wait_ge(s["iota_ok"], 1)
                after(a)
                for k in range(2):
                    a = did(dve.tensor_tensor(out=eq[:, k, hs, :], in0=iota[:, :].unsqueeze(1).to_broadcast([P, HALF, E0]),
                                                   in1=wide(topf[:, hs, k])(E0), op=ALU.is_equal))
                after(a)
                for k in range(2):
                    a = did(dve.tensor_tensor(out=eq[:, k, hs, :], in0=eq[:, k, hs, :], in1=wide(top[:, hs, k])(E0), op=ALU.mult))
                after(a)
                a = did(dve.tensor_tensor(out=eq[:, 0, hs, :], in0=eq[:, 0, hs, :], in1=eq[:, 1, hs, :], op=ALU.add))
                after(max(a, c))
                a = did(dve.tensor_tensor(out=eq[:, 1, hs, :], in0=eq[:, 0, hs, :], in1=wide(t3[:, hs])(E0), op=ALU.mult))
                after(a)
                dve.tensor_scalar(comb[:, hs, :], eq[:, 1, hs, :], 0.3, None, ALU.mult).then_inc(s["comb_ok"], 1)

            def x2_start(h):
                hs = halves(h)
                dve.wait_ge(s["av_ps"], GROUPS * BATCH)
                a = did(dve.tensor_tensor(out=x2[:, hs, :], in0=x1[:, hs, :], in1=xn[1][:, hs, :], op=ALU.add))
                after(a)
                dve.wait_ge(s["b2_ps"], h + 1)
                dve.tensor_tensor(out=x2[:, hs, :], in0=ps[:, 5, :].rearrange("p (b d) -> p b d", d=D), in1=x2[:, hs, :],
                                  op=ALU.add).then_inc(s["x2_init"], 1)

            def acc(h, e, first, end):
                k = h * E0 + e
                dve.wait_ge(s["h2_ps"], k + 1)
                if e == 0:
                    dve.wait_ge(s["x2_init"], h + 1)
                for i in range(first, end):
                    b = h * HALF + i
                    if e:
                        dve.wait_ge(s["moe_acc"], HALF * (k - 1) + i + 1)
                    dve.scalar_tensor_tensor(out=x2[:, b, :], in0=ps[:, 2 + k % 2, i * D:(i + 1) * D], scalar=comb[:, b, e:e + 1],
                                             in1=x2[:, b, :], op0=ALU.mult, op1=ALU.add).then_inc(s["moe_acc"], 1)

            def ln2(u):
                dve.wait_ge(s["moe_acc"], acc_done(u))
                var_of(2, x2, seqs(u))

            def sim(u):
                us, n = seqs(u), UNITS[u][1]
                dve.wait_ge(s["sim_ps"], u + 1)
                dve.wait_ge(s["sr_ok"], NHALF)
                dve.tensor_tensor(out=sc[1][:, us, :], in0=ps[:, bank_b[u], 0:n * CTX].rearrange("p (b c) -> p b c", c=CTX),
                                  in1=simrow[:, us, :], op=ALU.add).then_inc(s["sc1_ok"], 1)
                dve.wait_ge(s["sc1_ok"], u + 1)
                a = did(dve.tensor_reduce(mx[1][:, us], sc[1][:, us, :], axis=AX.X, op=ALU.max))
                after(a)
                dve.tensor_tensor(out=sc[1][:, us, :], in0=sc[1][:, us, :], in1=wide(mx[1][:, us])(CTX),
                                  op=ALU.subtract).then_inc(s["sim_sub"], 1)

            def nbmax(u):
                n = UNITS[u][1]
                dve.wait_ge(s["mxT_ps"], u + 1)
                dve.tensor_reduce(nbm[0:n, u:u + 1], ps[0:n, bank_c[u], 0:S], axis=AX.X, op=ALU.max, negate=True).then_inc(s["nbm_ok"], 1)

            def probs1(u):
                us, n = seqs(u), UNITS[u][1]
                dve.wait_ge(s["pr1_ok"], u + 1)
                a = did(dve.tensor_reduce(rs[1][:, us], pr[1][:, us, :], axis=AX.X, op=ALU.add))
                dve.wait_ge(s["bex_ok"], u + 1)
                c = did(dve.reciprocal(brec[0:n, u:u + 1], bsum[0:n, u:u + 1]))
                after(a)
                a = did(dve.reciprocal(rr[1][:, us], rs[1][:, us]))
                after(c)
                dve.tensor_scalar(batt[0:n, u, :], bex[0:n, u, :], brec[0:n, u:u + 1], None, ALU.mult).then_inc(s["batt_ok"], 1)
                after(a)
                dve.tensor_tensor(out=pr[1][:, us, :], in0=pr[1][:, us, :], in1=wide(rr[1][:, us])(CTX),
                                  op=ALU.mult).then_inc(s["pn1_ok"], 1)

            def products(u):
                dve.wait_ge(s["hb_ok"], u + 1)
                dve.wait_ge(s["qv_in"], 32)
                for b in range(seqs(u).start, seqs(u).stop):
                    last = dve.scalar_tensor_tensor(out=w14[:, b, :], in0=wqv[:, 3, :], scalar=hcbar[:, b:b + 1],
                                                    in1=wqv[:, 0, :], op0=ALU.mult, op1=ALU.add)
                last.then_inc(s["w14_ok"], 1)
                dve.wait_ge(s["hq_ok"], u + 1)
                dve.tensor_tensor(out=hhT[:, toks(u)], in0=hqT[:, toks(u)], in1=x3T[:, toks(u)], op=ALU.mult).then_inc(s["hh_ok"], 1)

            def p4_out(u):
                dve.wait_ge(s["qv_ps"], u + 1)
                dve.wait_ge(s["x2b_ok"], u + 1)
                dve.tensor_tensor(out=x3[:, seqs(u), :], in0=ps[:, bank_b[u], 0:UNITS[u][1] * D].rearrange("p (b d) -> p b d", d=D),
                                  in1=x2b[:, seqs(u), :], op=ALU.add).then_inc(s["x3_ok"], 1)

            def ln3(u):
                dve.wait_ge(s["x3_ok"], u + 1)
                var_of(3, x3, seqs(u))

            def router1(u):
                dve.wait_ge(s["xT3_ok"], u + 1)
                dve.wait_ge(s["x4hi_ok"], u + 1)
                dve.tensor_tensor(out=x4_lo[:, toks(u)], in0=x4T[:, toks(u)], in1=x4_hi[:, toks(u)].bitcast(FP32),
                                  op=ALU.subtract).then_inc(s["x4lo_ok"], 1)
                logits(seqs(u), bank_c[u], u, None, s["l7_ps"], s["l7_sub"], n7, lg7)

            def prob7(u):
                us = seqs(u)
                dve.wait_ge(s["ex7_ok"], u + 1)
                a = did(dve.tensor_reduce(s7[:, us], ex7[:, us, :], axis=AX.X, op=ALU.add))
                after(a)
                a = did(dve.reciprocal(n7[:, us], s7[:, us]))
                after(a)
                dve.tensor_tensor(out=p7[:, us], in0=ex7[:, us, EID], in1=n7[:, us], op=ALU.mult).then_inc(s["p7_ok"], 1)
                dve.wait_ge(s["p7_ok"], u + 1)
                dve.wait_ge(s["f_in"], 48)
                for b in range(us.start, us.stop):
                    last = dve.scalar_tensor_tensor(out=x3b[:, b, :], in0=fb2s[:, :], scalar=p7[:, b:b + 1],
                                                    in1=x3[:, b, :], op0=ALU.mult, op1=ALU.add)
                last.then_inc(s["x3b_ok"], 1)

            def last_add(u):
                a, n = UNITS[u]
                dve.wait_ge(s["x3b_ok"], u + 1)
                for i in range(n):
                    b = a + i
                    dve.wait_ge(s["f2_ps"], b + 1 if n <= 2 else a + n)
                    dve.scalar_tensor_tensor(out=y[:, b, :], in0=ps[:, (bank_a, bank_b)[i % 2][u], i // 2 * D:(i // 2 + 1) * D],
                                             scalar=p7[:, b:b + 1], in1=x3b[:, b, :], op0=ALU.mult, op1=ALU.add).then_inc(s["y_ok"], 1)

            run({"p1_stats": stats0, "ctxw": ctx_w, "p1_scores": scores0, "p1_soft": soft0, "p1_av": av0, "p1_ln": ln1,
                 "p1_qkv": qkv, "p1_v": add_v, "selg": sel_groups, "s1": s1, "msp": maxima, "norm": norm, "oproj": oproj, "router": router, "combine": combine, "x2_init": x2_start, "rows": rows_of,
                 "acc": acc, "p4_ln": ln2, "p4_norm": lambda u: norm_of(2, x2, seqs(u), u), "p4_simd": sim, "p4_nbm": nbmax,
                 "p4_probs": probs1, "p4_hh": products, "p4_outd": p4_out, "p5_ln": ln3,
                 "p5_norm": lambda u: norm_of(3, x3, seqs(u), u), "p5_router": router1, "p5_prob": prob7, "p5_end": last_add})

        @block.tensor
        def _(pe):
            def mm(dst, lhsT, rhs, start=True, stop=True):
                return nc.tensor.matmul(dst, lhsT, rhs, start=start, stop=stop)

            def setup():
                pe.wait_ge(s["ident_ok"], 1)
                pe.wait_ge(s["small_in"], 96)
                nc.tensor.transpose(ps[:, 0, 0:NROW], rows[:, :], ident[0:NROW, 0:NROW]).then_inc(s["cols_ps"], 1)
                pe.wait_ge(s["wr_in"], 16)
                pe.wait_ge(s["cols_ok"], 1)
                nc.tensor.transpose(ps[:, 0, 64:64 + E1], wrn[:, :], ident[0:E1, 0:E1]).then_inc(s["wr_ps"], 1)

            def to_T(i, h, bank):
                for n in range(HALF):
                    pe.wait_ge(s[f"ln{i}_norm"], h * HALF + n + 1)
                    last = nc.tensor.transpose(ps[:, bank, n * S:(n + 1) * S], xn[i][:, h * HALF + n, :], ident[:, :])
                last.then_inc(s[f"xT{i}_ps"], 1)

            def ctx_T(h):
                pe.wait_ge(s["ctx_in"], 16)
                pe.wait_ge(s["ident_ok"], 1)
                for n in range(HALF):
                    last = nc.tensor.transpose(ps[:, banks(h)[1], n * CTX:(n + 1) * CTX], ctxn[:, h * HALF + n, :], ident[0:CTX, 0:CTX])
                last.then_inc(s["ctxT_ps"], 1)

            def scores0(h):
                pe.wait_ge(s["xT0_ok"], h + 1)
                pe.wait_ge(s["ctxT_ok"], h + 1)
                for n in range(HALF):
                    last = mm(ps[:, banks(h)[1], n * CTX:(n + 1) * CTX], xT[0][:, h, n * S:(n + 1) * S], ctxT[:, h * HALF + n, :])
                last.then_inc(s["sc0_ps"], 1)

            def av0(h):
                pe.wait_ge(s["pr0_ok"], h + 1)
                for n in range(HALF):
                    last = nc.tensor.transpose(ps[0:CTX, banks(h)[0], n * S:(n + 1) * S], pr[0][:, h * HALF + n, :], ident[:, :])
                last.then_inc(s["pT0_ps"], 1)
                pe.wait_ge(s["sc0_sub"], h + 1)
                pe.wait_ge(s["pT0_ok"], h + 1)
                for n in range(HALF):
                    last = mm(ps[:, banks(h)[1], n * D:(n + 1) * D], pT[0][:, h, n * S:(n + 1) * S], ctxn[:, h * HALF + n, :])
                last.then_inc(s["av0_ps"], 1)

            def qkv(h):
                pe.wait_ge(s["xT1_ok"], h + 1)
                pe.wait_ge(s["wqk_ok"], 1)
                pe.wait_ge(s["x1_ok"], HALF * (h + 1))
                mm(ps[:, banks(h)[1], :], wqk[:, :], xT[1][:, h, :]).then_inc(s["qk_ps"], 1)
                pe.wait_ge(s["vw_in"], 32)
                for n in range(HALF):
                    last = mm(ps[:, banks(h)[0], n * LAT:(n + 1) * LAT], xT[1][:, h, n * S:(n + 1) * S], wv[:, :])
                last.then_inc(s["v_ps"], 1)

            def cols_of(b):
                return slice((b % HALF) * S, (b % HALF + 1) * S)

            def rows_of(g):
                pe.wait_ge(s["part_ok"], 1)
                pe.wait_ge(s["selqk_ok"], 2)
                pe.wait_ge(s["wr_ok"], 1)
                if g >= 2:
                    pe.wait_ge(s["qrow_ok"], g - 1)
                for sel, bank in ((selk, 0), (selq, 2)):
                    for q in range(PARTS):
                        last = mm(ps[:, bank + g % 2, :], sel[:, q, g, :], part[:, 0, q, :], q == 0, q == PARTS - 1)
                    last.then_inc(s["rows_ps"], 1)

            def s1(b, g):
                n, h = b * GROUPS + g, b // HALF
                if h:
                    pe.wait_ge(s["stack_in"], 16 * 2 * LANES)
                else:
                    pe.wait_ge(s["krow_ok"], g + 1)
                    pe.wait_ge(s["qbd_ok"], g + 1)
                if n >= 2:
                    pe.wait_ge(s["s1_max"], n - 1)
                elif n == 0:
                    pe.wait_ge(s["krow_ok"], GROUPS)
                for j in range(LANES):
                    last = mm(ps[:, n % 2, j * S:(j + 1) * S], qbd[h][:, g, j, cols_of(b)], kst[h][:, g, cols_of(b)])
                last.then_inc(s["s1_ps"], 1)

            def maxT(b):
                pe.wait_ge(s["msp_ok"], b + 1)
                pe.wait_ge(s["identb_ok"], 1)
                pe.wait_ge(s["mT_ok"] if b else s["qk_ok"], b or 1)
                for j in range(LANES):
                    last = mm(ps[0:MROWS, 7, j * S:(j + 1) * S], msp[:, b % 2, MROWS * j:MROWS * (j + 1)], identb[:, :])
                last.then_inc(s["mT_ps"], 1)

            def s2(b, g):
                n, h = b * GROUPS + g, b // HALF
                pe.wait_ge(s["mT_ok"], b + 1)
                pe.wait_ge(s["selg_ok"], 1)
                pe.wait_ge(s["p_ok"] if n >= 2 else s["qrow_ok"], n - 1 if n >= 2 else GROUPS)
                dst = ps[:, 2 + n % 2, :].rearrange("p (j q) -> p j q", j=LANES)
                mm(dst, kst[h][:, g, cols_of(b)], qbd[h][:, g, :, cols_of(b)], True, False)
                mm(dst, selg[:, g, :], mT[:, b % 2, :, :], False, True).then_inc(s["s2_ps"], 1)

            def av(b, g):
                n, h = b * GROUPS + g, b // HALF
                pe.wait_ge(s["p_ok"], n + 1)
                pe.wait_ge(s["v_ok"], h + 1)
                if g == 0 and b >= 2:
                    pe.wait_ge(s["un_ok"], b - 1)
                elif g == 0:
                    pe.wait_ge(s["qk_ok"], NHALF)
                for j in range(LANES):
                    last = mm(ps[ROWS * j:ROWS * (j + 1), 5 + b % 2, 0:S], vpad[h][:, b % HALF, g, j, :],
                              pexp[:, n % 3, j * S:(j + 1) * S], start=g == 0, stop=g == GROUPS - 1)
                last.then_inc(s["av_ps"], 1)

            def den(b):
                pe.wait_ge(s["un_ok"], b + 1)
                pe.wait_ge(s["selden_ok"], 1)
                pe.wait_ge(s["ln_ok"] if b else s["v_ok"], b or NHALF)
                if b >= HALF:
                    pe.wait_ge(s["mla_ok"], 1)
                if b >= HALF + 1:
                    pe.wait_ge(s["lg_sub"], 1)
                mm(ps[:, 4, 0:S], selden[:, :], un[:, b % 2, :]).then_inc(s["den_ps"], 1)

            def oproj(h):
                pe.wait_ge(s["ao_ok"], HALF * (h + 1))
                pe.wait_ge(s["ow_in"], 16 * LANES)
                mm(ps[:, 4, :], wo[:, :], aoT[:, h, :]).then_inc(s["o_ps"], 1)

            def router(h):
                pe.wait_ge(s["mla_ok"], h + 1)
                if h == 0:
                    pe.wait_ge(s["ln_ok"], HALF + 1)
                pe.wait_ge(s["w1_in"], 48)
                for n in range(HALF):
                    last = mm(ps[:, 4, n * E0:(n + 1) * E0], mlaT[:, h, n * S:(n + 1) * S], rw[:, :])
                last.then_inc(s["lg_ps"], 1)

            def comb_T(h):
                pe.wait_ge(s["comb_ok"], h + 1)
                if h:
                    pe.wait_ge(s["lg_sub"], NHALF)
                else:
                    pe.wait_ge(s["mT_ok"], BATCH)
                for n in range(HALF):
                    last = mm(ps[0:E0, (7, 4)[h], n * S:(n + 1) * S], comb[:, h * HALF + n, :], ident[:, :])
                last.then_inc(s["cT_ps"], 1)

            def bias2(h):
                pe.wait_ge(s["cT_ok"], h + 1)
                pe.wait_ge(s["w2_in"], 32)
                pe.wait_ge(s["x2_init"] if h else s["un_ok"], h or BATCH - 1)
                for n in range(HALF):
                    last = mm(ps[:, 5, n * D:(n + 1) * D], combT[:, h, n * S:(n + 1) * S], b2s[:, :])
                last.then_inc(s["b2_ps"], 1)

            def split3(dst, w_hi, w_lo, x_hi, x_lo):
                mm(dst, w_lo, x_hi, True, False)
                mm(dst, w_hi, x_lo, False, False)
                return mm(dst, w_hi, x_hi, False, True)

            def m1(h, e):
                k = h * E0 + e
                pe.wait_ge(s["w1_split"], 1)
                pe.wait_ge(s["mlalo_ok"], h + 1)
                if k == 0:
                    pe.wait_ge(s["sr_ok"], NHALF)
                if k == 1:
                    pe.wait_ge(s["un_ok"], BATCH)
                    pe.wait_ge(s["cT_ok"], 1)
                for c in range(F0):
                    if k >= 2:
                        pe.wait_ge(s["gelu_ok"], F0 * (k - 1 - (k == 2)) + c + 1)
                    f = slice(c * P, (c + 1) * P)
                    split3(ps[:, h1_bank(k, c), :], w1_hi[:, e, f], w1_lo[:, e, f], mla_hi[:, h, :], mla_lo[:, h, :]).then_inc(s["h1_ps"], 1)

            def m2(h, e):
                k = h * E0 + e
                pe.wait_ge(s["gelu_ok"], F0 * (k + 1))
                if k < 2:
                    pe.wait_ge(s["p_ok"], GROUPS * BATCH)
                else:
                    pe.wait_ge(s["moe_acc"], HALF * (k - 1))
                for n in range(HALF):
                    for c in range(F0):
                        last = mm(ps[:, 2 + k % 2, n * D:(n + 1) * D], hT[:, k % 2, c, n * S:(n + 1) * S],
                                  w2s[:, e * F0 + c, :], c == 0, c == F0 - 1)
                last.then_inc(s["h2_ps"], 1)

            def sim0(h):
                pe.wait_ge(s["w2sq_ok"], 1)
                pe.wait_ge(s["ctxT_ok"], h + 1)
                pe.wait_ge(s["s1_max"], GROUPS * BATCH)
                mm(ps[:, h, 0:HALF * CTX], w2sq[:, :], ctxT[:, halves(h), :].rearrange("p b c -> p (b c)")).then_inc(s["sr_ps"], 1)

            def unit_T(i, u):
                a, n = UNITS[u]
                for m in range(n):
                    pe.wait_ge(s[f"ln{i}_norm"], a + m + 1)
                    last = nc.tensor.transpose(ps[:, bank_a[u], m * S:(m + 1) * S], xn[i][:, a + m, :], ident[:, :])
                last.then_inc(s[f"xT{i}_ps"], 1)

            def xT2(u):
                pe.wait_ge(*((s["gelu_ok"], 2 * F0), (s["gelu_ok"], F0 * E0 * NHALF), (s["moe_acc"], HALF * E0 * NHALF))[u])
                unit_T(2, u)

            def sim(u):
                a, n = UNITS[u]
                pe.wait_ge(*((s["gelu_ok"], 2 * F0), (s["gelu_ok"], F0 * E0 * NHALF), (s["cT_ok"], NHALF))[u])
                pe.wait_ge(s["xT2_ok"], u + 1)
                pe.wait_ge(s["ctxw_ok"], NHALF)
                for m in range(n):
                    last = mm(ps[:, bank_b[u], m * CTX:(m + 1) * CTX], x3T[:, toks(u, m)], ctxw[:, a + m, :])
                last.then_inc(s["sim_ps"], 1)

            def max_T(u):
                pe.wait_ge(s["sim_sub"], u + 1)
                pe.wait_ge(*((s["x2_init"], NHALF), (s["moe_acc"], HALF * (E0 * NHALF - 1)), (s["l7_sub"], 1))[u])
                mm(ps[0:UNITS[u][1], bank_c[u], 0:S], mx[1][:, seqs(u)], ident[:, :]).then_inc(s["mxT_ps"], 1)

            def pT1(u):
                a, n = UNITS[u]
                pe.wait_ge(s["batt_ok"], u + 1)
                mm(ps[:, bank_c[u], 0:n], batt[0:n, u, :], ident[0:n, 0:n]).then_inc(s["bT_ps"], 1)
                pe.wait_ge(s["pn1_ok"], u + 1)
                for m in range(n):
                    last = nc.tensor.transpose(ps[0:CTX, bank_a[u], m * S:(m + 1) * S], pr[1][:, a + m, :], ident[:, :])
                last.then_inc(s["pT1_ps"], 1)

            def hq(u):
                a, n = UNITS[u]
                pe.wait_ge(s["bT_ok"], u + 1)
                for m in range(n):
                    last = mm(ps[:, bank_c[u], m:m + 1], xn[2][:, a + m, :], battc[:, a + m:a + m + 1])
                last.then_inc(s["hb_ps"], 1)
                pe.wait_ge(s["pT1_ok"], u + 1)
                pe.wait_ge(s["sc1_ok"], u + 1)
                for m in range(n):
                    last = mm(ps[:, bank_b[u], m * S:(m + 1) * S], ctxn[:, a + m, :], prT[:, toks(u, m)])
                last.then_inc(s["hq_ps"], 1)

            def p4_out(u):
                a, n = UNITS[u]
                pe.wait_ge(s["hq_ok"], u + 1)
                pe.wait_ge(s["hh_ok"], u + 1)
                pe.wait_ge(s["w14_ok"], u + 1)
                for m in range(n):
                    dst = ps[:, bank_b[u], m * D:(m + 1) * D]
                    mm(dst, hqT[:, toks(u, m)], wqv[:, 1, :], True, False)
                    mm(dst, hhT[:, toks(u, m)], wqv[:, 2, :], False, False)
                    last = mm(dst, x3T[:, toks(u, m)], w14[:, a + m, :], False, True)
                last.then_inc(s["qv_ps"], 1)

            def xT3(u):
                pe.wait_ge(s["pT1_ok"], u + 1)
                unit_T(3, u)

            def router1(u):
                pe.wait_ge(s["wr_ok"], 1)
                pe.wait_ge(s["xT3_ok"], u + 1)
                pe.wait_ge(s["hb_ok"], u + 1)
                for m in range(UNITS[u][1]):
                    last = mm(ps[:, bank_c[u], m * E1:(m + 1) * E1], x4T[:, toks(u, m)], wrT[:, :])
                last.then_inc(s["l7_ps"], 1)

            def f1(u, c):
                pe.wait_ge(s["f1_split"], 1)
                pe.wait_ge(s["x4lo_ok"], u + 1)
                k = F1 * u + c
                if c >= 2:
                    pe.wait_ge(s["g_ok"], k - 1)
                else:
                    pe.wait_ge(s["x3_ok"] if c else s["x4hi_ok"], u + 1)
                f = slice(c * P, (c + 1) * P)
                split3(ps[:, (bank_a, bank_b)[c % 2][u], 0:UNITS[u][1] * S], f1_hi[:, f], f1_lo[:, f],
                       x4_hi[:, toks(u)], x4_lo[:, toks(u)]).then_inc(s["f1_ps"], 1)

            def f2(u, i):
                pe.wait_ge(s["g_ok"], F1 * (u + 1))
                for c in range(F1):
                    last = mm(ps[:, (bank_a, bank_b)[i % 2][u], i // 2 * D:(i // 2 + 1) * D], gT[:, c, toks(u, i)], f2s[:, c, :],
                              c == 0, c == F1 - 1)
                last.then_inc(s["f2_ps"], 1)

            run({"setup": setup, "p1_ctx": ctx_T, "p1_T": lambda h: to_T(0, h, banks(h)[0]), "p1_scores": scores0, "p1_av": av0,
                 "p1_T2": lambda h: to_T(1, h, banks(h)[0]), "p1_qkv": qkv, "s1": s1, "mT": maxT, "s2": s2, "av": av,
                 "den": den, "oproj": oproj, "router": router, "cT": comb_T, "b2": bias2, "m1": m1, "rows": rows_of, "m2": m2, "p4_ctx": sim0,
                 "p4_T": xT2, "p4_sim": sim, "p4_mx": max_T, "p4_pT": pT1,
                 "p4_hq": hq, "p4_out": p4_out, "p5_T": xT3, "p5_router": router1, "p5_f1": f1, "p5_f2": f2})


_INS = ['x', 'ctx_1024', 'L0_ffn_q_w', 'L0_ffn_q_b', 'L0_ffn_k_w', 'L0_ffn_k_b', 'L0_ffn_v_w', 'L0_ffn_v_b', 'L0_ffn_o_w',
        'L0_ffn_o_b', 'L0_ffn_router_w', 'L0_ffn_router_b', 'L0_ffn_w1', 'L0_ffn_b1', 'L0_ffn_w2', 'L0_ffn_b2',
        'L1_xattn_w_sim', 'L1_xattn_b_sim', 'L1_xattn_W_qv', 'L1_xattn_b_qv', 'L1_ffn_Wr', 'L1_ffn_W1', 'L1_ffn_b1',
        'L1_ffn_W2', 'L1_ffn_b2']
_OUTS = [((BATCH, S, D), 'float32')]


def kernel(**inputs):
    import numpy as _np
    import concourse.bacc as _bacc
    from concourse import mybir as _mybir
    from concourse.bass_utils import run_bass_kernel_spmd as _run

    nc = _bacc.Bacc("TRN2", target_bir_lowering=False, num_devices=1)
    arrays, args = {}, []
    for name in _INS:
        a = _np.ascontiguousarray(inputs[name])
        arrays[f"in_{name}_dram"] = a
        args.append(nc.dram_tensor(f"in_{name}_dram", a.shape, _mybir.dt.from_np(a.dtype), kind="ExternalInput").ap())
    for i, (shape, dtype) in enumerate(_OUTS):
        dt = _mybir.dt.from_np(_np.dtype(dtype))
        args.append(nc.dram_tensor(f"out_{i}_dram", shape, dt, kind="ExternalOutput").ap())
    build(nc, *args)
    r = _run(nc, [arrays], core_ids=[0])
    got = tuple(r.results[0][f"out_{i}_dram"] for i in range(len(_OUTS)))
    return got[0]
```

```python
import concourse.bass as bass
from concourse import mybir
from contextlib import ExitStack

FP32 = mybir.dt.float32
FP32R = mybir.dt.float32r
BF16 = mybir.dt.bfloat16
U32 = mybir.dt.uint32
ALU = mybir.AluOpType
ACT = mybir.ActivationFunctionType
AX = mybir.AxisListType

P = 128
D = 128
S = 128
BATCH = 8
CTX = 77
HALF = 4
NHALF = BATCH // HALF
UNITS = ((0, HALF), (HALF, HALF // 2), (HALF + HALF // 2, HALF // 2))
T = HALF * S
HEADS = 16
KPH = 4
LAT = HEADS * KPH
HD = D // HEADS
E0 = 8
F0 = 2
F1 = 4
E1 = 8
EID = E1 - 1
LN_EPS = 1e-5
TERMS = 6
Q_RUNS = ((0, 0, 3), (1, 3, 2), (2, 5, 1))
K_RUNS = ((0, 0, 3), (0, 3, 2), (0, 5, 1))
GROUPS = 4
LANES = 4
ROWS = 32
USED = TERMS * KPH
PARTS = 3
MROWS = LANES * PARTS * GROUPS


def build(nc, x, ctx_in, q_w, q_b, k_w, k_b, v_w, v_b, o_w, o_b, router_w, router_b, w1, b1, w2, b2,
          w_sim, b_sim, w_qv, b_qv, wr, fw1, fb1, fw2, fb2, out):
    stack = ExitStack()
    with stack:
        def sb(name, shape, dt=FP32):
            return stack.enter_context(nc.sbuf_tensor(name, shape, dt))

        def sem(name):
            return stack.enter_context(nc.semaphore(name))

        x0 = sb("x0", [P, BATCH, D])
        x1 = sb("x1", [P, BATCH, D])
        y = x0
        xn = [sb(f"xn{i}", [P, BATCH, D]) for i in range(3)] + [x1]
        stats = sb("stats", [P, 4, BATCH, 6])
        mv = sb("mv", [P, 4, BATCH, 2])
        veps = sb("veps", [P, 4, BATCH])
        lnv = sb("lnv", [P, 4, BATCH])
        rstd = sb("rstd", [P, 4, BATCH])
        xT = [sb(f"xT{i}", [D, NHALF, T]) for i in range(2)]
        xT += xT
        ctxn = sb("ctxn", [CTX, BATCH, D])
        ctxT = sb("ctxT", [D, BATCH, CTX])
        ctxw = sb("ctxw", [D, BATCH, CTX])
        w2sq = sb("w2sq", [D, P])
        simrow = sb("simrow", [P, BATCH, CTX])
        sc = [sb("sc", [P, BATCH, CTX])] * 2
        pr = [sb("pr", [P, BATCH, CTX])] * 2
        mx = [sb(f"mx{i}", [P, BATCH]) for i in range(2)]
        rs = [sb(f"rs{i}", [P, BATCH]) for i in range(2)]
        rr = [sb(f"rr{i}", [P, BATCH]) for i in range(2)]
        pT = [sb("pT", [CTX, NHALF, T])] * 2
        wqk = sb("wqk", [D, 2 * LAT])
        qw_full = sb("qw_full", [D, D])
        wv = sb("wv", [D, LAT])
        vb = sb("vb", [P, LAT])
        qk = sb("qk", [P, NHALF, T])
        res1 = sb("res1", [P, NHALF, T])
        part = sb("part", [P, NHALF, PARTS, T], BF16)
        qbd = [sb(f"qbd{i}", [P, GROUPS, LANES, T], BF16) for i in range(NHALF)]
        kst = [sb(f"kst{i}", [P, GROUPS, T], BF16) for i in range(NHALF)]
        pexp = sb("pexp", [P, 3, LANES * S])
        un = sb("un", [P, 2, S])
        aoT = sb("aoT", [P, NHALF, T])
        mlaT = sb("mlaT", [D, NHALF, T])
        vpad = [sb(f"vpad{i}", [P, HALF, GROUPS, LANES, ROWS]) for i in range(NHALF)]
        selq, selk = (v[:, :, :].rearrange("p h t -> p (h t)").bitcast(BF16)[:, 0:PARTS * GROUPS * P].rearrange("p (q g c) -> p q g c", q=PARTS, g=GROUPS)
                      for v in (mlaT, aoT))
        qrow = pexp[:, 0, :].bitcast(BF16).rearrange("p (a t) -> p a t", a=2)
        dead = [v[:, :, :, :, :].rearrange("p b g j c -> p (b g j c)") for v in vpad]
        hT = dead[0].rearrange("p (a c t) -> p a c t", a=2, c=F0)
        gT = qbd[0][:, :, :, :].rearrange("p g j t -> p (g j t)").bitcast(FP32).rearrange("p (c t) -> p c t", c=F1)
        x2, x3 = (dead[1][:, n * BATCH * D:(n + 1) * BATCH * D].rearrange("p (b d) -> p b d", d=D) for n in range(2))
        nmax = sb("nmax", [P, BATCH, GROUPS, LANES])
        nres1 = sb("nres1", [P, BATCH, GROUPS, LANES])
        DIAG = MROWS + PARTS * GROUPS
        msp = sb("msp", [P, 2, LANES * DIAG], BF16)
        mT = sb("mT", [MROWS, 2, LANES, S], BF16)
        selg = sb("selg", [MROWS, GROUPS, S], BF16)
        selg_m = sb("selg_m", [MROWS, GROUPS, MROWS // GROUPS])
        selg_c = sb("selg_c", [MROWS, GROUPS])
        rden = sb("rden", [P, 2, S])
        wo = sb("wo", [P, D])
        mla_hi = sb("mla_hi", [D, NHALF, T], FP32R)
        mla_lo = sb("mla_lo", [D, NHALF, T], FP32R)
        rw = sb("rw", [D, E0])
        rb = sb("rb", [P, E0])
        iota = sb("iota", [P, E0])
        lg = sb("lg", [P, BATCH, E0])
        ex = sb("ex", [P, BATCH, E0])
        pb = sb("pb", [P, BATCH, E0])
        lg7 = sb("lg7", [P, BATCH, E1])
        power = sb("power", [P, BATCH])
        eps = sb("eps", [P, 1])
        t1 = sb("t1", [P, BATCH])
        t2 = sb("t2", [P, BATCH])
        t3 = sb("t3", [P, BATCH])
        top = sb("top", [P, BATCH, 8])
        topi = sb("topi", [P, BATCH, 8], U32)
        topf = sb("topf", [P, BATCH, 2])
        eq = sb("eq", [P, 2, BATCH, E0])
        comb = sb("comb", [P, BATCH, E0])
        combT = sb("combT", [E0, NHALF, T])
        w1s = sb("w1s", [D, E0, F0 * P])
        w1_hi = sb("w1_hi", [D, E0, F0 * P], FP32R)
        w1_lo = sb("w1_lo", [D, E0, F0 * P], FP32R)
        w2s = sb("w2s", [P, E0 * F0, D])
        b2s = sb("b2s", [E0, D])
        wqv = sb("wqv", [D, 4, D])
        bqv = sb("bqv", [P, D])
        bsim = sb("bsim", [P, 1])
        flat = lambda v: v[:, :, :].rearrange("p h t -> p (h t)")
        x3T, x4T, x4_hi, x4_lo, prT = (flat(v) for v in (xT[2], xT[3], mla_hi, mla_lo, pT[1]))
        hqT, hhT = flat(qk), flat(res1)
        nbm = sb("nbm", [HALF, len(UNITS)])
        bex = sb("bex", [HALF, len(UNITS), S])
        bsum = sb("bsum", [HALF, len(UNITS)])
        brec = sb("brec", [HALF, len(UNITS)])
        batt = sb("batt", [HALF, len(UNITS), S])
        battc = sb("battc", [P, BATCH])
        hcbar = sb("hcbar", [D, BATCH])
        w14 = xn[1]
        x2b = xn[0]
        wrn = sb("wrn", [E1, D])
        wrT = sb("wrT", [D, E1])
        f1s = sb("f1s", [D, F1 * P])
        f1_hi = sb("f1_hi", [D, F1 * P], FP32R)
        f1_lo = sb("f1_lo", [D, F1 * P], FP32R)
        f2s = sb("f2s", [P, F1, D])
        fb2s = sb("fb2s", [P, D])
        ex7 = sb("ex7", [P, BATCH, E1])
        s7 = sb("s7", [P, BATCH])
        n7 = sb("n7", [P, BATCH])
        p7 = sb("p7", [P, BATCH])
        x3b = xn[2]
        ident = sb("ident", [P, P])
        identb = sb("identb", [P, P], BF16)
        selden = sb("selden", [P, P])
        ones = sb("ones", [P, P])
        NROW = E0 * F0 + F1 + 3 + 1 + 1
        R_FB1, R_SIM, R_OB, R_QK = E0 * F0, E0 * F0 + F1, E0 * F0 + F1 + 3, E0 * F0 + F1 + 4
        rows = sb("rows", [NROW, P])
        cols = sb("cols", [P, NROW])

        ps = stack.enter_context(nc.psum_tensor("ps", [P, 8, 512], FP32))
        scratch_q = nc.dram_tensor("scratch_q", (LAT, TERMS, T), BF16, kind="Internal").ap()
        scratch_k = nc.dram_tensor("scratch_k", (LAT, TERMS, T), BF16, kind="Internal").ap()

        names = """x_in0 x_in1 ctx_in small_in sim_in wr_in qkw_in vw_in ow_in w1_in w2_in qv_in f_in
            ident_ok identb_ok selden_ok zero_q zero_k ones_v wo_zero ones_ok iota_ok wqk_ok
            cols_ps cols_ok wr_ps wr_ok ctxw_ok w2sq_ok w1_split f1_split
            ln0_var ln1_var ln2_var ln3_var ln0_rstd ln1_rstd ln2_rstd ln3_rstd
            ln0_norm ln1_norm ln2_norm ln3_norm xT0_ps xT1_ps xT2_ps xT3_ps xT0_ok xT1_ok xT2_ok xT3_ok
            ctxT_ps ctxT_ok sc0_ps sc0_sub pr0_ok rr0_ok pT0_ps pT0_ok av0_ps x1_ok
            qk_ps qk_ok v_ps v_ok part_ok parts_out stack_in selqk_ok rows_ps krow_ok qrow_ok qbd_ok
            s1_ps s1_max msp_zero msp_ok selm_ok selc_ok selg_ok mT_ps mT_ok s2_ps p_ok av_ps un_ok den_ps ln_ok rden_ok ao_ok
            o_ps mla_ok mlahi_ok mlalo_ok lg_ps lg_sub ex_ok comb_ok cT_ps cT_ok b2_ps x2_init
            h1_ps gelu_ok h2_ps moe_acc
            sr_ps sr_ok sim_ps sc1_ok sim_sub pr1_ok pn1_ok pT1_ps pT1_ok hq_ps hq_ok hh_ok
            mxT_ps nbm_ok eps_ok power_ok bex_ok batt_ok bT_ps bT_ok hb_ps hb_ok w14_ok x2b_ok qv_ps x3_ok
            x4hi_ok x4lo_ok l7_ps l7_sub ex7_ok p7_ok x3b_ok f1_ps g_ok f2_ps y_ok stored
            dve_step act_step pool_step""".split()
        s = {n: sem(n) for n in names}

        def counter(eng, steps):
            done = [0]

            def did(ins):
                ins.then_inc(steps, 1)
                done[0] += 1
                return done[0]

            def after(n):
                eng.wait_ge(steps, n)

            return did, after

        def halves(h):
            return slice(h * HALF, (h + 1) * HALF)

        def seqs(u):
            return slice(UNITS[u][0], sum(UNITS[u]))

        def toks(u, i=None):
            a, n = UNITS[u]
            return slice(a * S, (a + n) * S) if i is None else slice((a + i) * S, (a + i + 1) * S)

        def through(u, each=1):
            return sum(UNITS[u]) * each

        bank_a, bank_b = (6, 4, 0), (7, 5, 1)

        def sums(k):
            return sum(UNITS[j // E0][1] for j in range(k))

        def wide(t):
            return lambda n: t.unsqueeze(2).to_broadcast([t.shape[0], t.shape[1], n])

        def h1_bank(k, c):
            if k % 2 == 0 or k >= 2 * E0:
                return c
            return (6 if k < E0 else 4) + c

        def banks(h):
            return (6, 7) if h == 0 else (4, 5)

        block = stack.enter_context(nc.Block())

        def stages_of(text):
            found = [w.partition(":") for w in text.split()]
            return [(name, tuple(int(a) for a in args.split(",")) if args else ()) for name, _, args in found]

        plan = stages_of("""
            p1_stats:0 warm:19 p1_ctx:0 p1_ctx:1 warm:4 p1_T:0 p1_stats:1 p1_scores:0 p1_T:1 p1_soft:0 warm:2
            p1_av:0 p1_ln:0 warm:14 p1_scores:1 p1_T2:0 setup p1_soft:1 p1_qkv:0 p1_av:1 warm:4 p1_ln:1 selg rows:0
            rows:1 rows:2 rows:3 p1_T2:1
        """)
        LEAD = 6
        steps = BATCH * GROUPS
        meanwhile = {
            ('s1', (0, 1)): "p1_v:0",
            ('msp', (0,)): "p1_qkv:1",
            ('s2', (0, 2)): "p1_v:1",
            ('av', (0, 3)): "p1_parts",
            ('s2', (1, 2)): "ctxw:0",
            ('av', (1, 1)): "ctxw:1",
            ('s2', (5, 1)): "oproj:0",
            ('av', (5, 2)): "router:0",
            ('av', (6, 1)): "combine:0",
            ('s2', (7, 0)): "p4_ctx:0",
            ('s2', (7, 2)): "p4_ctx:1",
            ('s2', (7, 3)): "cT:0",
            ('un', (7,)): "m1:0,0,0",
            ('den', (7,)): "m1:0,0,1 b2:0",
        }
        attention = []
        for n in range(-LEAD, steps + 3):
            b, g = n // GROUPS, n % GROUPS
            ahead_b, ahead_g = (n + LEAD) // GROUPS, (n + LEAD) % GROUPS
            if n + LEAD < steps:
                attention.append(("s1", (ahead_b, ahead_g)))
                if ahead_g == GROUPS - 1:
                    attention.append(("msp", (ahead_b,)))
                if ahead_b == 0 and ahead_g == GROUPS - 1:
                    attention.append(("mT", (0,)))
            if 0 <= n < steps:
                attention.append(("s2", (b, g)))
            if 1 <= n <= steps:
                attention.append(("av", ((n - 1) // GROUPS, (n - 1) % GROUPS)))
            if g == 0 and b > 0:
                attention.append(("un", (b - 1,)))
            if g == 2 and 0 <= b < BATCH - 1:
                attention.append(("mT", (b + 1,)))
            if g == 2 and b > 0:
                attention += [("den", (b - 1,)), ("norm", (b - 1,))]
        for stage in attention:
            plan += [stage] + stages_of(meanwhile.get(stage, ""))
        plan += stages_of("""
            m1:0,1,0 gelu:0,0 x2_init:0 acc:0,0 oproj:1 m1:0,1,1 gelu:0,1 m2:0,0 router:1 m1:0,2,0 gelu:0,2
            m1:0,2,1 gelu:0,3 m1:0,3,0 acc:0,1 acc:0,2 m1:0,3,1 m2:0,1 m1:0,4,0 m2:0,2 m1:0,4,1 m2:0,3 gelu:0,4
            combine:1 acc:0,3 m1:0,5,0 m2:0,4 acc:0,4 acc:0,5 m1:0,5,1 m1:0,6,0 x2_init:1 m1:0,6,1 gelu:0,5 cT:1
            m1:0,7,0 m2:0,5 b2:1 m2:0,6 x2b:0 gelu:0,6 m1:0,7,1 acc:0,6 m1:1,0,0 acc:0,7 m1:1,0,1 acc:1,0 gelu:0,7
            gelu:1,0 m1:1,1,0 gelu:1,1 m1:1,1,1 m2:0,7 m2:1,0 gelu:1,2 gelu:1,3 p4_ln:0 acc:1,1 m1:1,2,0 m1:1,2,1
            m1:1,3,0 gelu:1,4 gelu:1,5 m2:1,1 p4_norm:0 m1:1,3,1 m1:1,4,0 m1:1,4,1 m2:1,2 acc:1,2 m1:1,5,0 m2:1,3
            m1:1,5,1 acc:1,3 gelu:1,6 p4_T:0 m2:1,4 acc:1,4 m1:1,6,0 m1:1,6,1 acc:1,5 m1:1,7,0 m2:1,5 m1:1,7,1
            p4_simd:0 m1:2,0,0 m2:1,6 gelu:1,7 p4_sim:0 m1:2,0,1 acc:1,6 m2:1,7 p4_nbm:0 m1:2,1,0 p4_mx:0
            p4_probs:0 gelu:2,0 acc:1,7 m2:2,0 p4_ln:1 p4_exp:0 gelu:2,1 m1:2,1,1 p4_pT:0 m1:2,2,0 m2:2,1 gelu:2,2
            acc:2,0 p4_norm:1 m1:2,2,1 p4_hq:0 gelu:2,3 acc:2,1 p4_hh:0 m1:2,3,0 p4_T:1 gelu:2,4 x2b:1 m1:2,3,1
            m2:2,2 acc:2,2 m1:2,4,0 m1:2,4,1 p4_outd:0 p4_out:0 m1:2,5,0 m2:2,3 m1:2,5,1 acc:2,3 m2:2,4 m1:2,6,0
            gelu:2,5 p5_ln:0 m1:2,6,1 p4_simd:1 gelu:2,6 p4_sim:1 m2:2,5 p4_exp:1 gelu:2,7 m1:2,7,0 p4_mx:1 acc:2,4
            p4_nbm:1 p5_norm:0 p4_probs:1 acc:2,5 acc:2,6 m2:2,6 m1:2,7,1 p5_T:0 p4_pT:1 m2:2,7 acc:2,7 p5_router:0
            p4_ln:2 x2b:2 p4_hh:1 p4_norm:2 p4_hq:1 p5_f1:0,0 p5_f1:0,1 p5_f1:0,2 p4_T:2 p5_exp:0 p4_outd:1
            p4_out:1 p4_sim:2 p4_simd:2 p5_f1:0,3 p5_f2:0,0 p4_exp:2 p5_ln:1 p4_mx:2 p5_f2:0,1 p5_prob:0 p5_T:1
            p5_f2:0,2 p4_pT:2 p5_norm:1 p4_nbm:2 p4_probs:2 p5_router:1 p4_hh:2 p4_hq:2 p5_end:0 p5_exp:1 p5_f2:0,3
            p5_f1:1,0 p4_out:2 p5_f1:1,1 p5_f1:1,2 p5_f1:1,3 p5_T:2 p4_outd:2 p5_ln:2 p5_norm:2 p5_f2:1,0
            p5_router:2 p5_prob:1 p5_f2:1,1 p5_prob:2 p5_exp:2 p5_f1:2,0 p5_end:1 p5_end:2 p5_f1:2,1 p5_f1:2,2
            p5_f1:2,3 p5_f2:2,0 p5_f2:2,1
        """)

        def run(stages):
            for name, args in plan:
                if name in stages:
                    stages[name](*args)

        @block.sync
        def _(sp):
            xv = x.rearrange("b t d -> t b d")
            sp.dma_start(x0[:, 0:HALF, :], xv[:, 0:HALF, :]).then_inc(s["x_in0"], 16)
            cv = ctx_in.rearrange("b t d -> t b d")
            sp.dma_start(ctxn[:, :, :], cv).then_inc(s["ctx_in"], 16)
            sp.dma_start(x0[:, HALF:BATCH, :], xv[:, HALF:BATCH, :]).then_inc(s["x_in1"], 16)
            sp.dma_start(qw_full[:, :], q_w).then_inc(s["qkw_in"], 16)
            sp.dma_start(wqk[:, LAT:2 * LAT], k_w).then_inc(s["qkw_in"], 16)
            sp.dma_start(wv[:, :], v_w).then_inc(s["vw_in"], 16)
            sp.dma_start(vb[:, :], v_b.partition_broadcast(P)).then_inc(s["vw_in"], 16)
            small = [
                (rows[0:E0 * F0, :], b1.rearrange("e (c p) -> (e c) p", c=F0)),
                (rows[R_FB1:R_FB1 + F1, :], fb1[EID, :].rearrange("(c p) -> c p", c=F1)),
                (rows[R_SIM:R_SIM + 3, :], w_sim.rearrange("(c p) -> c p", c=3)),
                (rows[R_OB:R_OB + 1, :], o_b.rearrange("(a p) -> a p", a=1)),
                (rows[R_QK:R_QK + 1, 0:LAT].rearrange("a (h k) -> a h k", k=KPH),
                 q_b.rearrange("(a h d) -> a h d", a=1, d=HD)[:, :, 0:KPH]),
                (rows[R_QK:R_QK + 1, LAT:2 * LAT], k_b.rearrange("(a p) -> a p", a=1)),
            ]
            for dst, src in small:
                sp.dma_start(dst, src).then_inc(s["small_in"], 16)
            sp.dma_start(bsim[:, :], b_sim.partition_broadcast(P)).then_inc(s["sim_in"], 16)
            sp.dma_start(wrn[:, :], wr).then_inc(s["wr_in"], 16)
            sp.wait_ge(s["wo_zero"], 1)
            ow = o_w[0:LAT, :].rearrange("(g j v) d -> j g v d", g=GROUPS, j=LANES)
            for j in range(LANES):
                sp.dma_start(wo[ROWS * j:ROWS * j + LAT // LANES, :],
                             ow[j]).then_inc(s["ow_in"], 16)
            sp.dma_start(w1s[:, :, :], w1.rearrange("e p f -> p e f")).then_inc(s["w1_in"], 16)
            sp.dma_start(rw[:, :], router_w).then_inc(s["w1_in"], 16)
            sp.dma_start(rb[:, :], router_b.partition_broadcast(P)).then_inc(s["w1_in"], 16)
            sp.dma_start(w2s[:, :, :], w2.rearrange("e (c p) d -> p (e c) d", c=F0)).then_inc(s["w2_in"], 16)
            sp.dma_start(b2s[:, :], b2).then_inc(s["w2_in"], 16)

            def parts():
                sp.wait_ge(s["part_ok"], NHALF)
                for q, r, n in Q_RUNS:
                    sp.dma_start(scratch_q[:, r:r + n, :],
                                 part[0:LAT, 1, q:q + 1, :].to_broadcast([LAT, n, T])).then_inc(s["parts_out"], 16)
                for q, r, n in K_RUNS:
                    sp.dma_start(scratch_k[:, r:r + n, :],
                                 part[LAT:2 * LAT, 1, q:q + n, :]).then_inc(s["parts_out"], 16)
                sp.wait_ge(s["parts_out"], 16 * (len(Q_RUNS) + len(K_RUNS)))
                sp.wait_ge(s["zero_q"], NHALF)
                sp.wait_ge(s["zero_k"], 1)
                for j in range(LANES):
                    rows_ = slice(ROWS * j, ROWS * j + USED)
                    sq = scratch_q.rearrange("(g j k) r n -> j (k r) g n", g=GROUPS, j=LANES)[j]
                    sk = scratch_k.rearrange("(g j k) r n -> j (k r) g n", g=GROUPS, j=LANES)[j]
                    sp.dma_start(qbd[1][rows_, :, j, :], sq).then_inc(s["stack_in"], 16)
                    sp.dma_start(kst[1][rows_, :, :], sk).then_inc(s["stack_in"], 16)
                sp.dma_start(wqv[:, :, :], w_qv.rearrange("(k p) d -> p k d", k=4)).then_inc(s["qv_in"], 16)
                sp.dma_start(bqv[:, :], b_qv.partition_broadcast(P)).then_inc(s["qv_in"], 16)
                sp.dma_start(f1s[:, :], fw1[EID]).then_inc(s["f_in"], 16)
                sp.dma_start(f2s[:, :, :], fw2[EID].rearrange("(c p) d -> p c d", c=F1)).then_inc(s["f_in"], 16)
                sp.dma_start(fb2s[:, :], fb2[EID].partition_broadcast(P)).then_inc(s["f_in"], 16)

            def store(u):
                sp.wait_ge(s["y_ok"], through(u))
                sp.dma_start(out.rearrange("b t d -> t b d")[:, seqs(u), :], y[:, seqs(u), :]).then_inc(s["stored"], 16)

            run({"p1_parts": parts, "p5_end": store})
            sp.wait_ge(s["stored"], 16 * len(UNITS))

        @block.gpsimd
        def _(pool):
            did, after = counter(pool, s["pool_step"])
            a = did(pool.memset(ident[:, :], 0.0))
            after(a)
            pool.affine_select(out=ident[:, :], in_=ident[:, :], compare_op=ALU.not_equal, fill=1.0, base=0,
                               pattern=[[-1, P]], channel_multiplier=1).then_inc(s["ident_ok"], 1)
            pool.memset(eps[:, :], LN_EPS).then_inc(s["eps_ok"], 1)
            pool.memset(wo[:, :], 0.0).then_inc(s["wo_zero"], 1)
            pool.wait_ge(s["qkw_in"], 32)
            pool.tensor_copy(wqk[:, 0:LAT].rearrange("p (h k) -> p h k", k=KPH),
                             qw_full[:, :].rearrange("p (h d) -> p h d", d=HD)[:, :, 0:KPH]).then_inc(s["wqk_ok"], 1)
            def sel_rows(tile, parts_terms, first):
                a = did(pool.memset(tile.rearrange("p q g c -> p (q g c)").bitcast(U32), 0))
                after(a)
                for q, terms in enumerate(parts_terms):
                    heads = tile[:, q, :, :].rearrange("p g (j c) -> p (g j) c", j=LANES)
                    for r in terms:
                        v = heads[:, :, r:USED:TERMS]
                        last = pool.affine_select(out=v, in_=v, compare_op=ALU.not_equal, fill=1.0, base=-first,
                                                  pattern=[[-KPH, HEADS], [-1, KPH]], channel_multiplier=1)
                last.then_inc(s["selqk_ok"], 1)

            def values(h):
                a = did(pool.memset(vpad[h][:, :, :, :, :], 0.0))
                after(a)
                for g in range(GROUPS):
                    last = pool.memset(vpad[h][:, :, g, :, 16 + KPH * g:16 + KPH * (g + 1)], 1.0)
                last.then_inc(s["ones_v"], 1)

            def queries(h):
                pool.memset(qbd[h][:, :, :, :].bitcast(U32), 0).then_inc(s["zero_q"], 1)

            sel_rows(selq, [(0, 1, 2), (3, 4), (5,)], 0)
            sel_rows(selk, [(0, 3, 5), (1, 4), (2,)], LAT)
            queries(0)
            a = did(pool.memset(identb[:, :], 0.0))
            after(a)
            pool.affine_select(out=identb[:, :], in_=identb[:, :], compare_op=ALU.not_equal, fill=1.0, base=0,
                               pattern=[[-1, P]], channel_multiplier=1).then_inc(s["identb_ok"], 1)
            pool.memset(msp[:, :, :], 0.0).then_inc(s["msp_zero"], 1)
            a = did(pool.memset(selg_m[:, :, :], 0.0))
            after(a)
            pool.affine_select(out=selg_m[:, :, :], in_=selg_m[:, :, :], compare_op=ALU.not_equal, fill=1.0, base=0,
                               pattern=[[-1, GROUPS], [-GROUPS, MROWS // GROUPS]], channel_multiplier=1).then_inc(s["selm_ok"], 1)
            values(0)
            queries(1)
            pool.memset(kst[1][:, :, :].bitcast(U32), 0).then_inc(s["zero_k"], 1)
            values(1)
            a = did(pool.memset(selden[:, :], 0.0))
            after(a)
            v = selden[:, :].rearrange("p (j x) -> p j x", j=LANES)
            for lo, base in ((0, -16), (16, -16)):
                last = pool.affine_select(out=v[:, :, lo:lo + 16], in_=v[:, :, lo:lo + 16], compare_op=ALU.not_equal,
                                          fill=1.0, base=base, pattern=[[-ROWS, LANES], [-1, 16]], channel_multiplier=1)
            last.then_inc(s["selden_ok"], 1)
            pool.wait_ge(s["selc_ok"], 1)
            pool.tensor_copy(selg[:, :, :], selg_c[:, :].unsqueeze(2).to_broadcast([MROWS, GROUPS, S])).then_inc(s["selg_ok"], 1)
            for e in range(E0):
                last = pool.memset(iota[:, e:e + 1], float(e))
            last.then_inc(s["iota_ok"], 1)
            pool.memset(power[:, :], -0.5).then_inc(s["power_ok"], 1)
            pool.wait_ge(s["w1_in"], 48)
            a = did(pool.tensor_copy(w1_hi[:, :, :], w1s[:, :, :]))
            after(a)
            pool.tensor_tensor(out=w1_lo[:, :, :], in0=w1s[:, :, :], in1=w1_hi[:, :, :].bitcast(FP32),
                               op=ALU.subtract).then_inc(s["w1_split"], 1)
            pool.wait_ge(s["f_in"], 48)
            a = did(pool.tensor_copy(f1_hi[:, :], f1s[:, :]))
            after(a)
            pool.tensor_tensor(out=f1_lo[:, :], in0=f1s[:, :], in1=f1_hi[:, :].bitcast(FP32),
                               op=ALU.subtract).then_inc(s["f1_split"], 1)

            def x2_bias(u):
                pool.wait_ge(s["moe_acc"], sums(E0 * (u + 1)))
                pool.wait_ge(s["qv_in"], 32)
                pool.tensor_tensor(out=x2b[:, seqs(u), :], in0=x2[:, seqs(u), :],
                                   in1=bqv[:, :].unsqueeze(1).to_broadcast([P, UNITS[u][1], D]), op=ALU.add).then_inc(s["x2b_ok"], 1)

            def rstd_of(i, u):
                pool.wait_ge(s[f"ln{i}_var"], u + 1)
                pool.wait_ge(s["power_ok"], 1)
                pool.tensor_tensor(out=rstd[:, i, seqs(u)], in0=veps[:, i, seqs(u)], in1=power[:, seqs(u)],
                                   op=ALU.pow).then_inc(s[f"ln{i}_rstd"], 1)

            run({"p4_ln": lambda u: rstd_of(2, u), "x2b": x2_bias, "p5_ln": lambda u: rstd_of(3, u)})

        @block.scalar
        def _(act):
            did, after = counter(act, s["act_step"])
            act.preload_act_table_set("natural_log_exp_and_others")

            def rstd_of(i, h):
                act.wait_ge(s[f"ln{i}_var"], h + 1)
                act.wait_ge(s["eps_ok"], 1)
                a = did(act.activation(lnv[:, i, halves(h)], mv[:, i, halves(h), 1], ACT.Ln, bias=eps[:, 0:1]))
                after(a)
                act.activation(rstd[:, i, halves(h)], lnv[:, i, halves(h)], ACT.Exp, scale=-0.5).then_inc(s[f"ln{i}_rstd"], 1)

            def xT_of(i, h, bank):
                act.wait_ge(s[f"xT{i}_ps"], h + 1)
                act.activation(xT[i][:, h, :], ps[:, bank, :], ACT.Copy).then_inc(s[f"xT{i}_ok"], 1)

            def setup():
                act.wait_ge(s["cols_ps"], 1)
                act.activation(cols[:, :], ps[:, 0, 0:NROW], ACT.Copy).then_inc(s["cols_ok"], 1)
                act.wait_ge(s["wr_ps"], 1)
                act.activation(wrT[:, :], ps[:, 0, 64:64 + E1], ACT.Copy).then_inc(s["wr_ok"], 1)

            def ctx_T(h):
                act.wait_ge(s["ctxT_ps"], h + 1)
                act.activation(ctxT[:, halves(h), :], ps[:, banks(h)[1], 0:HALF * CTX].rearrange("p (b c) -> p b c", c=CTX),
                               ACT.Copy).then_inc(s["ctxT_ok"], 1)

            def soft0(h):
                act.wait_ge(s["sc0_sub"], h + 1)
                act.activation(pr[0][:, halves(h), :], sc[0][:, halves(h), :], ACT.Exp).then_inc(s["pr0_ok"], 1)

            def pT0(h):
                act.wait_ge(s["pT0_ps"], h + 1)
                act.activation(pT[0][:, h, :], ps[0:CTX, banks(h)[0], :], ACT.Copy).then_inc(s["pT0_ok"], 1)

            def qk_bias(h):
                act.wait_ge(s["qk_ps"], h + 1)
                if h == 0:
                    act.wait_ge(s["cols_ok"], 1)
                act.activation(qk[:, h, :], ps[:, banks(h)[1], :], ACT.Identity, bias=cols[:, R_QK:R_QK + 1]).then_inc(s["qk_ok"], 1)

            def rows_of(g):
                act.wait_ge(s["rows_ps"], 2 * g + 1)
                act.activation(kst[0][:, g, :], ps[:, g % 2, :], ACT.Copy).then_inc(s["krow_ok"], 1)
                act.wait_ge(s["rows_ps"], 2 * g + 2)
                if g >= 2:
                    act.wait_ge(s["qbd_ok"], g - 1)
                act.activation(qrow[:, g % 2, :], ps[:, 2 + g % 2, :], ACT.Copy).then_inc(s["qrow_ok"], 1)

            def maxT(b):
                act.wait_ge(s["mT_ps"], b + 1)
                if b >= 2:
                    act.wait_ge(s["s2_ps"], GROUPS * (b - 1))
                act.activation(mT[:, b % 2, :, :], ps[0:MROWS, 7, :].rearrange("p (j q) -> p j q", j=LANES), ACT.Copy).then_inc(s["mT_ok"], 1)

            def soft(b, g):
                n = b * GROUPS + g
                act.wait_ge(s["s2_ps"], n + 1)
                if n >= 3:
                    act.wait_ge(s["av_ps"], n - 2)
                act.activation(pexp[:, n % 3, :], ps[:, 2 + n % 2, :], ACT.Exp, scale=KPH ** -0.5).then_inc(s["p_ok"], 1)

            def unnorm(b):
                act.wait_ge(s["av_ps"], GROUPS * (b + 1))
                if b >= 2:
                    act.wait_ge(s["ao_ok"], b - 1)
                act.activation(un[:, b % 2, :], ps[:, 5 + b % 2, 0:S], ACT.Copy).then_inc(s["un_ok"], 1)

            def inverse(b):
                act.wait_ge(s["den_ps"], b + 1)
                if b >= 2:
                    act.wait_ge(s["ao_ok"], b - 1)
                act.activation(rden[:, b % 2, :], ps[:, 4, 0:S], ACT.Ln).then_inc(s["ln_ok"], 1)
                act.wait_ge(s["ln_ok"], b + 1)
                act.activation(rden[:, b % 2, :], rden[:, b % 2, :], ACT.Exp, scale=-1.0).then_inc(s["rden_ok"], 1)

            def oproj(h):
                act.wait_ge(s["o_ps"], h + 1)
                act.activation(mlaT[:, h, :], ps[:, 4, :], ACT.Identity, bias=cols[:, R_OB:R_OB + 1]).then_inc(s["mla_ok"], 1)
                act.wait_ge(s["mla_ok"], h + 1)
                act.activation(mla_hi[:, h, :], mlaT[:, h, :], ACT.Copy).then_inc(s["mlahi_ok"], 1)

            def router(h):
                act.wait_ge(s["lg_sub"], h + 1)
                act.activation(ex[:, halves(h), :], lg[:, halves(h), :], ACT.Exp).then_inc(s["ex_ok"], 1)

            def comb_T(h):
                act.wait_ge(s["cT_ps"], h + 1)
                act.activation(combT[:, h, :], ps[0:E0, (7, 4)[h], :], ACT.Copy).then_inc(s["cT_ok"], 1)

            def gelu0(u, e):
                k, n = u * E0 + e, UNITS[u][1] * S
                for c in range(F0):
                    act.wait_ge(s["h1_ps"], F0 * k + c + 1)
                    if k >= 2:
                        act.wait_ge(s["h2_ps"], k - 1)
                    act.activation(hT[:, k % 2, c, 0:n], ps[:, h1_bank(k, c), 0:n], ACT.Gelu,
                                   bias=cols[:, e * F0 + c:e * F0 + c + 1]).then_inc(s["gelu_ok"], 1)

            def sim0(h):
                act.wait_ge(s["sr_ps"], h + 1)
                act.wait_ge(s["sim_in"], 16)
                act.activation(simrow[:, halves(h), :], ps[:, h, 0:HALF * CTX].rearrange("p (b c) -> p b c", c=CTX),
                               ACT.Identity, bias=bsim[:, 0:1]).then_inc(s["sr_ok"], 1)

            def x3_T(u):
                act.wait_ge(s["xT2_ps"], u + 1)
                act.activation(x3T[:, toks(u)], ps[:, bank_a[u], 0:UNITS[u][1] * S], ACT.Copy).then_inc(s["xT2_ok"], 1)

            def exps(u):
                act.wait_ge(s["sim_sub"], u + 1)
                act.activation(pr[1][:, seqs(u), :], sc[1][:, seqs(u), :], ACT.Exp).then_inc(s["pr1_ok"], 1)
                n = UNITS[u][1]
                act.wait_ge(s["nbm_ok"], u + 1)
                act.activation(bex[0:n, u, :], ps[0:n, bank_b[u], 0:S], ACT.Exp, bias=nbm[0:n, u:u + 1],
                               accum_out=bsum[0:n, u:u + 1]).then_inc(s["bex_ok"], 1)

            def pT_and_batt(u):
                n = UNITS[u][1]
                act.wait_ge(s["bT_ps"], u + 1)
                act.activation(battc[:, seqs(u)], ps[:, bank_b[u], 0:n], ACT.Copy).then_inc(s["bT_ok"], 1)
                act.wait_ge(s["pT1_ps"], u + 1)
                act.activation(prT[:, toks(u)], ps[0:CTX, bank_a[u], 0:n * S], ACT.Copy).then_inc(s["pT1_ok"], 1)

            def hq(u):
                n = UNITS[u][1]
                act.wait_ge(s["hb_ps"], u + 1)
                act.activation(hcbar[:, seqs(u)], ps[:, bank_b[u], 0:n], ACT.Copy).then_inc(s["hb_ok"], 1)
                act.wait_ge(s["hq_ps"], u + 1)
                act.activation(hqT[:, toks(u)], ps[:, bank_a[u], 0:n * S], ACT.Copy).then_inc(s["hq_ok"], 1)

            def x4_T(u):
                v = ps[:, bank_a[u], 0:UNITS[u][1] * S]
                act.wait_ge(s["xT3_ps"], u + 1)
                act.activation(x4T[:, toks(u)], v, ACT.Copy).then_inc(s["xT3_ok"], 1)
                act.activation(x4_hi[:, toks(u)], v, ACT.Copy).then_inc(s["x4hi_ok"], 1)

            def exp7(u):
                act.wait_ge(s["l7_sub"], u + 1)
                act.activation(ex7[:, seqs(u), :], lg7[:, seqs(u), :], ACT.Exp).then_inc(s["ex7_ok"], 1)

            def gelu1(u, c):
                k = F1 * u + c
                act.wait_ge(s["f1_ps"], k + 1)
                act.activation(gT[:, c, toks(u)], ps[:, (bank_a, bank_b)[c % 2][u], 0:UNITS[u][1] * S], ACT.Gelu,
                               bias=cols[:, R_FB1 + c:R_FB1 + c + 1]).then_inc(s["g_ok"], 1)

            run({"setup": setup, "p1_stats": lambda h: rstd_of(0, h), "p1_ctx": ctx_T, "p1_T": lambda h: xT_of(0, h, banks(h)[0]),
                 "p1_soft": soft0, "p1_av": pT0, "p1_ln": lambda h: rstd_of(1, h), "p1_T2": lambda h: xT_of(1, h, banks(h)[0]),
                 "p1_qkv": qk_bias, "p4_ctx": sim0, "mT": maxT, "s2": soft, "un": unnorm, "den": inverse, "oproj": oproj, "router": router,
                 "cT": comb_T, "gelu": gelu0, "rows": rows_of, "p4_T": x3_T, "p4_exp": exps, "p4_pT": pT_and_batt,
                 "p4_hq": hq, "p5_T": x4_T, "p5_f1": gelu1, "p5_exp": exp7})

        @block.vector
        def _(dve):
            did, after = counter(dve, s["dve_step"])
            dve.memset(ones[:, :], 1.0).then_inc(s["ones_ok"], 1)

            def var_of(i, src, group):
                span = range(group.start, group.stop)
                for b in span:
                    a = did(dve.bn_stats(stats[:, i, b, :], src[:, b, :]))
                after(a)
                if i < 2:
                    for b in span:
                        last = dve.bn_aggr(mv[:, i, b, :], stats[:, i, b, :])
                    last.then_inc(s[f"ln{i}_var"], 1)
                    return
                for b in span:
                    a = did(dve.bn_aggr(mv[:, i, b, :], stats[:, i, b, :]))
                after(a)
                dve.tensor_scalar(veps[:, i, group], mv[:, i, group, 1], LN_EPS, None, ALU.add).then_inc(s[f"ln{i}_var"], 1)

            def norm_of(i, src, group, u):
                dve.wait_ge(s[f"ln{i}_rstd"], u + 1)
                for b in range(group.start, group.stop):
                    dve.tensor_scalar(xn[i][:, b, :], src[:, b, :], mv[:, i, b, 0:1], rstd[:, i, b:b + 1],
                                      ALU.subtract, ALU.mult).then_inc(s[f"ln{i}_norm"], 1)

            def sel_groups():
                dve.wait_ge(s["selm_ok"], 1)
                dve.tensor_reduce(selg_c[:, :], selg_m[:, :, :], axis=AX.X, op=ALU.add).then_inc(s["selc_ok"], 1)

            def stats0(h):
                dve.wait_ge(s[f"x_in{h}"], 16)
                var_of(0, x0, halves(h))
                norm_of(0, x0, halves(h), h)

            def ctx_w(h):
                dve.wait_ge(s["ctxT_ok"], h + 1)
                dve.wait_ge(s["cols_ok"], 1)
                dve.tensor_scalar(ctxw[:, halves(h), :], ctxT[:, halves(h), :], cols[:, R_SIM + 2:R_SIM + 3],
                                  cols[:, R_SIM:R_SIM + 1], ALU.mult, ALU.add).then_inc(s["ctxw_ok"], 1)
                if h == 0:
                    dve.wait_ge(s["ones_ok"], 1)
                    dve.tensor_scalar(w2sq[:, :], ones[:, :], cols[:, R_SIM + 1:R_SIM + 2], None, ALU.mult).then_inc(s["w2sq_ok"], 1)

            def scores0(h):
                dve.wait_ge(s["sc0_ps"], h + 1)
                v = ps[:, banks(h)[1], 0:HALF * CTX].rearrange("p (b c) -> p b c", c=CTX)
                a = did(dve.tensor_reduce(mx[0][:, halves(h)], v, axis=AX.X, op=ALU.max))
                after(a)
                dve.tensor_tensor(out=sc[0][:, halves(h), :], in0=v, in1=wide(mx[0][:, halves(h)])(CTX),
                                  op=ALU.subtract).then_inc(s["sc0_sub"], 1)

            def soft0(h):
                dve.wait_ge(s["pr0_ok"], h + 1)
                a = did(dve.tensor_reduce(rs[0][:, halves(h)], pr[0][:, halves(h), :], axis=AX.X, op=ALU.add))
                after(a)
                dve.reciprocal(rr[0][:, halves(h)], rs[0][:, halves(h)]).then_inc(s["rr0_ok"], 1)

            def av0(h):
                dve.wait_ge(s["av0_ps"], h + 1)
                dve.wait_ge(s["rr0_ok"], h + 1)
                for i in range(HALF):
                    b = h * HALF + i
                    dve.scalar_tensor_tensor(out=x1[:, b, :], in0=ps[:, banks(h)[1], i * D:(i + 1) * D], scalar=rr[0][:, b:b + 1],
                                             in1=x0[:, b, :], op0=ALU.mult, op1=ALU.add).then_inc(s["x1_ok"], 1)

            def ln1(h):
                dve.wait_ge(s["x1_ok"], HALF * (h + 1))
                var_of(1, x1, halves(h))
                norm_of(1, x1, halves(h), h)

            def qkv(h):
                dve.wait_ge(s["qk_ok"], h + 1)
                a = did(dve.tensor_copy(part[:, h, 0, :], qk[:, h, :]))
                after(a)
                a = did(dve.tensor_tensor(out=res1[:, h, :], in0=qk[:, h, :], in1=part[:, h, 0, :], op=ALU.subtract))
                after(a)
                a = did(dve.tensor_copy(part[:, h, 1, :], res1[:, h, :]))
                after(a)
                dve.tensor_tensor(out=part[:, h, 2, :], in0=res1[:, h, :], in1=part[:, h, 1, :],
                                  op=ALU.subtract).then_inc(s["part_ok"], 1)

            def add_v(h):
                dve.wait_ge(s["v_ps"], h + 1)
                dve.wait_ge(s["ones_v"], h + 1)
                dve.wait_ge(s["vw_in"], 32)
                for g in range(GROUPS):
                    w = GROUPS * KPH
                    last = dve.tensor_tensor(
                        out=vpad[h][:, :, g, :, KPH * g:KPH * (g + 1)],
                        in0=ps[:, banks(h)[0], 0:HALF * LAT].rearrange("p (b n) -> p b n", n=LAT)[:, :, w * g:w * (g + 1)].rearrange("p b (j v) -> p b j v", v=KPH),
                        in1=vb[:, w * g:w * (g + 1)].rearrange("p (j v) -> p j v", v=KPH).unsqueeze(1).to_broadcast([P, HALF, LANES, KPH]),
                        op=ALU.add)
                last.then_inc(s["v_ok"], 1)

            def rows_of(g):
                dve.wait_ge(s["qrow_ok"], g + 1)
                dve.wait_ge(s["zero_q"], 1)
                for j in range(LANES):
                    r = slice(ROWS * j, ROWS * (j + 1))
                    last = dve.tensor_copy(qbd[0][r, g, j, :], qrow[r, g % 2, :])
                last.then_inc(s["qbd_ok"], 1)

            def s1(b, g):
                n = b * GROUPS + g
                dve.wait_ge(s["s1_ps"], n + 1)
                dve.tensor_reduce(nmax[:, b, g, :], ps[:, n % 2, :].rearrange("p (j t) -> p j t", t=S), axis=AX.X,
                                  op=ALU.max, negate=True).then_inc(s["s1_max"], 1)

            def maxima(b):
                dve.wait_ge(s["s1_max"], GROUPS * (b + 1))
                dve.wait_ge(s["msp_zero"], 1)
                if b >= 2:
                    dve.wait_ge(s["mT_ps"], b - 1)
                v = nmax[:, b].rearrange("p g j -> p j g")
                r1 = nres1[:, b].rearrange("p g j -> p j g")
                m = msp[:, b % 2, :].rearrange("p (j q g) -> p j q g", j=LANES, g=GROUPS)
                a = did(dve.tensor_copy(m[:, :, 0, :], v))
                after(a)
                a = did(dve.tensor_tensor(out=r1, in0=v, in1=m[:, :, 0, :], op=ALU.subtract))
                after(a)
                a = did(dve.tensor_copy(m[:, :, 1, :], r1))
                after(a)
                dve.tensor_tensor(out=m[:, :, 2, :], in0=r1, in1=m[:, :, 1, :], op=ALU.subtract).then_inc(s["msp_ok"], 1)

            def norm(b):
                h, i = b // HALF, b % HALF
                dve.wait_ge(s["rden_ok"], b + 1)
                dve.tensor_tensor(out=aoT[:, h, i * S:(i + 1) * S], in0=un[:, b % 2, :], in1=rden[:, b % 2, :],
                                  op=ALU.mult).then_inc(s["ao_ok"], 1)

            def oproj(h):
                dve.wait_ge(s["mlahi_ok"], h + 1)
                dve.tensor_tensor(out=mla_lo[:, h, :], in0=mlaT[:, h, :], in1=mla_hi[:, h, :].bitcast(FP32),
                                  op=ALU.subtract).then_inc(s["mlalo_ok"], 1)

            def logits(hs, bank, h, bias, psum_ready, sub_done, neg, lg):
                n = hs.stop - hs.start
                v = ps[:, bank, 0:n * E0].rearrange("p (b e) -> p b e", e=E0)
                dve.wait_ge(psum_ready, h + 1)
                if bias is None:
                    a = did(dve.tensor_copy(pb[:, hs, :], v))
                else:
                    a = did(dve.tensor_tensor(out=pb[:, hs, :], in0=v, in1=bias[:, :].unsqueeze(1).to_broadcast([P, HALF, E0]), op=ALU.add))
                after(a)
                a = did(dve.tensor_reduce(neg[:, hs], pb[:, hs, :], axis=AX.X, op=ALU.max, negate=True))
                after(a)
                dve.tensor_tensor(out=lg[:, hs, :], in0=pb[:, hs, :], in1=wide(neg[:, hs])(E0), op=ALU.add).then_inc(sub_done, 1)

            def router(h):
                hs = halves(h)
                dve.wait_ge(s["w1_in"], 48)
                logits(hs, 4, h, rb, s["lg_ps"], s["lg_sub"], t1, lg)

            def combine(h):
                hs = halves(h)
                dve.wait_ge(s["ex_ok"], h + 1)
                a = did(dve.tensor_reduce(t2[:, hs], ex[:, hs, :], axis=AX.X, op=ALU.add))
                after(a)
                a = did(dve.reciprocal(t3[:, hs], t2[:, hs]))
                after(a)
                a = did(dve.tensor_tensor(out=pb[:, hs, :], in0=ex[:, hs, :], in1=wide(t3[:, hs])(E0), op=ALU.mult))
                after(a)
                for b in range(h * HALF, (h + 1) * HALF):
                    a = did(dve.max(top[:, b, :], pb[:, b, :]))
                after(a)
                for b in range(h * HALF, (h + 1) * HALF):
                    a = did(dve.max_index(topi[:, b, :], top[:, b, :], pb[:, b, :]))
                c = did(dve.tensor_tensor(out=t1[:, hs], in0=top[:, hs, 0], in1=top[:, hs, 1], op=ALU.add))
                after(a)
                a = did(dve.tensor_copy(topf[:, hs, :], topi[:, hs, 0:2]))
                after(c)
                c = did(dve.tensor_scalar(t2[:, hs], t1[:, hs], 1e-8, None, ALU.add))
                after(c)
                c = did(dve.reciprocal(t3[:, hs], t2[:, hs]))
                dve.wait_ge(s["iota_ok"], 1)
                after(a)
                for k in range(2):
                    a = did(dve.tensor_tensor(out=eq[:, k, hs, :], in0=iota[:, :].unsqueeze(1).to_broadcast([P, HALF, E0]),
                                                   in1=wide(topf[:, hs, k])(E0), op=ALU.is_equal))
                after(a)
                for k in range(2):
                    a = did(dve.tensor_tensor(out=eq[:, k, hs, :], in0=eq[:, k, hs, :], in1=wide(top[:, hs, k])(E0), op=ALU.mult))
                after(a)
                a = did(dve.tensor_tensor(out=eq[:, 0, hs, :], in0=eq[:, 0, hs, :], in1=eq[:, 1, hs, :], op=ALU.add))
                after(max(a, c))
                a = did(dve.tensor_tensor(out=eq[:, 1, hs, :], in0=eq[:, 0, hs, :], in1=wide(t3[:, hs])(E0), op=ALU.mult))
                after(a)
                dve.tensor_scalar(comb[:, hs, :], eq[:, 1, hs, :], 0.3, None, ALU.mult).then_inc(s["comb_ok"], 1)

            def x2_start(h):
                hs = halves(h)
                dve.wait_ge(s["av_ps"], GROUPS * BATCH)
                a = did(dve.tensor_tensor(out=x2[:, hs, :], in0=x1[:, hs, :], in1=xn[1][:, hs, :], op=ALU.add))
                after(a)
                dve.wait_ge(s["b2_ps"], h + 1)
                dve.tensor_tensor(out=x2[:, hs, :], in0=ps[:, 5, :].rearrange("p (b d) -> p b d", d=D), in1=x2[:, hs, :],
                                  op=ALU.add).then_inc(s["x2_init"], 1)

            def acc(u, e):
                a, n = UNITS[u]
                k = u * E0 + e
                dve.wait_ge(s["h2_ps"], k + 1)
                if e == 0:
                    dve.wait_ge(s["x2_init"], min(u, 1) + 1)
                for i in range(n):
                    if e:
                        dve.wait_ge(s["moe_acc"], sums(k - 1) + i + 1)
                    dve.scalar_tensor_tensor(out=x2[:, a + i, :], in0=ps[:, 2 + k % 2, i * D:(i + 1) * D], scalar=comb[:, a + i, e:e + 1],
                                             in1=x2[:, a + i, :], op0=ALU.mult, op1=ALU.add).then_inc(s["moe_acc"], 1)

            def ln2(u):
                dve.wait_ge(s["moe_acc"], sums(E0 * (u + 1)))
                var_of(2, x2, seqs(u))

            def sim(u):
                us, n = seqs(u), UNITS[u][1]
                dve.wait_ge(s["sim_ps"], u + 1)
                dve.wait_ge(s["sr_ok"], NHALF)
                dve.tensor_tensor(out=sc[1][:, us, :], in0=ps[:, bank_b[u], 0:n * CTX].rearrange("p (b c) -> p b c", c=CTX),
                                  in1=simrow[:, us, :], op=ALU.add).then_inc(s["sc1_ok"], 1)
                dve.wait_ge(s["sc1_ok"], u + 1)
                a = did(dve.tensor_reduce(mx[1][:, us], sc[1][:, us, :], axis=AX.X, op=ALU.max))
                after(a)
                dve.tensor_tensor(out=sc[1][:, us, :], in0=sc[1][:, us, :], in1=wide(mx[1][:, us])(CTX),
                                  op=ALU.subtract).then_inc(s["sim_sub"], 1)

            def nbmax(u):
                n = UNITS[u][1]
                dve.wait_ge(s["mxT_ps"], u + 1)
                dve.tensor_reduce(nbm[0:n, u:u + 1], ps[0:n, bank_b[u], 0:S], axis=AX.X, op=ALU.max, negate=True).then_inc(s["nbm_ok"], 1)

            def probs1(u):
                us, n = seqs(u), UNITS[u][1]
                dve.wait_ge(s["pr1_ok"], u + 1)
                a = did(dve.tensor_reduce(rs[1][:, us], pr[1][:, us, :], axis=AX.X, op=ALU.add))
                dve.wait_ge(s["bex_ok"], u + 1)
                c = did(dve.reciprocal(brec[0:n, u:u + 1], bsum[0:n, u:u + 1]))
                after(a)
                a = did(dve.reciprocal(rr[1][:, us], rs[1][:, us]))
                after(c)
                dve.tensor_scalar(batt[0:n, u, :], bex[0:n, u, :], brec[0:n, u:u + 1], None, ALU.mult).then_inc(s["batt_ok"], 1)
                after(a)
                dve.tensor_tensor(out=pr[1][:, us, :], in0=pr[1][:, us, :], in1=wide(rr[1][:, us])(CTX),
                                  op=ALU.mult).then_inc(s["pn1_ok"], 1)

            def products(u):
                dve.wait_ge(s["hb_ok"], u + 1)
                dve.wait_ge(s["qv_in"], 32)
                for b in range(seqs(u).start, seqs(u).stop):
                    last = dve.scalar_tensor_tensor(out=w14[:, b, :], in0=wqv[:, 3, :], scalar=hcbar[:, b:b + 1],
                                                    in1=wqv[:, 0, :], op0=ALU.mult, op1=ALU.add)
                last.then_inc(s["w14_ok"], 1)
                dve.wait_ge(s["hq_ok"], u + 1)
                dve.tensor_tensor(out=hhT[:, toks(u)], in0=hqT[:, toks(u)], in1=x3T[:, toks(u)], op=ALU.mult).then_inc(s["hh_ok"], 1)

            def p4_out(u):
                dve.wait_ge(s["qv_ps"], u + 1)
                dve.wait_ge(s["x2b_ok"], u + 1)
                dve.tensor_tensor(out=x3[:, seqs(u), :], in0=ps[:, bank_b[u], 0:UNITS[u][1] * D].rearrange("p (b d) -> p b d", d=D),
                                  in1=x2b[:, seqs(u), :], op=ALU.add).then_inc(s["x3_ok"], 1)

            def ln3(u):
                dve.wait_ge(s["x3_ok"], u + 1)
                var_of(3, x3, seqs(u))

            def router1(u):
                dve.wait_ge(s["xT3_ok"], u + 1)
                dve.wait_ge(s["x4hi_ok"], u + 1)
                dve.tensor_tensor(out=x4_lo[:, toks(u)], in0=x4T[:, toks(u)], in1=x4_hi[:, toks(u)].bitcast(FP32),
                                  op=ALU.subtract).then_inc(s["x4lo_ok"], 1)
                logits(seqs(u), bank_b[u], u, None, s["l7_ps"], s["l7_sub"], n7, lg7)

            def prob7(u):
                us = seqs(u)
                dve.wait_ge(s["ex7_ok"], u + 1)
                a = did(dve.tensor_reduce(s7[:, us], ex7[:, us, :], axis=AX.X, op=ALU.add))
                after(a)
                a = did(dve.reciprocal(n7[:, us], s7[:, us]))
                after(a)
                dve.tensor_tensor(out=p7[:, us], in0=ex7[:, us, EID], in1=n7[:, us], op=ALU.mult).then_inc(s["p7_ok"], 1)
                dve.wait_ge(s["p7_ok"], u + 1)
                dve.wait_ge(s["f_in"], 48)
                for b in range(us.start, us.stop):
                    last = dve.scalar_tensor_tensor(out=x3b[:, b, :], in0=fb2s[:, :], scalar=p7[:, b:b + 1],
                                                    in1=x3[:, b, :], op0=ALU.mult, op1=ALU.add)
                last.then_inc(s["x3b_ok"], 1)

            def last_add(u):
                a, n = UNITS[u]
                dve.wait_ge(s["x3b_ok"], u + 1)
                for i in range(n):
                    b = a + i
                    dve.wait_ge(s["f2_ps"], b + 1 if n <= 2 else a + n)
                    dve.scalar_tensor_tensor(out=y[:, b, :], in0=ps[:, (bank_a, bank_b)[i % 2][u], i // 2 * D:(i // 2 + 1) * D],
                                             scalar=p7[:, b:b + 1], in1=x3b[:, b, :], op0=ALU.mult, op1=ALU.add).then_inc(s["y_ok"], 1)

            run({"p1_stats": stats0, "ctxw": ctx_w, "p1_scores": scores0, "p1_soft": soft0, "p1_av": av0, "p1_ln": ln1,
                 "p1_qkv": qkv, "p1_v": add_v, "selg": sel_groups, "s1": s1, "msp": maxima, "norm": norm, "oproj": oproj, "router": router, "combine": combine, "x2_init": x2_start, "rows": rows_of,
                 "acc": acc, "p4_ln": ln2, "p4_norm": lambda u: norm_of(2, x2, seqs(u), u), "p4_simd": sim, "p4_nbm": nbmax,
                 "p4_probs": probs1, "p4_hh": products, "p4_outd": p4_out, "p5_ln": ln3,
                 "p5_norm": lambda u: norm_of(3, x3, seqs(u), u), "p5_router": router1, "p5_prob": prob7, "p5_end": last_add})

        @block.tensor
        def _(pe):
            def mm(dst, lhsT, rhs, start=True, stop=True):
                return nc.tensor.matmul(dst, lhsT, rhs, start=start, stop=stop)

            def warm(n):
                pe.wait_ge(s["ones_ok"], 1)
                v = ones[:, :].bitcast(BF16)
                for _ in range(n):
                    mm(ps[:, 3, 0:2 * P], v[:, 0:P], v[:, :])

            def setup():
                pe.wait_ge(s["ident_ok"], 1)
                pe.wait_ge(s["small_in"], 96)
                nc.tensor.transpose(ps[:, 0, 0:NROW], rows[:, :], ident[0:NROW, 0:NROW]).then_inc(s["cols_ps"], 1)
                pe.wait_ge(s["wr_in"], 16)
                pe.wait_ge(s["cols_ok"], 1)
                nc.tensor.transpose(ps[:, 0, 64:64 + E1], wrn[:, :], ident[0:E1, 0:E1]).then_inc(s["wr_ps"], 1)

            def to_T(i, h, bank):
                for n in range(HALF):
                    pe.wait_ge(s[f"ln{i}_norm"], h * HALF + n + 1)
                    last = nc.tensor.transpose(ps[:, bank, n * S:(n + 1) * S], xn[i][:, h * HALF + n, :], ident[:, :])
                last.then_inc(s[f"xT{i}_ps"], 1)

            def ctx_T(h):
                pe.wait_ge(s["ctx_in"], 16)
                pe.wait_ge(s["ident_ok"], 1)
                for n in range(HALF):
                    last = nc.tensor.transpose(ps[:, banks(h)[1], n * CTX:(n + 1) * CTX], ctxn[:, h * HALF + n, :], ident[0:CTX, 0:CTX])
                last.then_inc(s["ctxT_ps"], 1)

            def scores0(h):
                pe.wait_ge(s["xT0_ok"], h + 1)
                pe.wait_ge(s["ctxT_ok"], h + 1)
                for n in range(HALF):
                    last = mm(ps[:, banks(h)[1], n * CTX:(n + 1) * CTX], xT[0][:, h, n * S:(n + 1) * S], ctxT[:, h * HALF + n, :])
                last.then_inc(s["sc0_ps"], 1)

            def av0(h):
                pe.wait_ge(s["pr0_ok"], h + 1)
                for n in range(HALF):
                    last = nc.tensor.transpose(ps[0:CTX, banks(h)[0], n * S:(n + 1) * S], pr[0][:, h * HALF + n, :], ident[:, :])
                last.then_inc(s["pT0_ps"], 1)
                pe.wait_ge(s["sc0_sub"], h + 1)
                pe.wait_ge(s["pT0_ok"], h + 1)
                for n in range(HALF):
                    last = mm(ps[:, banks(h)[1], n * D:(n + 1) * D], pT[0][:, h, n * S:(n + 1) * S], ctxn[:, h * HALF + n, :])
                last.then_inc(s["av0_ps"], 1)

            def qkv(h):
                pe.wait_ge(s["xT1_ok"], h + 1)
                pe.wait_ge(s["wqk_ok"], 1)
                pe.wait_ge(s["x1_ok"], HALF * (h + 1))
                mm(ps[:, banks(h)[1], :], wqk[:, :], xT[1][:, h, :]).then_inc(s["qk_ps"], 1)
                pe.wait_ge(s["vw_in"], 32)
                for n in range(HALF):
                    last = mm(ps[:, banks(h)[0], n * LAT:(n + 1) * LAT], xT[1][:, h, n * S:(n + 1) * S], wv[:, :])
                last.then_inc(s["v_ps"], 1)

            def cols_of(b):
                return slice((b % HALF) * S, (b % HALF + 1) * S)

            def rows_of(g):
                pe.wait_ge(s["part_ok"], 1)
                pe.wait_ge(s["selqk_ok"], 2)
                pe.wait_ge(s["wr_ok"], 1)
                if g >= 2:
                    pe.wait_ge(s["qrow_ok"], g - 1)
                for sel, bank in ((selk, 0), (selq, 2)):
                    for q in range(PARTS):
                        last = mm(ps[:, bank + g % 2, :], sel[:, q, g, :], part[:, 0, q, :], q == 0, q == PARTS - 1)
                    last.then_inc(s["rows_ps"], 1)

            def s1(b, g):
                n, h = b * GROUPS + g, b // HALF
                if h:
                    pe.wait_ge(s["stack_in"], 16 * 2 * LANES)
                else:
                    pe.wait_ge(s["krow_ok"], g + 1)
                    pe.wait_ge(s["qbd_ok"], g + 1)
                if n >= 2:
                    pe.wait_ge(s["s1_max"], n - 1)
                elif n == 0:
                    pe.wait_ge(s["krow_ok"], GROUPS)
                for j in range(LANES):
                    last = mm(ps[:, n % 2, j * S:(j + 1) * S], qbd[h][:, g, j, cols_of(b)], kst[h][:, g, cols_of(b)])
                last.then_inc(s["s1_ps"], 1)

            def maxT(b):
                pe.wait_ge(s["msp_ok"], b + 1)
                pe.wait_ge(s["identb_ok"], 1)
                pe.wait_ge(s["mT_ok"] if b else s["qk_ok"], b or 1)
                for j in range(LANES):
                    last = mm(ps[0:MROWS, 7, j * S:(j + 1) * S], msp[:, b % 2, MROWS * j:MROWS * (j + 1)], identb[:, :])
                last.then_inc(s["mT_ps"], 1)

            def s2(b, g):
                n, h = b * GROUPS + g, b // HALF
                pe.wait_ge(s["mT_ok"], b + 1)
                pe.wait_ge(s["selg_ok"], 1)
                pe.wait_ge(s["p_ok"] if n >= 2 else s["qrow_ok"], n - 1 if n >= 2 else GROUPS)
                dst = ps[:, 2 + n % 2, :].rearrange("p (j q) -> p j q", j=LANES)
                mm(dst, kst[h][:, g, cols_of(b)], qbd[h][:, g, :, cols_of(b)], True, False)
                mm(dst, selg[:, g, :], mT[:, b % 2, :, :], False, True).then_inc(s["s2_ps"], 1)

            def av(b, g):
                n, h = b * GROUPS + g, b // HALF
                pe.wait_ge(s["p_ok"], n + 1)
                pe.wait_ge(s["v_ok"], h + 1)
                if g == 0 and b >= 2:
                    pe.wait_ge(s["un_ok"], b - 1)
                elif g == 0:
                    pe.wait_ge(s["qk_ok"], NHALF)
                for j in range(LANES):
                    last = mm(ps[ROWS * j:ROWS * (j + 1), 5 + b % 2, 0:S], vpad[h][:, b % HALF, g, j, :],
                              pexp[:, n % 3, j * S:(j + 1) * S], start=g == 0, stop=g == GROUPS - 1)
                last.then_inc(s["av_ps"], 1)

            def den(b):
                pe.wait_ge(s["un_ok"], b + 1)
                pe.wait_ge(s["selden_ok"], 1)
                pe.wait_ge(s["ln_ok"] if b else s["v_ok"], b or NHALF)
                if b >= HALF:
                    pe.wait_ge(s["mla_ok"], 1)
                if b >= HALF + 1:
                    pe.wait_ge(s["lg_sub"], 1)
                mm(ps[:, 4, 0:S], selden[:, :], un[:, b % 2, :]).then_inc(s["den_ps"], 1)

            def oproj(h):
                pe.wait_ge(s["ao_ok"], HALF * (h + 1))
                pe.wait_ge(s["ow_in"], 16 * LANES)
                mm(ps[:, 4, :], wo[:, :], aoT[:, h, :]).then_inc(s["o_ps"], 1)

            def router(h):
                pe.wait_ge(s["mla_ok"], h + 1)
                if h == 0:
                    pe.wait_ge(s["ln_ok"], HALF + 1)
                pe.wait_ge(s["w1_in"], 48)
                for n in range(HALF):
                    last = mm(ps[:, 4, n * E0:(n + 1) * E0], mlaT[:, h, n * S:(n + 1) * S], rw[:, :])
                last.then_inc(s["lg_ps"], 1)

            def comb_T(h):
                pe.wait_ge(s["comb_ok"], h + 1)
                if h:
                    pe.wait_ge(s["lg_sub"], NHALF)
                else:
                    pe.wait_ge(s["mT_ok"], BATCH)
                for n in range(HALF):
                    last = mm(ps[0:E0, (7, 4)[h], n * S:(n + 1) * S], comb[:, h * HALF + n, :], ident[:, :])
                last.then_inc(s["cT_ps"], 1)

            def bias2(h):
                pe.wait_ge(s["cT_ok"], h + 1)
                pe.wait_ge(s["w2_in"], 32)
                pe.wait_ge(s["x2_init"] if h else s["un_ok"], h or BATCH - 1)
                for n in range(HALF):
                    last = mm(ps[:, 5, n * D:(n + 1) * D], combT[:, h, n * S:(n + 1) * S], b2s[:, :])
                last.then_inc(s["b2_ps"], 1)

            def split3(dst, w_hi, w_lo, x_hi, x_lo):
                mm(dst, w_lo, x_hi, True, False)
                mm(dst, w_hi, x_lo, False, False)
                return mm(dst, w_hi, x_hi, False, True)

            def m1(u, e, c):
                k, n = u * E0 + e, UNITS[u][1] * S
                pe.wait_ge(s["w1_split"], 1)
                pe.wait_ge(s["mlalo_ok"], min(u, 1) + 1)
                if k == 0:
                    pe.wait_ge(s["sr_ok"], NHALF)
                elif k == 1:
                    pe.wait_ge(s["un_ok"], BATCH)
                    pe.wait_ge(s["cT_ok"], 1)
                elif k == E0 + 1:
                    pe.wait_ge(s["cT_ok"], NHALF)
                    pe.wait_ge(s["x2_init"], NHALF)
                else:
                    pe.wait_ge(s["gelu_ok"], F0 * (k - (2 if k <= 2 * E0 else 1)) + c + 1)
                f = slice(c * P, (c + 1) * P)
                split3(ps[:, h1_bank(k, c), 0:n], w1_hi[:, e, f], w1_lo[:, e, f], x4_hi[:, toks(u)], x4_lo[:, toks(u)]).then_inc(s["h1_ps"], 1)

            def m2(u, e):
                k = u * E0 + e
                pe.wait_ge(s["gelu_ok"], F0 * (k + 1))
                if k < 2:
                    pe.wait_ge(s["p_ok"], GROUPS * BATCH)
                else:
                    pe.wait_ge(s["moe_acc"], sums(k - 1))
                for i in range(UNITS[u][1]):
                    for c in range(F0):
                        last = mm(ps[:, 2 + k % 2, i * D:(i + 1) * D], hT[:, k % 2, c, i * S:(i + 1) * S],
                                  w2s[:, e * F0 + c, :], c == 0, c == F0 - 1)
                last.then_inc(s["h2_ps"], 1)

            def sim0(h):
                pe.wait_ge(s["w2sq_ok"], 1)
                pe.wait_ge(s["ctxT_ok"], h + 1)
                pe.wait_ge(s["s1_max"], GROUPS * BATCH)
                mm(ps[:, h, 0:HALF * CTX], w2sq[:, :], ctxT[:, halves(h), :].rearrange("p b c -> p (b c)")).then_inc(s["sr_ps"], 1)

            def unit_T(i, u):
                a, n = UNITS[u]
                for m in range(n):
                    pe.wait_ge(s[f"ln{i}_norm"], a + m + 1)
                    last = nc.tensor.transpose(ps[:, bank_a[u], m * S:(m + 1) * S], xn[i][:, a + m, :], ident[:, :])
                last.then_inc(s[f"xT{i}_ps"], 1)

            def xT2(u):
                pe.wait_ge(s["gelu_ok"], F0 * E0 * (u + 1))
                unit_T(2, u)

            def sim(u):
                a, n = UNITS[u]
                pe.wait_ge(s["xT2_ok"], u + 1)
                pe.wait_ge(s["ctxw_ok"], NHALF)
                for m in range(n):
                    last = mm(ps[:, bank_b[u], m * CTX:(m + 1) * CTX], x3T[:, toks(u, m)], ctxw[:, a + m, :])
                last.then_inc(s["sim_ps"], 1)

            def max_T(u):
                pe.wait_ge(s["sim_sub"], u + 1)
                mm(ps[0:UNITS[u][1], bank_b[u], 0:S], mx[1][:, seqs(u)], ident[:, :]).then_inc(s["mxT_ps"], 1)

            def pT1(u):
                a, n = UNITS[u]
                pe.wait_ge(s["batt_ok"], u + 1)
                mm(ps[:, bank_b[u], 0:n], batt[0:n, u, :], ident[0:n, 0:n]).then_inc(s["bT_ps"], 1)
                pe.wait_ge(s["pn1_ok"], u + 1)
                for m in range(n):
                    last = nc.tensor.transpose(ps[0:CTX, bank_a[u], m * S:(m + 1) * S], pr[1][:, a + m, :], ident[:, :])
                last.then_inc(s["pT1_ps"], 1)

            def hq(u):
                a, n = UNITS[u]
                pe.wait_ge(s["bT_ok"], u + 1)
                for m in range(n):
                    last = mm(ps[:, bank_b[u], m:m + 1], xn[2][:, a + m, :], battc[:, a + m:a + m + 1])
                last.then_inc(s["hb_ps"], 1)
                pe.wait_ge(s["pT1_ok"], u + 1)
                for m in range(n):
                    last = mm(ps[:, bank_a[u], m * S:(m + 1) * S], ctxn[:, a + m, :], prT[:, toks(u, m)])
                last.then_inc(s["hq_ps"], 1)

            def p4_out(u):
                a, n = UNITS[u]
                pe.wait_ge(s["hq_ok"], u + 1)
                pe.wait_ge(s["hh_ok"], u + 1)
                pe.wait_ge(s["w14_ok"], u + 1)
                for m in range(n):
                    dst = ps[:, bank_b[u], m * D:(m + 1) * D]
                    mm(dst, hqT[:, toks(u, m)], wqv[:, 1, :], True, False)
                    mm(dst, hhT[:, toks(u, m)], wqv[:, 2, :], False, False)
                    last = mm(dst, x3T[:, toks(u, m)], w14[:, a + m, :], False, True)
                last.then_inc(s["qv_ps"], 1)

            def xT3(u):
                pe.wait_ge(s["hq_ok"], u + 1)
                unit_T(3, u)

            def router1(u):
                pe.wait_ge(s["wr_ok"], 1)
                pe.wait_ge(s["xT3_ok"], u + 1)
                pe.wait_ge(s["x3_ok"], u + 1)
                for m in range(UNITS[u][1]):
                    last = mm(ps[:, bank_b[u], m * E1:(m + 1) * E1], x4T[:, toks(u, m)], wrT[:, :])
                last.then_inc(s["l7_ps"], 1)

            def f1(u, c):
                pe.wait_ge(s["f1_split"], 1)
                pe.wait_ge(s["x4lo_ok"], u + 1)
                k = F1 * u + c
                if c >= 2:
                    pe.wait_ge(s["g_ok"], k - 1)
                else:
                    pe.wait_ge(s["l7_sub"] if c else s["x4hi_ok"], u + 1)
                f = slice(c * P, (c + 1) * P)
                split3(ps[:, (bank_a, bank_b)[c % 2][u], 0:UNITS[u][1] * S], f1_hi[:, f], f1_lo[:, f],
                       x4_hi[:, toks(u)], x4_lo[:, toks(u)]).then_inc(s["f1_ps"], 1)

            def f2(u, i):
                pe.wait_ge(s["g_ok"], F1 * (u + 1))
                for c in range(F1):
                    last = mm(ps[:, (bank_a, bank_b)[i % 2][u], i // 2 * D:(i // 2 + 1) * D], gT[:, c, toks(u, i)], f2s[:, c, :],
                              c == 0, c == F1 - 1)
                last.then_inc(s["f2_ps"], 1)

            run({"warm": warm, "setup": setup, "p1_ctx": ctx_T, "p1_T": lambda h: to_T(0, h, banks(h)[0]), "p1_scores": scores0, "p1_av": av0,
                 "p1_T2": lambda h: to_T(1, h, banks(h)[0]), "p1_qkv": qkv, "s1": s1, "mT": maxT, "s2": s2, "av": av,
                 "den": den, "oproj": oproj, "router": router, "cT": comb_T, "b2": bias2, "m1": m1, "rows": rows_of, "m2": m2, "p4_ctx": sim0,
                 "p4_T": xT2, "p4_sim": sim, "p4_mx": max_T, "p4_pT": pT1,
                 "p4_hq": hq, "p4_out": p4_out, "p5_T": xT3, "p5_router": router1, "p5_f1": f1, "p5_f2": f2})


_INS = ['x', 'ctx_1024', 'L0_ffn_q_w', 'L0_ffn_q_b', 'L0_ffn_k_w', 'L0_ffn_k_b', 'L0_ffn_v_w', 'L0_ffn_v_b', 'L0_ffn_o_w',
        'L0_ffn_o_b', 'L0_ffn_router_w', 'L0_ffn_router_b', 'L0_ffn_w1', 'L0_ffn_b1', 'L0_ffn_w2', 'L0_ffn_b2',
        'L1_xattn_w_sim', 'L1_xattn_b_sim', 'L1_xattn_W_qv', 'L1_xattn_b_qv', 'L1_ffn_Wr', 'L1_ffn_W1', 'L1_ffn_b1',
        'L1_ffn_W2', 'L1_ffn_b2']
_OUTS = [((BATCH, S, D), 'float32')]


def kernel(**inputs):
    import numpy as _np
    import concourse.bacc as _bacc
    from concourse import mybir as _mybir
    from concourse.bass_utils import run_bass_kernel_spmd as _run

    nc = _bacc.Bacc("TRN2", target_bir_lowering=False, num_devices=1)
    arrays, args = {}, []
    for name in _INS:
        a = _np.ascontiguousarray(inputs[name])
        arrays[f"in_{name}_dram"] = a
        args.append(nc.dram_tensor(f"in_{name}_dram", a.shape, _mybir.dt.from_np(a.dtype), kind="ExternalInput").ap())
    for i, (shape, dtype) in enumerate(_OUTS):
        dt = _mybir.dt.from_np(_np.dtype(dtype))
        args.append(nc.dram_tensor(f"out_{i}_dram", shape, dt, kind="ExternalOutput").ap())
    build(nc, *args)
    r = _run(nc, [arrays], core_ids=[0])
    got = tuple(r.results[0][f"out_{i}_dram"] for i in range(len(_OUTS)))
    return got[0]
```
